# Optimizing a Trainium2 kernel written in Bass

```python
import numpy as np
import jax
import jax.numpy as jnp

def _softmax(x, axis=-1):
    return jax.nn.softmax(x, axis=axis)

def _gelu(x):
    return jax.nn.gelu(x, approximate=True)

def _silu(x):
    return jax.nn.silu(x)

def _sigmoid(x):
    return jax.nn.sigmoid(x)

def _layernorm(x, axis=-1, eps=1e-05):
    m = jnp.mean(x, axis=axis, keepdims=True)
    v = jnp.var(x, axis=axis, keepdims=True)
    return (x - m) / jnp.sqrt(v + eps)

def _scatter_add(tgt, idx, src, axis=0):
    return tgt.at[idx].add(src)

def _segment_sum(src, seg, n):
    return jax.ops.segment_sum(src, seg, n)
kernel_name = 'mk_decoder_preln_d4_seqx_r8_a1200e'

def setup_inputs(seed: int=0):
    np.random.seed(seed)
    _w = jnp.asarray

    def _rec_inputs():
        import jax
        import jax.numpy as jnp
        _rk = jax.random.key(seed)
        x = -0.0002928 + 1 * jax.random.normal(jax.random.fold_in(_rk, 1), (8, 128, 128), jnp.float32)
        _lenS = 128 - jax.random.randint(jax.random.fold_in(_rk, 7), (8,), 0, max(1, 128 // 4) + 1, jnp.int32)
        _lenS2 = 128 - jax.random.randint(jax.random.fold_in(_rk, 8), (8,), 0, max(1, 128 // 4) + 1, jnp.int32)
        _ctx_1024P = jax.random.normal(jax.random.fold_in(_rk, 11), (8, 16, 128), jnp.float32)
        _ctx_1024c = jax.random.dirichlet(jax.random.fold_in(_rk, 511), 0.3 * jnp.ones((16,), jnp.float32), (8, 128))
        _ctx_1024t = jnp.einsum('bsk,bkd->bsd', _ctx_1024c, _ctx_1024P)
        _ctx_1024t = _ctx_1024t * jax.lax.rsqrt(jnp.mean(jnp.square(_ctx_1024t)) + 1e-12) * 0.953939
        ctx_1024 = -1.39393e-06 + 0.999914 * (_ctx_1024t + 0.3 * jax.random.normal(jax.random.fold_in(_rk, 611), (8, 128, 128), jnp.float32))
        return (x, ctx_1024)
    x, ctx_1024 = _rec_inputs()

    def _L0_attn_setup():
        import jax, jax.numpy as jnp
        import numpy as np
        N_HEAD = 16
        LATENT = 32

        def _rotate_half(x):
            xe = x[..., ::2]
            xo = x[..., 1::2]
            return jnp.stack((-xo, xe), axis=-1).reshape(x.shape)

        def _rope_tables(T, latent_dim, dtype):
            inv_freq = 1.0 / 10000.0 ** (jnp.arange(0, latent_dim, 2, dtype=jnp.float32) / latent_dim)
            t = jnp.arange(T, dtype=jnp.float32)
            freqs = jnp.outer(t, inv_freq)
            cos = jnp.repeat(jnp.cos(freqs), 2, axis=-1)[:, :latent_dim]
            sin = jnp.repeat(jnp.sin(freqs), 2, axis=-1)[:, :latent_dim]
            return (cos.astype(dtype), sin.astype(dtype))
        key = jax.random.key(seed)
        ks = jax.random.split(key, 14)
        C = 128
        hd = C // N_HEAD
        L = LATENT
        s = 0.02
        return {'x': jax.random.normal(ks[0], (4, 256, C), jnp.float32), 'c_attn_w': jax.random.normal(ks[1], (3 * C, C), jnp.float32) * s, 'c_attn_b': jnp.zeros((3 * C,), jnp.float32), 'q2l_w': jax.random.normal(ks[2], (L, hd), jnp.float32) * s, 'q2l_b': jnp.zeros((L,), jnp.float32), 'kv2l_w': jax.random.normal(ks[3], (L, hd), jnp.float32) * s, 'kv2l_b': jnp.zeros((L,), jnp.float32), 'l2o_w': jax.random.normal(ks[4], (hd, L), jnp.float32) * s, 'l2o_b': jnp.zeros((hd,), jnp.float32), 'wqk_w': jax.random.normal(ks[5], (L, L), jnp.float32) * s, 'wqk_b': jnp.zeros((L,), jnp.float32), 'cproj_w': jax.random.normal(ks[6], (C, C), jnp.float32) * s, 'cproj_b': jnp.zeros((C,), jnp.float32)}
    _L0_attn_all = _L0_attn_setup()
    _L0_attn_in = {k: v for k, v in _L0_attn_all.items() if k in ('c_attn_w', 'c_attn_b', 'q2l_w', 'q2l_b', 'kv2l_w', 'kv2l_b', 'l2o_w', 'l2o_b', 'wqk_w', 'wqk_b', 'cproj_w', 'cproj_b')}
    del _L0_attn_all

    def _L0_xattn_setup():
        import jax, jax.numpy as jnp
        import numpy as np
        B, T, D, H = (2, 256, 128, 16)
        DH = D // H
        key = jax.random.key(seed)
        ks = jax.random.split(key, 11)
        s = 1.0 / np.sqrt(D)
        return {'q': jax.random.normal(ks[0], (B, T, D), jnp.float32), 'k': jax.random.normal(ks[1], (B, T, D), jnp.float32), 'v': jax.random.normal(ks[2], (B, T, D), jnp.float32), 'wq_w': jax.random.normal(ks[3], (D, D), jnp.float32) * s, 'wq_b': jnp.zeros((D,), jnp.float32), 'wk_w': jax.random.normal(ks[4], (D, D), jnp.float32) * s, 'wk_b': jnp.zeros((D,), jnp.float32), 'wv_w': jax.random.normal(ks[5], (D, D), jnp.float32) * s, 'wv_b': jnp.zeros((D,), jnp.float32), 'wo_w': jax.random.normal(ks[6], (D, D), jnp.float32) * s, 'wo_b': jnp.zeros((D,), jnp.float32)}
    _L0_xattn_all = _L0_xattn_setup()
    _L0_xattn_in = {k: v for k, v in _L0_xattn_all.items() if k in ('wq_w', 'wq_b', 'wk_w', 'wk_b', 'wv_w', 'wv_b', 'wo_w', 'wo_b')}
    del _L0_xattn_all

    def _L0_ffn_setup():
        import jax, jax.numpy as jnp
        import numpy as np
        D_MODEL = 128
        M = 64
        INNER = 16
        key = jax.random.key(seed)
        ks = jax.random.split(key, 9)

        def init(k, shape, fan_in):
            bound = 1.0 / np.sqrt(fan_in)
            return jax.random.uniform(k, shape, jnp.float32, -bound, bound)
        x = jax.random.normal(ks[0], (16, 512, D_MODEL), dtype=jnp.float32)
        Win = init(ks[1], (D_MODEL, M), D_MODEL)
        bin_ = init(ks[2], (M,), D_MODEL)
        W1 = init(ks[3], (M, INNER), 1)
        b1 = init(ks[4], (M, INNER), 1)
        W2 = init(ks[5], (M, INNER), INNER)
        b2 = init(ks[6], (M,), INNER)
        Wout = init(ks[7], (M, D_MODEL), M)
        bout = init(ks[8], (D_MODEL,), M)
        return {'x': x, 'Win': Win, 'bin_': bin_, 'W1': W1, 'b1': b1, 'W2': W2, 'b2': b2, 'Wout': Wout, 'bout': bout}
    _L0_ffn_all = _L0_ffn_setup()
    _L0_ffn_in = {k: v for k, v in _L0_ffn_all.items() if k in ('Win', 'bin_', 'W1', 'b1', 'W2', 'b2', 'Wout', 'bout')}
    del _L0_ffn_all

    def _L1_attn_setup():
        import jax, jax.numpy as jnp
        import numpy as np
        import math
        B, L, D, MAXL = (4, 512, 128, 2048)

        def _shift1(a):
            return jnp.concatenate([jnp.zeros_like(a[:, :1]), a[:, :-1]], axis=1)
        key = jax.random.key(seed)
        ks = jax.random.split(key, 12)
        s = 0.02

        def w(k, shape):
            return jax.random.normal(k, shape, jnp.float32) * s
        return {'x': jax.random.normal(ks[0], (B, L, D), jnp.float32), 'pos_phases': jax.random.normal(ks[1], (MAXL, D), jnp.float32) * math.pi, 'Wpv': w(ks[2], (D, D)), 'bpv': jnp.zeros((D,), jnp.float32), 'Wk': w(ks[3], (D, D)), 'bk': jnp.zeros((D,), jnp.float32), 'Wkv': w(ks[4], (D, D)), 'bkv': jnp.zeros((D,), jnp.float32), 'Wg1': w(ks[5], (2 * D, D)), 'bg1': jnp.zeros((D,), jnp.float32), 'Wg2': w(ks[6], (D, 1)), 'bg2': jnp.zeros((1,), jnp.float32), 'Wb1': w(ks[7], (D, D // 2)), 'bb1': jnp.zeros((D // 2,), jnp.float32), 'Wb2': w(ks[8], (D // 2, 2)), 'bb2': jnp.zeros((2,), jnp.float32), 'ln_g': jnp.ones((D,), jnp.float32), 'ln_b': jnp.zeros((D,), jnp.float32), 'Wo': w(ks[9], (D, D)), 'bo': jnp.zeros((D,), jnp.float32)}
    _L1_attn_all = _L1_attn_setup()
    _L1_attn_in = {k: v for k, v in _L1_attn_all.items() if k in ('pos_phases', 'Wpv', 'bpv', 'Wk', 'bk', 'Wkv', 'bkv', 'Wg1', 'bg1', 'Wg2', 'bg2', 'Wb1', 'bb1', 'Wb2', 'bb2', 'ln_g', 'ln_b', 'Wo', 'bo')}
    del _L1_attn_all

    def _L1_xattn_setup():
        import jax, jax.numpy as jnp
        import numpy as np
        D_MODEL = 128
        NUM_HEADS = 16
        DEPTH = D_MODEL // NUM_HEADS

        def _split_heads(x, B):
            return x.reshape(B, -1, NUM_HEADS, DEPTH).transpose(0, 2, 1, 3)
        key = jax.random.key(seed)
        ks = jax.random.split(key, 10)
        B, LQ, LK = (4, 256, 256)
        bound = float(np.sqrt(6.0 / (D_MODEL + D_MODEL)))

        def w(k):
            return jax.random.uniform(k, (D_MODEL, D_MODEL), jnp.float32, -bound, bound)
        return {'query': jax.random.normal(ks[0], (B, LQ, D_MODEL), jnp.float32), 'value': jax.random.normal(ks[1], (B, LK, D_MODEL), jnp.float32), 'wq': w(ks[2]), 'bq': jnp.zeros((D_MODEL,), jnp.float32), 'wk': w(ks[3]), 'bk': jnp.zeros((D_MODEL,), jnp.float32), 'wv': w(ks[4]), 'bv': jnp.zeros((D_MODEL,), jnp.float32), 'wo': w(ks[5]), 'bo': jnp.zeros((D_MODEL,), jnp.float32)}
    _L1_xattn_all = _L1_xattn_setup()
    _L1_xattn_in = {k: v for k, v in _L1_xattn_all.items() if k in ('wq', 'bq', 'wk', 'bk', 'wv', 'bv', 'wo', 'bo')}
    del _L1_xattn_all

    def _L1_ffn_setup():
        import jax, jax.numpy as jnp
        import numpy as np
        QB = 127.0
        EPS = 1e-05

        def _ste(x, q):
            return x + jax.lax.stop_gradient(q - x)

        def bitlinear(x, W, b):
            w_scale = jnp.clip(jnp.mean(jnp.abs(W)), EPS, None)
            Wq = _ste(W, jnp.clip(jnp.round(W / w_scale), -1.0, 1.0) * w_scale)
            x_scale = jnp.clip(jnp.max(jnp.abs(x), axis=-1, keepdims=True), EPS, None)
            xq = _ste(x, jnp.clip(jnp.round(x * (QB / x_scale)), -QB - 1.0, QB) * (x_scale / QB))
            return jnp.einsum('bnd,hd->bnh', xq, Wq) + b
        key = jax.random.key(seed)
        k0, k1, k2 = jax.random.split(key, 3)
        B, N, D = (8, 512, 128)
        H = int(D * 4.0)
        x = jax.random.normal(k0, (B, N, D), dtype=jnp.float32)
        W1 = jax.random.normal(k1, (H, D), dtype=jnp.float32) * 0.02
        b1 = jnp.zeros((H,), dtype=jnp.float32)
        W2 = jax.random.normal(k2, (D, H), dtype=jnp.float32) * 0.02
        b2 = jnp.zeros((D,), dtype=jnp.float32)
        return {'x': x, 'W1': W1, 'b1': b1, 'W2': W2, 'b2': b2}
    _L1_ffn_all = _L1_ffn_setup()
    _L1_ffn_in = {k: v for k, v in _L1_ffn_all.items() if k in ('W1', 'b1', 'W2', 'b2')}
    del _L1_ffn_all

    def _L2_attn_setup():
        import jax, jax.numpy as jnp
        import numpy as np
        B, T, D, H = (64, 64, 128, 128)
        key = jax.random.key(seed)
        k1, k2, k3 = jax.random.split(key, 3)
        scale = 0.02
        return {'x': jax.random.normal(k1, (B, T, D), dtype=jnp.float32), 'Wi': jax.random.normal(k2, (H, D), dtype=jnp.float32) * scale, 'bi': jnp.zeros((H,), dtype=jnp.float32), 'Wh': jax.random.normal(k3, (H, H), dtype=jnp.float32) * scale, 'bh': jnp.zeros((H,), dtype=jnp.float32)}
    _L2_attn_all = _L2_attn_setup()
    _L2_attn_in = {k: v for k, v in _L2_attn_all.items() if k in ('Wi', 'bi', 'Wh', 'bh')}
    del _L2_attn_all

    def _L2_xattn_setup():
        import jax, jax.numpy as jnp
        import numpy as np
        EPS = 1e-10
        DONUT_MIN = 0.001
        DONUT_MAX = 100.0

        def donut(x, mn=DONUT_MIN, mx=DONUT_MAX):
            return jnp.sign(x + mn / 2) * jnp.clip(jnp.abs(x), mn, mx)
        key = jax.random.key(seed)
        ks = jax.random.split(key, 8)
        b, s, hd = (2, 256, 128)
        std = 1.0 / np.sqrt(hd)
        return {'query': jax.random.normal(ks[0], (b, s, hd), dtype=jnp.float32), 'context': jax.random.normal(ks[1], (b, s, hd), dtype=jnp.float32), 'WQ': jax.random.normal(ks[2], (hd, hd), dtype=jnp.float32) * std, 'WK': jax.random.normal(ks[3], (hd, hd), dtype=jnp.float32) * std, 'WV': jax.random.normal(ks[4], (hd, hd), dtype=jnp.float32) * std, 'Wout': jax.random.normal(ks[5], (hd, hd), dtype=jnp.float32) * std, 'p_param': 1.0 + 0.02 * jax.random.normal(ks[6], (hd,), dtype=jnp.float32), 'shift': jnp.ones((hd,), dtype=jnp.float32) * 5.0}
    _L2_xattn_all = _L2_xattn_setup()
    _L2_xattn_in = {k: v for k, v in _L2_xattn_all.items() if k in ('WQ', 'WK', 'WV', 'Wout', 'p_param', 'shift')}
    del _L2_xattn_all

    def _L2_ffn_setup():
        import jax, jax.numpy as jnp
        import numpy as np
        TOP_K = 2
        EPS = 1e-09
        key = jax.random.key(seed)
        ks = jax.random.split(key, 6)
        B, T, D, H, E = (4, 256, 128, 256, 8)
        x = jax.random.normal(ks[0], (B, T, D), dtype=jnp.float32)
        Wg = jax.random.normal(ks[1], (E, D), dtype=jnp.float32) * 0.02
        W1 = jax.random.normal(ks[2], (E, 2 * H, D), dtype=jnp.float32) * 0.02
        b1 = jax.random.normal(ks[3], (E, 2 * H), dtype=jnp.float32) * 0.02
        Wo = jax.random.normal(ks[4], (D, H), dtype=jnp.float32) * 0.02
        bo = jax.random.normal(ks[5], (D,), dtype=jnp.float32) * 0.02
        return {'x': x, 'Wg': Wg, 'W1': W1, 'b1': b1, 'Wo': Wo, 'bo': bo}
    _L2_ffn_all = _L2_ffn_setup()
    _L2_ffn_in = {k: v for k, v in _L2_ffn_all.items() if k in ('Wg', 'W1', 'b1', 'Wo', 'bo')}
    del _L2_ffn_all

    def _L3_attn_setup():
        import jax, jax.numpy as jnp
        import numpy as np
        DIM = 128
        N_HEADS = 16
        HEAD_DIM = DIM // N_HEADS
        WINDOW = 32
        STRIDE = 64
        PATTERN = 'combined'

        def _sparse_mask(T):
            rows = jnp.arange(T)[:, None]
            cols = jnp.arange(T)[None, :]
            causal = cols <= rows
            sliding = causal & (cols >= rows - WINDOW + 1)
            strided = causal & ((rows - cols) % STRIDE == 0)
            if PATTERN == 'sliding':
                return sliding
            if PATTERN == 'strided':
                return strided
            return sliding | strided
        key = jax.random.key(seed)
        kx, kq, kk, kv, ko = jax.random.split(key, 5)
        s = 1.0 / np.sqrt(DIM)
        return {'x': jax.random.normal(kx, (1, 512, DIM), dtype=jnp.float32), 'Wq': jax.random.normal(kq, (DIM, DIM), dtype=jnp.float32) * s, 'Wk': jax.random.normal(kk, (DIM, DIM), dtype=jnp.float32) * s, 'Wv': jax.random.normal(kv, (DIM, DIM), dtype=jnp.float32) * s, 'Wo': jax.random.normal(ko, (DIM, DIM), dtype=jnp.float32) * s}
    _L3_attn_all = _L3_attn_setup()
    _L3_attn_in = {k: v for k, v in _L3_attn_all.items() if k in ('Wq', 'Wk', 'Wv', 'Wo')}
    del _L3_attn_all

    def _L3_xattn_setup():
        import jax, jax.numpy as jnp
        import numpy as np
        import math
        D_MODEL = 128
        N_HEADS = 16
        HEAD_DIM = D_MODEL // N_HEADS

        def _compute_slopes(n_heads: int) -> np.ndarray:

            def pow2_slopes(n):
                start = 2.0 ** (-2.0 ** (-(math.log2(n) - 3)))
                return [start * start ** i for i in range(n)]
            if math.log2(n_heads).is_integer():
                s = pow2_slopes(n_heads)
            else:
                cp = 2 ** math.floor(math.log2(n_heads))
                s = pow2_slopes(cp) + pow2_slopes(2 * cp)[0::2][:n_heads - cp]
            return np.asarray(s, dtype=np.float32)
        key = jax.random.key(seed)
        ks = jax.random.split(key, 11)
        B, T, D = (2, 256, D_MODEL)
        scale = 1.0 / math.sqrt(D)
        inp = {'query': jax.random.normal(ks[0], (B, T, D), jnp.float32), 'key': jax.random.normal(ks[1], (B, T, D), jnp.float32), 'value': jax.random.normal(ks[2], (B, T, D), jnp.float32), 'Wq': jax.random.normal(ks[3], (D, D), jnp.float32) * scale, 'bq': jnp.zeros((D,), jnp.float32), 'Wk': jax.random.normal(ks[4], (D, D), jnp.float32) * scale, 'bk': jnp.zeros((D,), jnp.float32), 'Wv': jax.random.normal(ks[5], (D, D), jnp.float32) * scale, 'bv': jnp.zeros((D,), jnp.float32), 'Wo': jax.random.normal(ks[6], (D, D), jnp.float32) * scale, 'bo': jnp.zeros((D,), jnp.float32)}
        return inp
    _L3_xattn_all = _L3_xattn_setup()
    _L3_xattn_in = {k: v for k, v in _L3_xattn_all.items() if k in ('Wq', 'bq', 'Wk', 'bk', 'Wv', 'bv', 'Wo', 'bo')}
    del _L3_xattn_all

    def _L3_ffn_setup():
        import jax, jax.numpy as jnp
        import numpy as np
        EPS = 1e-05

        def act_quant(x):
            scale = 127.0 / jnp.clip(jnp.max(jnp.abs(x), axis=-1, keepdims=True), EPS, None)
            q = jnp.clip(jnp.round(x * scale), -128.0, 127.0) / scale
            return x + jax.lax.stop_gradient(q - x)

        def weight_quant(w):
            scale = 1.0 / jnp.clip(jnp.mean(jnp.abs(w)), EPS, None)
            q = jnp.clip(jnp.round(w * scale), -1.0, 1.0) / scale
            return w + jax.lax.stop_gradient(q - w)

        def bitlinear(x, w):
            return act_quant(x) @ weight_quant(w).T
        key = jax.random.key(seed)
        k1, k2, k3, k4 = jax.random.split(key, 4)
        H, I = (128, 512)
        B, S = (4, 512)
        init = 0.02
        x = jax.random.normal(k1, (B, S, H), dtype=jnp.float32)
        w_gate = jax.random.normal(k2, (I, H), dtype=jnp.float32) * init
        w_up = jax.random.normal(k3, (I, H), dtype=jnp.float32) * init
        w_down = jax.random.normal(k4, (H, I), dtype=jnp.float32) * init
        return {'x': x, 'w_gate': w_gate, 'w_up': w_up, 'w_down': w_down}
    _L3_ffn_all = _L3_ffn_setup()
    _L3_ffn_in = {k: v for k, v in _L3_ffn_all.items() if k in ('w_gate', 'w_up', 'w_down')}
    del _L3_ffn_all
    return {'x': x, 'ctx_1024': ctx_1024, 'L0_attn_c_attn_w': _L0_attn_in['c_attn_w'], 'L0_attn_c_attn_b': _L0_attn_in['c_attn_b'], 'L0_attn_q2l_w': _L0_attn_in['q2l_w'], 'L0_attn_q2l_b': _L0_attn_in['q2l_b'], 'L0_attn_kv2l_w': _L0_attn_in['kv2l_w'], 'L0_attn_kv2l_b': _L0_attn_in['kv2l_b'], 'L0_attn_l2o_w': _L0_attn_in['l2o_w'], 'L0_attn_l2o_b': _L0_attn_in['l2o_b'], 'L0_attn_wqk_w': _L0_attn_in['wqk_w'], 'L0_attn_wqk_b': _L0_attn_in['wqk_b'], 'L0_attn_cproj_w': _L0_attn_in['cproj_w'], 'L0_attn_cproj_b': _L0_attn_in['cproj_b'], 'L0_xattn_wq_w': _L0_xattn_in['wq_w'], 'L0_xattn_wq_b': _L0_xattn_in['wq_b'], 'L0_xattn_wk_w': _L0_xattn_in['wk_w'], 'L0_xattn_wk_b': _L0_xattn_in['wk_b'], 'L0_xattn_wv_w': _L0_xattn_in['wv_w'], 'L0_xattn_wv_b': _L0_xattn_in['wv_b'], 'L0_xattn_wo_w': _L0_xattn_in['wo_w'], 'L0_xattn_wo_b': _L0_xattn_in['wo_b'], 'L0_ffn_Win': _L0_ffn_in['Win'], 'L0_ffn_bin_': _L0_ffn_in['bin_'], 'L0_ffn_W1': _L0_ffn_in['W1'], 'L0_ffn_b1': _L0_ffn_in['b1'], 'L0_ffn_W2': _L0_ffn_in['W2'], 'L0_ffn_b2': _L0_ffn_in['b2'], 'L0_ffn_Wout': _L0_ffn_in['Wout'], 'L0_ffn_bout': _L0_ffn_in['bout'], 'L1_attn_pos_phases': _L1_attn_in['pos_phases'], 'L1_attn_Wpv': _L1_attn_in['Wpv'], 'L1_attn_bpv': _L1_attn_in['bpv'], 'L1_attn_Wk': _L1_attn_in['Wk'], 'L1_attn_bk': _L1_attn_in['bk'], 'L1_attn_Wkv': _L1_attn_in['Wkv'], 'L1_attn_bkv': _L1_attn_in['bkv'], 'L1_attn_Wg1': _L1_attn_in['Wg1'], 'L1_attn_bg1': _L1_attn_in['bg1'], 'L1_attn_Wg2': _L1_attn_in['Wg2'], 'L1_attn_bg2': _L1_attn_in['bg2'], 'L1_attn_Wb1': _L1_attn_in['Wb1'], 'L1_attn_bb1': _L1_attn_in['bb1'], 'L1_attn_Wb2': _L1_attn_in['Wb2'], 'L1_attn_bb2': _L1_attn_in['bb2'], 'L1_attn_ln_g': _L1_attn_in['ln_g'], 'L1_attn_ln_b': _L1_attn_in['ln_b'], 'L1_attn_Wo': _L1_attn_in['Wo'], 'L1_attn_bo': _L1_attn_in['bo'], 'L1_xattn_wq': _L1_xattn_in['wq'], 'L1_xattn_bq': _L1_xattn_in['bq'], 'L1_xattn_wk': _L1_xattn_in['wk'], 'L1_xattn_bk': _L1_xattn_in['bk'], 'L1_xattn_wv': _L1_xattn_in['wv'], 'L1_xattn_bv': _L1_xattn_in['bv'], 'L1_xattn_wo': _L1_xattn_in['wo'], 'L1_xattn_bo': _L1_xattn_in['bo'], 'L1_ffn_W1': _L1_ffn_in['W1'], 'L1_ffn_b1': _L1_ffn_in['b1'], 'L1_ffn_W2': _L1_ffn_in['W2'], 'L1_ffn_b2': _L1_ffn_in['b2'], 'L2_attn_Wi': _L2_attn_in['Wi'], 'L2_attn_bi': _L2_attn_in['bi'], 'L2_attn_Wh': _L2_attn_in['Wh'], 'L2_attn_bh': _L2_attn_in['bh'], 'L2_xattn_WQ': _L2_xattn_in['WQ'], 'L2_xattn_WK': _L2_xattn_in['WK'], 'L2_xattn_WV': _L2_xattn_in['WV'], 'L2_xattn_Wout': _L2_xattn_in['Wout'], 'L2_xattn_p_param': _L2_xattn_in['p_param'], 'L2_xattn_shift': _L2_xattn_in['shift'], 'L2_ffn_Wg': _L2_ffn_in['Wg'], 'L2_ffn_W1': _L2_ffn_in['W1'], 'L2_ffn_b1': _L2_ffn_in['b1'], 'L2_ffn_Wo': _L2_ffn_in['Wo'], 'L2_ffn_bo': _L2_ffn_in['bo'], 'L3_attn_Wq': _L3_attn_in['Wq'], 'L3_attn_Wk': _L3_attn_in['Wk'], 'L3_attn_Wv': _L3_attn_in['Wv'], 'L3_attn_Wo': _L3_attn_in['Wo'], 'L3_xattn_Wq': _L3_xattn_in['Wq'], 'L3_xattn_bq': _L3_xattn_in['bq'], 'L3_xattn_Wk': _L3_xattn_in['Wk'], 'L3_xattn_bk': _L3_xattn_in['bk'], 'L3_xattn_Wv': _L3_xattn_in['Wv'], 'L3_xattn_bv': _L3_xattn_in['bv'], 'L3_xattn_Wo': _L3_xattn_in['Wo'], 'L3_xattn_bo': _L3_xattn_in['bo'], 'L3_ffn_w_gate': _L3_ffn_in['w_gate'], 'L3_ffn_w_up': _L3_ffn_in['w_up'], 'L3_ffn_w_down': _L3_ffn_in['w_down']}

def reference(x, ctx_1024, L0_attn_c_attn_w, L0_attn_c_attn_b, L0_attn_q2l_w, L0_attn_q2l_b, L0_attn_kv2l_w, L0_attn_kv2l_b, L0_attn_l2o_w, L0_attn_l2o_b, L0_attn_wqk_w, L0_attn_wqk_b, L0_attn_cproj_w, L0_attn_cproj_b, L0_xattn_wq_w, L0_xattn_wq_b, L0_xattn_wk_w, L0_xattn_wk_b, L0_xattn_wv_w, L0_xattn_wv_b, L0_xattn_wo_w, L0_xattn_wo_b, L0_ffn_Win, L0_ffn_bin_, L0_ffn_W1, L0_ffn_b1, L0_ffn_W2, L0_ffn_b2, L0_ffn_Wout, L0_ffn_bout, L1_attn_pos_phases, L1_attn_Wpv, L1_attn_bpv, L1_attn_Wk, L1_attn_bk, L1_attn_Wkv, L1_attn_bkv, L1_attn_Wg1, L1_attn_bg1, L1_attn_Wg2, L1_attn_bg2, L1_attn_Wb1, L1_attn_bb1, L1_attn_Wb2, L1_attn_bb2, L1_attn_ln_g, L1_attn_ln_b, L1_attn_Wo, L1_attn_bo, L1_xattn_wq, L1_xattn_bq, L1_xattn_wk, L1_xattn_bk, L1_xattn_wv, L1_xattn_bv, L1_xattn_wo, L1_xattn_bo, L1_ffn_W1, L1_ffn_b1, L1_ffn_W2, L1_ffn_b2, L2_attn_Wi, L2_attn_bi, L2_attn_Wh, L2_attn_bh, L2_xattn_WQ, L2_xattn_WK, L2_xattn_WV, L2_xattn_Wout, L2_xattn_p_param, L2_xattn_shift, L2_ffn_Wg, L2_ffn_W1, L2_ffn_b1, L2_ffn_Wo, L2_ffn_bo, L3_attn_Wq, L3_attn_Wk, L3_attn_Wv, L3_attn_Wo, L3_xattn_Wq, L3_xattn_bq, L3_xattn_Wk, L3_xattn_bk, L3_xattn_Wv, L3_xattn_bv, L3_xattn_Wo, L3_xattn_bo, L3_ffn_w_gate, L3_ffn_w_up, L3_ffn_w_down):
    import jax
    import jax.numpy as jnp

    def _L0_attn_ref(x, c_attn_w, c_attn_b, q2l_w, q2l_b, kv2l_w, kv2l_b, l2o_w, l2o_b, wqk_w, wqk_b, cproj_w, cproj_b):
        import jax, jax.numpy as jnp
        import numpy as np
        N_HEAD = 16
        LATENT = 32

        def _rotate_half(x):
            xe = x[..., ::2]
            xo = x[..., 1::2]
            return jnp.stack((-xo, xe), axis=-1).reshape(x.shape)

        def _rope_tables(T, latent_dim, dtype):
            inv_freq = 1.0 / 10000.0 ** (jnp.arange(0, latent_dim, 2, dtype=jnp.float32) / latent_dim)
            t = jnp.arange(T, dtype=jnp.float32)
            freqs = jnp.outer(t, inv_freq)
            cos = jnp.repeat(jnp.cos(freqs), 2, axis=-1)[:, :latent_dim]
            sin = jnp.repeat(jnp.sin(freqs), 2, axis=-1)[:, :latent_dim]
            return (cos.astype(dtype), sin.astype(dtype))
        B, T, C = x.shape
        H = N_HEAD
        hd = C // H
        L = q2l_w.shape[0]
        qkv = x @ c_attn_w.T + c_attn_b
        q, k, v = jnp.split(qkv, 3, axis=2)

        def heads(t):
            return t.reshape(B, T, H, hd).transpose(0, 2, 1, 3)
        q, k, v = (heads(q), heads(k), heads(v))
        q_lat = q @ q2l_w.T + q2l_b
        k_lat = k @ kv2l_w.T + kv2l_b
        v_lat = v @ kv2l_w.T + kv2l_b
        cos, sin = _rope_tables(T, L, x.dtype)
        cos = cos[None, None]
        sin = sin[None, None]
        q_lat = q_lat * cos + _rotate_half(q_lat) * sin
        k_lat = k_lat * cos + _rotate_half(k_lat) * sin
        q_for_k = q_lat @ wqk_w.T + wqk_b
        att = jnp.einsum('bhql,bhkl->bhqk', q_for_k, k_lat) * L ** (-0.5)
        causal = jnp.tril(jnp.ones((T, T), dtype=bool))
        att = jnp.where(causal[None, None], att, -jnp.inf)
        att = jax.nn.softmax(att, axis=-1)
        y_lat = jnp.einsum('bhqk,bhkl->bhql', att, v_lat)
        y = y_lat @ l2o_w.T + l2o_b
        y = y.transpose(0, 2, 1, 3).reshape(B, T, C)
        return y @ cproj_w.T + cproj_b

    def _L0_xattn_ref(q, k, v, wq_w, wq_b, wk_w, wk_b, wv_w, wv_b, wo_w, wo_b):
        import jax, jax.numpy as jnp
        import numpy as np
        B, T, D, H = (2, 256, 128, 16)
        DH = D // H
        b, t, d = q.shape
        wq = (q @ wq_w.T + wq_b).reshape(b, t, H, DH)
        wk = (k @ wk_w.T + wk_b).reshape(b, t, H, DH)
        wv = (v @ wv_w.T + wv_b).reshape(b, t, H, DH)
        scores = jnp.einsum('bthd,bshd->bhts', wq, wk) / jnp.sqrt(jnp.float32(DH))
        probs = jax.nn.softmax(scores, axis=-1)
        attn = jnp.einsum('bhts,bshd->bthd', probs, wv)
        attn = attn.reshape(b, t, d)
        return attn @ wo_w.T + wo_b

    def _L0_ffn_ref(x, Win, bin_, W1, b1, W2, b2, Wout, bout):
        import jax, jax.numpy as jnp
        import numpy as np
        D_MODEL = 128
        M = 64
        INNER = 16
        s = jnp.einsum('btd,dm->btm', x, Win) + bin_
        h = jax.nn.relu(s[..., None] * W1 + b1)
        g = jnp.einsum('btmh,mh->btm', h, W2) + b2
        out = jnp.einsum('btm,md->btd', g, Wout) + bout
        return out

    def _L1_attn_ref(x, pos_phases, Wpv, bpv, Wk, bk, Wkv, bkv, Wg1, bg1, Wg2, bg2, Wb1, bb1, Wb2, bb2, ln_g, ln_b, Wo, bo):
        import jax, jax.numpy as jnp
        import numpy as np
        import math
        B, L, D, MAXL = (4, 512, 128, 2048)

        def _shift1(a):
            return jnp.concatenate([jnp.zeros_like(a[:, :1]), a[:, :-1]], axis=1)
        Bq, Lq, Dq = x.shape
        sqrtD = jnp.sqrt(jnp.float32(Dq))
        pp = pos_phases[:Lq]
        pos_cos, pos_sin = (jnp.cos(pp), jnp.sin(pp))
        pos_values = x @ Wpv + bpv
        pos_mem_cos = jnp.cumsum(pos_cos * pos_values, axis=1)
        pos_mem_sin = jnp.cumsum(pos_sin * pos_values, axis=1)
        pos_ret = (pos_cos * pos_mem_cos + pos_sin * pos_mem_sin) / sqrtD
        key_ph = jnp.tanh(x @ Wk + bk) * jnp.pi
        key_cos, key_sin = (jnp.cos(key_ph), jnp.sin(key_ph))
        kv_values = x @ Wkv + bkv
        x_shifted = _shift1(x)
        gate_in = jnp.concatenate([x, x_shifted], axis=-1)
        gh = jax.nn.gelu(gate_in @ Wg1 + bg1, approximate=False)
        value_gates = jax.nn.sigmoid(gh @ Wg2 + bg2)
        kc_s = _shift1(key_cos)
        ks_s = _shift1(key_sin)
        kv_mem_cos = jnp.cumsum(kc_s * kv_values * value_gates, axis=1)
        kv_mem_sin = jnp.cumsum(ks_s * kv_values * value_gates, axis=1)
        gate_cumsum = jnp.maximum(jnp.cumsum(value_gates, axis=1), 1.0)
        kv_ret = (key_cos * kv_mem_cos + key_sin * kv_mem_sin) / (jnp.sqrt(gate_cumsum) * sqrtD)
        bh = jax.nn.gelu(x @ Wb1 + bb1, approximate=False)
        bw = jax.nn.softmax(bh @ Wb2 + bb2, axis=-1)
        blended = bw[..., 0:1] * pos_ret + bw[..., 1:2] * kv_ret
        mu = jnp.mean(blended, axis=-1, keepdims=True)
        var = jnp.var(blended, axis=-1, keepdims=True)
        ln = (blended - mu) / jnp.sqrt(var + 1e-05) * ln_g + ln_b
        return x + ln @ Wo + bo

    def _L1_xattn_ref(query, value, wq, bq, wk, bk, wv, bv, wo, bo):
        import jax, jax.numpy as jnp
        import numpy as np
        D_MODEL = 128
        NUM_HEADS = 16
        DEPTH = D_MODEL // NUM_HEADS

        def _split_heads(x, B):
            return x.reshape(B, -1, NUM_HEADS, DEPTH).transpose(0, 2, 1, 3)
        B = query.shape[0]
        q = _split_heads(query @ wq.T + bq, B)
        k = _split_heads(value @ wk.T + bk, B)
        v = _split_heads(value @ wv.T + bv, B)
        scale = jnp.sqrt(jnp.asarray(DEPTH, dtype=q.dtype))
        scores = jnp.einsum('bhqd,bhkd->bhqk', q, k) / scale
        attn = jax.nn.softmax(scores, axis=-1)
        ctx = jnp.einsum('bhqk,bhkd->bhqd', attn, v)
        ctx = ctx.transpose(0, 2, 1, 3).reshape(B, -1, D_MODEL)
        return ctx @ wo.T + bo

    def _L1_ffn_ref(x, W1, b1, W2, b2):
        import jax, jax.numpy as jnp
        import numpy as np
        QB = 127.0
        EPS = 1e-05

        def _ste(x, q):
            return x + jax.lax.stop_gradient(q - x)

        def bitlinear(x, W, b):
            w_scale = jnp.clip(jnp.mean(jnp.abs(W)), EPS, None)
            Wq = _ste(W, jnp.clip(jnp.round(W / w_scale), -1.0, 1.0) * w_scale)
            x_scale = jnp.clip(jnp.max(jnp.abs(x), axis=-1, keepdims=True), EPS, None)
            xq = _ste(x, jnp.clip(jnp.round(x * (QB / x_scale)), -QB - 1.0, QB) * (x_scale / QB))
            return jnp.einsum('bnd,hd->bnh', xq, Wq) + b
        h = bitlinear(x, W1, b1)
        h = jax.nn.gelu(h, approximate=False)
        return bitlinear(h, W2, b2)

    def _L2_attn_ref(x, Wi, bi, Wh, bh):
        import jax, jax.numpy as jnp
        import numpy as np
        B, T, D, H = (64, 64, 128, 128)
        xi = jnp.einsum('btd,hd->bth', x, Wi) + bi

        def step(h, xt):
            h_new = jnp.tanh(xt + h @ Wh.T + bh)
            return (h_new, h_new)
        h0 = jnp.zeros((x.shape[0], Wh.shape[0]), dtype=x.dtype)
        _, hs = jax.lax.scan(step, h0, jnp.swapaxes(xi, 0, 1))
        return jnp.swapaxes(hs, 0, 1)

    def _L2_xattn_ref(query, context, WQ, WK, WV, Wout, p_param, shift):
        import jax, jax.numpy as jnp
        import numpy as np
        EPS = 1e-10
        DONUT_MIN = 0.001
        DONUT_MAX = 100.0

        def donut(x, mn=DONUT_MIN, mx=DONUT_MAX):
            return jnp.sign(x + mn / 2) * jnp.clip(jnp.abs(x), mn, mx)
        b, q_len, hd = query.shape
        c_len = context.shape[1]
        h = 16
        a = hd // h
        scale = 1.0 / np.sqrt(hd)
        q = query @ WQ.T
        k = context @ WK.T
        v = context @ WV.T
        p = donut(p_param)
        v = jnp.clip(jnp.abs(v + shift), EPS)
        z = p * jnp.log(v)
        z_max = jnp.max(z, axis=1, keepdims=True)
        v = jnp.exp(z - z_max)
        q = q.reshape(b, q_len, h, a)
        k = k.reshape(b, c_len, h, a)
        v = v.reshape(b, c_len, h, a)
        attn_weights = jnp.einsum('bqha,bkha->bqkh', q, k)
        attn_weights = jax.nn.softmax(attn_weights * scale, axis=2)
        attn = jnp.einsum('bqvh,bvha->bqha', attn_weights, v).reshape(b, q_len, hd)
        gem = jnp.exp((z_max + jnp.log(attn)) / p) - shift
        return gem @ Wout.T

    def _L2_ffn_ref(x, Wg, W1, b1, Wo, bo):
        import jax, jax.numpy as jnp
        import numpy as np
        TOP_K = 2
        EPS = 1e-09
        E = Wg.shape[0]
        gate_logits = jnp.einsum('btd,ed->bte', x, Wg)
        gate_scores = jax.nn.softmax(gate_logits, axis=-1)
        topk_val, topk_idx = jax.lax.top_k(gate_scores, TOP_K)
        topk_val = topk_val / (topk_val.sum(axis=-1, keepdims=True) + EPS)
        comb = (jax.nn.one_hot(topk_idx, E, dtype=x.dtype) * topk_val[..., None]).sum(axis=-2)
        out = jnp.zeros_like(x)
        for e in range(E):
            h = jnp.einsum('btd,hd->bth', x, W1[e]) + b1[e]
            a, b = jnp.split(h, 2, axis=-1)
            g = a * jax.nn.sigmoid(b)
            eo = jnp.einsum('bth,dh->btd', g, Wo) + bo
            out = out + eo * comb[..., e:e + 1]
        return out

    def _L3_attn_ref(x, Wq, Wk, Wv, Wo):
        import jax, jax.numpy as jnp
        import numpy as np
        DIM = 128
        N_HEADS = 16
        HEAD_DIM = DIM // N_HEADS
        WINDOW = 32
        STRIDE = 64
        PATTERN = 'combined'

        def _sparse_mask(T):
            rows = jnp.arange(T)[:, None]
            cols = jnp.arange(T)[None, :]
            causal = cols <= rows
            sliding = causal & (cols >= rows - WINDOW + 1)
            strided = causal & ((rows - cols) % STRIDE == 0)
            if PATTERN == 'sliding':
                return sliding
            if PATTERN == 'strided':
                return strided
            return sliding | strided
        B, T, C = x.shape
        scale = HEAD_DIM ** (-0.5)

        def split_heads(t):
            return t.reshape(B, T, N_HEADS, HEAD_DIM).transpose(0, 2, 1, 3)
        Q = split_heads(jnp.einsum('btc,dc->btd', x, Wq))
        K = split_heads(jnp.einsum('btc,dc->btd', x, Wk))
        V = split_heads(jnp.einsum('btc,dc->btd', x, Wv))
        scores = jnp.einsum('bhqd,bhkd->bhqk', Q, K) * scale
        mask = _sparse_mask(T)
        scores = jnp.where(mask[None, None], scores, -jnp.inf)
        attn = jax.nn.softmax(scores, axis=-1)
        attn = jnp.nan_to_num(attn, nan=0.0)
        out = jnp.einsum('bhqk,bhkd->bhqd', attn, V)
        out = out.transpose(0, 2, 1, 3).reshape(B, T, C)
        return jnp.einsum('btc,dc->btd', out, Wo)

    def _L3_xattn_ref(query, key, value, Wq, bq, Wk, bk, Wv, bv, Wo, bo):
        import jax, jax.numpy as jnp
        import numpy as np
        import math
        D_MODEL = 128
        N_HEADS = 16
        HEAD_DIM = D_MODEL // N_HEADS

        def _compute_slopes(n_heads: int) -> np.ndarray:

            def pow2_slopes(n):
                start = 2.0 ** (-2.0 ** (-(math.log2(n) - 3)))
                return [start * start ** i for i in range(n)]
            if math.log2(n_heads).is_integer():
                s = pow2_slopes(n_heads)
            else:
                cp = 2 ** math.floor(math.log2(n_heads))
                s = pow2_slopes(cp) + pow2_slopes(2 * cp)[0::2][:n_heads - cp]
            return np.asarray(s, dtype=np.float32)
        B, Tq, D = query.shape
        Tk = key.shape[1]
        H, hd = (N_HEADS, HEAD_DIM)
        scale = hd ** (-0.5)
        Q = (query @ Wq + bq).reshape(B, Tq, H, hd).transpose(0, 2, 1, 3)
        K = (key @ Wk + bk).reshape(B, Tk, H, hd).transpose(0, 2, 1, 3)
        V = (value @ Wv + bv).reshape(B, Tk, H, hd).transpose(0, 2, 1, 3)
        attn = jnp.einsum('bhqd,bhkd->bhqk', Q, K) * scale
        slopes = jnp.asarray(_compute_slopes(H))
        pos = jnp.arange(Tq)
        dist = -jnp.abs(pos[None, :] - pos[:, None]).astype(jnp.float32)
        bias = slopes[:, None, None] * dist[None]
        attn = attn + bias[None]
        attn = jax.nn.softmax(attn, axis=-1)
        out = jnp.einsum('bhqk,bhkd->bhqd', attn, V)
        out = out.transpose(0, 2, 1, 3).reshape(B, Tq, D)
        return out @ Wo + bo

    def _L3_ffn_ref(x, w_gate, w_up, w_down):
        import jax, jax.numpy as jnp
        import numpy as np
        EPS = 1e-05

        def act_quant(x):
            scale = 127.0 / jnp.clip(jnp.max(jnp.abs(x), axis=-1, keepdims=True), EPS, None)
            q = jnp.clip(jnp.round(x * scale), -128.0, 127.0) / scale
            return x + jax.lax.stop_gradient(q - x)

        def weight_quant(w):
            scale = 1.0 / jnp.clip(jnp.mean(jnp.abs(w)), EPS, None)
            q = jnp.clip(jnp.round(w * scale), -1.0, 1.0) / scale
            return w + jax.lax.stop_gradient(q - w)

        def bitlinear(x, w):
            return act_quant(x) @ weight_quant(w).T
        g = bitlinear(x, w_gate)
        u = bitlinear(x, w_up)
        h = jnp.square(jax.nn.relu(g)) * u
        return bitlinear(h, w_down)
    x = x + _L0_attn_ref(_layernorm(x, axis=-1), L0_attn_c_attn_w, L0_attn_c_attn_b, L0_attn_q2l_w, L0_attn_q2l_b, L0_attn_kv2l_w, L0_attn_kv2l_b, L0_attn_l2o_w, L0_attn_l2o_b, L0_attn_wqk_w, L0_attn_wqk_b, L0_attn_cproj_w, L0_attn_cproj_b)
    x = x + _L0_xattn_ref(_layernorm(x, axis=-1), ctx_1024, ctx_1024, L0_xattn_wq_w, L0_xattn_wq_b, L0_xattn_wk_w, L0_xattn_wk_b, L0_xattn_wv_w, L0_xattn_wv_b, L0_xattn_wo_w, L0_xattn_wo_b)
    x = x + _L0_ffn_ref(_layernorm(x, axis=-1), L0_ffn_Win, L0_ffn_bin_, L0_ffn_W1, L0_ffn_b1, L0_ffn_W2, L0_ffn_b2, L0_ffn_Wout, L0_ffn_bout)
    x = x + _L1_attn_ref(_layernorm(x, axis=-1), L1_attn_pos_phases, L1_attn_Wpv, L1_attn_bpv, L1_attn_Wk, L1_attn_bk, L1_attn_Wkv, L1_attn_bkv, L1_attn_Wg1, L1_attn_bg1, L1_attn_Wg2, L1_attn_bg2, L1_attn_Wb1, L1_attn_bb1, L1_attn_Wb2, L1_attn_bb2, L1_attn_ln_g, L1_attn_ln_b, L1_attn_Wo, L1_attn_bo)
    x = x + _L1_xattn_ref(_layernorm(x, axis=-1), ctx_1024, L1_xattn_wq, L1_xattn_bq, L1_xattn_wk, L1_xattn_bk, L1_xattn_wv, L1_xattn_bv, L1_xattn_wo, L1_xattn_bo)
    x = x + _L1_ffn_ref(_layernorm(x, axis=-1), L1_ffn_W1, L1_ffn_b1, L1_ffn_W2, L1_ffn_b2)
    x = x + _L2_attn_ref(_layernorm(x, axis=-1), L2_attn_Wi, L2_attn_bi, L2_attn_Wh, L2_attn_bh)
    x = x + _L2_xattn_ref(_layernorm(x, axis=-1), ctx_1024, L2_xattn_WQ, L2_xattn_WK, L2_xattn_WV, L2_xattn_Wout, L2_xattn_p_param, L2_xattn_shift)
    x = x + _L2_ffn_ref(_layernorm(x, axis=-1), L2_ffn_Wg, L2_ffn_W1, L2_ffn_b1, L2_ffn_Wo, L2_ffn_bo)
    x = x + _L3_attn_ref(_layernorm(x, axis=-1), L3_attn_Wq, L3_attn_Wk, L3_attn_Wv, L3_attn_Wo)
    x = x + _L3_xattn_ref(_layernorm(x, axis=-1), ctx_1024, ctx_1024, L3_xattn_Wq, L3_xattn_bq, L3_xattn_Wk, L3_xattn_bk, L3_xattn_Wv, L3_xattn_bv, L3_xattn_Wo, L3_xattn_bo)
    x = x + _L3_ffn_ref(_layernorm(x, axis=-1), L3_ffn_w_gate, L3_ffn_w_up, L3_ffn_w_down)
    return x

_drawn_inputs = setup_inputs


def setup_inputs(seed=0):
    import zlib

    import numpy as np

    out = dict(_drawn_inputs(seed))
    spreads = {'L0_attn_c_attn_b': (0.0, 0.8),
     'L0_attn_q2l_b': (0.0, 0.8),
     'L0_attn_kv2l_b': (0.0, 0.8),
     'L0_attn_l2o_b': (0.0, 0.332),
     'L0_attn_wqk_b': (0.0, 0.8),
     'L0_attn_cproj_b': (0.0, 0.1),
     'L0_xattn_wq_b': (0.0, 0.471),
     'L0_xattn_wk_b': (0.0, 2.0),
     'L0_xattn_wv_b': (0.0, 0.1),
     'L0_xattn_wo_b': (0.0, 0.1),
     'L1_attn_bpv': (0.0, 0.1),
     'L1_attn_bk': (0.0, 0.8),
     'L1_attn_bkv': (0.0, 0.312),
     'L1_attn_bg1': (0.0, 2.0),
     'L1_attn_bb1': (0.0, 0.8),
     'L1_attn_bb2': (0.0, 0.8),
     'L1_attn_ln_g': (1.0, 0.6),
     'L1_attn_ln_b': (0.0, 0.8),
     'L1_attn_bo': (0.0, 0.1),
     'L1_xattn_bq': (0.0, 0.788),
     'L1_xattn_bk': (0.0, 2.0),
     'L1_xattn_bv': (0.0, 0.1),
     'L1_xattn_bo': (0.0, 0.1),
     'L1_ffn_b1': (0.0, 0.8),
     'L1_ffn_b2': (0.0, 0.1),
     'L2_attn_bi': (0.0, 0.1),
     'L2_attn_bh': (0.0, 0.1),
     'L2_xattn_shift': (5.0, 0.6),
     'L3_xattn_bq': (0.0, 0.747),
     'L3_xattn_bk': (0.0, 2.0),
     'L3_xattn_bv': (0.0, 0.1),
     'L3_xattn_bo': (0.0, 0.1)}
    factors = {'L0_attn_c_attn_w': 8.0,
     'L0_attn_q2l_w': 8.0,
     'L0_attn_kv2l_w': 8.0,
     'L0_attn_l2o_w': 8.0,
     'L0_attn_wqk_w': 8.0,
     'L0_ffn_bin_': 8.0,
     'L1_attn_Wk': 5.493,
     'L1_attn_Wg1': 8.0,
     'L1_attn_Wg2': 8.0,
     'L1_attn_Wb1': 8.0,
     'L1_attn_Wb2': 8.0,
     'L1_ffn_W1': 5.728,
     'L1_ffn_W2': 4.571,
     'L2_xattn_WQ': 2.821,
     'L2_xattn_WK': 2.759,
     'L2_xattn_p_param': 25.909,
     'L2_ffn_Wg': 6.438,
     'L2_ffn_W1': 5.495,
     'L2_ffn_b1': 8.0,
     'L2_ffn_Wo': 5.419,
     'L2_ffn_bo': 5.691,
     'L3_ffn_w_gate': 8.0,
     'L3_ffn_w_up': 8.0,
     'L3_ffn_w_down': 8.0}
    for name, (base, spread) in spreads.items():
        noise = np.random.default_rng([zlib.crc32(name.encode()), seed]).standard_normal(out[name].shape)
        drawn = base * np.exp(spread * noise) if base else spread * noise
        out[name] = jnp.asarray(drawn.astype(out[name].dtype))
    for name, factor in factors.items():
        out[name] = (out[name] * factor).astype(out[name].dtype)
    return out
```

```python
from contextlib import ExitStack

import numpy as np

import concourse.bass as bass
from concourse import mybir

ALU = mybir.AluOpType
ACT = mybir.ActivationFunctionType
AXIS_X = mybir.AxisListType.X
F32 = mybir.dt.float32
BF16 = mybir.dt.bfloat16

B, T, D = 8, 128, 128
H, HD = 16, 8
HH = H // 2
LAT, GROUPS = 32, 4
HB = B // 2
FF = 512
M, INNER = 64, 16
EXPERTS, EH = 8, 256
LN_EPS = 1e-5
MASKED = -1e30
ROUND = 12582912.0
PI = float(np.float32(np.pi))
PI_BELOW = float(np.nextafter(np.float32(np.pi), np.float32(0)))
LOG_LIFT = 60

COLUMNS = {
    "L0": [("qkv", 3 * D), ("q_lat", 4 * 128), ("q_swap", 4 * 128), ("kv_lat", 4 * 128), ("k_swap", 4 * 128),
           ("l2o", 4 * 128), ("wqk", 128), ("cproj", D), ("qkv_b", 3), ("q_lat_b", 1), ("q_swap_b", 1),
           ("kv_lat_b", 1), ("k_swap_b", 1), ("wqk_b", 1), ("l2o_b", 1), ("cproj_b", D),
           ("cos", T), ("sin", T), ("causal", T),
           ("xq", D), ("xk", D), ("xv", D), ("xo", D), ("xq_b", 1), ("xk_b", 1), ("xv_b", D), ("xo_b", D),
           ("win", 128), ("wout", D), ("bin", 1), ("w1", 8), ("b1", 8), ("w2", 8), ("b2", 1), ("bout", D)],
    "L1": [("phases", T), ("wpv", D), ("wk", D), ("wkv", D), ("wg1", D), ("wg1_shift", D), ("wg2", D),
           ("wb1", 64), ("wb2_0", D), ("wb2_1", D), ("wo", D), ("bpv", 1), ("bk", 1), ("bkv", 1), ("bg1", 1),
           ("bg2", 1), ("bb1", 1), ("bb2_0", 1), ("bb2_1", 1), ("ln_g", 1), ("ln_b", 1), ("bo", D),
           ("xq", D), ("xk", D), ("xv", D), ("xo", D), ("xq_b", 1), ("xk_b", 1), ("xv_b", D), ("xo_b", D),
           ("up", FF), ("down", FF), ("up_b", FF), ("down_b", D)],
    "L2": [("wi", D), ("wh", D), ("ih_b", 2 * D), ("xq", D), ("xk", D), ("xv", D), ("xo", D), ("p", 1), ("shift", 1),
           ("wg", EXPERTS), ("experts", EXPERTS * 2 * EH), ("experts_b", EXPERTS * 4), ("wo", 2 * D), ("bo", D)],
    "L3": [("sq", D), ("sk", D), ("sv", D), ("so", D), ("sparse", T),
           ("xq", D), ("xk", D), ("xv", D), ("xo", D), ("xq_b", 1), ("xk_b", 1), ("xv_b", D), ("xo_b", D),
           ("alibi", H * T), ("gate", FF), ("up", FF), ("down", FF)],
    "C": [("identity", 128), ("head_mask", H), ("latent_mask", GROUPS), ("pick", EXPERTS * 128), ("priority", EXPERTS)],
}
WIDTH = {pack: sum(w for _, w in parts) for pack, parts in COLUMNS.items()}


class Steps:

    def __init__(self):
        self.base, self.names, self.n = 0, [], 0

    def plan(self, *names):
        assert self.n == len(self.names), self.names[self.n:]
        self.base += self.n
        self.names, self.n = [x for name in names for x in ([name] if isinstance(name, str) else name)], 0

    def step(self, name):
        assert self.names[self.n] == name, (self.names[self.n], name)
        self.n += 1
        return 1

    def after(self, name):
        return self.base + self.names.index(name) + 1


def batches(engine, first, last):
    yield first
    with engine.Fori(first + 1, last) as b:
        yield b


def build(nc, packs, x_dram, ctx_dram, out_dram):
    with ExitStack() as ctx:
        def sb(name, shape, dt=F32):
            return ctx.enter_context(nc.sbuf_tensor(name, shape, dt))

        def sem(name):
            return ctx.enter_context(nc.semaphore(name))

        weights = {p: sb(f"weights_{p}", [128, WIDTH[p]]) for p in COLUMNS}
        where = {}
        for p, parts in COLUMNS.items():
            at = 0
            for name, w in parts:
                where[p, name] = (at, w)
                at += w

        def W(pack, name, start=0, width=None, rows=slice(0, 128)):
            at, w = where[pack, name]
            return weights[pack][rows, at + start:at + start + (w - start if width is None else width)]

        def over_batches(table, n):
            return table.unsqueeze(1).broadcast_to([128, n, table.shape[1]])

        residual = sb("residual", [128, B, D])
        normed = sb("normed", [128, B, D])
        normedT_padded = sb("normedT_padded", [128, B, T + 1])
        normedT = normedT_padded[:, :, 1:T + 1]
        contextT = sb("contextT", [128, B, T])
        stats = sb("stats", [128, B, 6])
        moments = sb("moments", [128, B, 2])
        rstd = sb("rstd", [128, B])
        minus_half = sb("minus_half", [128, B])
        ones = sb("ones", [128, 512])
        values = sb("values", [128, B, H, HD + 1])
        qT = sb("qT", [128, GROUPS, T])
        kT = sb("kT", [128, T])
        k_heads = sb("k_heads", [128, H, T])
        shifted = sb("shifted", [128, H, T])
        probs = sb("probs", [128, H, T])
        probsT = sb("probsT", [128, H, T])
        row_max = sb("row_max", [128, H])
        row_rec = sb("row_rec", [128, H])
        small = sb("small", [128, 24, 8])
        half_pi = sb("half_pi", [128, 1])
        minus_round = sb("minus_round", [128, 1])
        ident16 = sb("ident16", [128, 128], BF16)
        scratch = sb("scratch", [128, 14, B, T])
        psum = ctx.enter_context(nc.psum_tensor("psum", [128, 8, 512], F32))

        ident = W("C", "identity")

        pe_done, act_done, vec_done, pool_done = (sem(x) for x in ("pe_done", "act_done", "vec_done", "pool_done"))
        P, A, V, G = Steps(), Steps(), Steps(), Steps()
        (qk_made, q_ready, k_ready, scores_made, half_shifted, half_exp, half_turned, half_copied, pv_made,
         ctx_made, max_made, rec_made, biased_made) = (sem(x) for x in (
             "qk_made", "q_ready", "k_ready", "scores_made", "half_shifted", "half_exp", "half_turned", "half_copied",
             "pv_made", "ctx_made", "max_made", "rec_made", "biased_made"))
        state_made, sum_made = sem("state_made"), sem("sum_made")
        loaded = {name: sem(f"loaded_{name}") for name in ("C", "x", "ctx", "L0", "L1", "L2", "L3")}
        stored = sem("stored")

        def plan(pe=(), act=(), vec=(), pool=()):
            P.plan(*pe), A.plan(*act), V.plan(*vec), G.plan(*pool)

        def bank(n, width=512, rows=128):
            return psum[0:rows, n, 0:width]

        def banks(n, m):
            return psum[:, n:n + m, :].rearrange("p k c -> p (k c)")

        def by_batch(n, m=1):
            return psum[:, n:n + m, :].rearrange("p k (b c) -> p (k b) c", c=128)

        def S(i):
            return scratch[:, i]

        def flat(ap):
            return ap.rearrange("p b c -> p (b c)")

        plan(pe=["ctxT0", "ctxT1"], act=["ctx0", "ctx1"], vec=["const"])
        with nc.Block() as block:
            @block.sync
            def _(sync):
                sync.dma_start(weights["C"][:], packs["C"]).then_inc(loaded["C"], 16)
                sync.dma_start(residual[:], x_dram.rearrange("b t d -> t b d")).then_inc(loaded["x"], 16)
                sync.dma_start(S(0), ctx_dram.rearrange("b t d -> t b d")).then_inc(loaded["ctx"], 16)
                for p in ("L0", "L1", "L2", "L3"):
                    sync.dma_start(weights[p][:], packs[p]).then_inc(loaded[p], 16)

            @block.gpsimd
            def _(pool):
                if FIRST:
                    for x in loaded.values():
                        pool.wait_ge(x, 16)

            @block.vector
            def _(vec):
                vec.memset(ones[:], 1.0)
                vec.memset(values[:], 1.0)
                vec.memset(minus_half[:], -0.5)
                vec.memset(half_pi[:], float(np.pi / 2))
                vec.memset(minus_round[:], -ROUND)
                vec.wait_ge(loaded["C"], 16)
                vec.tensor_copy(ident16[:], ident)
                vec.memset(normedT_padded[:, :, 0:1], 0.0).then_inc(vec_done, V.step("const"))

            @block.tensor
            def _(pe):
                pe.wait_ge(loaded["C"], 16)
                pe.wait_ge(loaded["ctx"], 16)
                for h in range(2):
                    for i in range(HB):
                        last = pe.transpose(by_batch(h)[:, i], S(0)[:, HB * h + i], ident)
                    last.then_inc(pe_done, P.step(f"ctxT{h}"))

            @block.scalar
            def _(act):
                for h in range(2):
                    act.wait_ge(pe_done, P.after(f"ctxT{h}"))
                    act.copy(contextT[:, HB * h:HB * h + HB], by_batch(h)).then_inc(act_done, A.step(f"ctx{h}"))

        LN = dict(pe=["xT0", "xT1"], act=["xnT0", "xnT1"], vec=["stats", "aggr", "xn0", "xn1"], pool=["eps", "rstd"])

        def ln_vector(vec, source, target):
            vec.wait_ge(loaded["x"], 16)
            for b in range(B):
                last = vec.bn_stats(stats[:, b], source[:, b])
            last.then_inc(vec_done, V.step("stats"))
            vec.wait_ge(vec_done, V.after("stats"))
            for b in range(B):
                last = vec.bn_aggr(moments[:, b], stats[:, b])
            last.then_inc(vec_done, V.step("aggr"))
            vec.wait_ge(pool_done, G.after("rstd"))
            for h in range(2):
                for b in range(HB * h, HB * h + HB):
                    last = vec.tensor_scalar(target[:, b], source[:, b], moments[:, b, 0:1], rstd[:, b:b + 1],
                                             ALU.subtract, ALU.mult)
                last.then_inc(vec_done, V.step(f"xn{h}"))

        def ln_pool(pool):
            pool.wait_ge(vec_done, V.after("aggr"))
            pool.tensor_scalar(rstd[:], moments[:, :, 1], LN_EPS, None, ALU.add).then_inc(pool_done, G.step("eps"))
            pool.wait_ge(pool_done, G.after("eps"))
            pool.tensor_tensor(rstd[:], rstd[:], minus_half[:], ALU.pow).then_inc(pool_done, G.step("rstd"))

        def ln_tensor(pe):
            for h in range(2):
                pe.wait_ge(vec_done, V.after(f"xn{h}"))
                for i in range(HB):
                    last = pe.transpose(by_batch(h)[:, i], normed[:, HB * h + i], ident)
                last.then_inc(pe_done, P.step(f"xT{h}"))

        def ln_scalar(act):
            for h in range(2):
                act.wait_ge(pe_done, P.after(f"xT{h}"))
                act.copy(normedT[:, HB * h:HB * h + HB], by_batch(h)).then_inc(act_done, A.step(f"xnT{h}"))

        def add_bias(pool, bias):
            pool.wait_ge(vec_done, V.after("xn1"))
            pool.tensor_tensor(residual[:], residual[:], over_batches(bias, B), ALU.add).then_inc(
                pool_done, G.step("bias"))

        def half(ap, h):
            return ap[:, HB * h:HB * h + HB]

        attentions = {"all": 0, "biased": 0}

        def heads_first(h):
            return by_batch(2 * h, 2)

        def attention_loop(scale, table=None, q=None, q_b=None, k=None, k_b=None, k_source=None, latent=None):
            first = B * attentions["all"]
            first_biased = B * attentions["biased"]
            attentions["all"] += 1
            attentions["biased"] += table is not None
            ctx_all = normed

            with nc.Block() as block:
                @block.tensor
                def _(pe):
                    def project(b):
                        if not (isinstance(b, int) and b == 0):
                            pe.wait_ge(q_ready, first + b)
                        if latent is None:
                            pe.matmul(bank(6)[:, 0:T], q, normedT[:, bass.ds(b, 1)], start=True, stop=True)
                            last = pe.matmul(bank(6)[:, T:2 * T], k, k_source[:, bass.ds(b, 1)], start=True, stop=True)
                        else:
                            for g in range(GROUPS):
                                last = pe.matmul(bank(6)[:, g * T:(g + 1) * T], W("L0", "wqk"),
                                                 latent[0][:, g, bass.ds(b, 1)], start=True, stop=True)
                        last.then_inc(qk_made, 1)

                    def scores(b, h):
                        pe.wait_ge(k_ready, first + b + 1)
                        if not (isinstance(b, int) and b == 0):
                            pe.wait_ge(half_shifted, 2 * first + 2 * b + h - 1)
                        for g in range(2):
                            quad = 2 * h + g
                            last = pe.matmul(bank(quad), qT[:, quad if latent else 0],
                                             k_heads[:, 4 * quad:4 * quad + 4], start=True, stop=True)
                        last.then_inc(scores_made, 1)

                    def turn(b, h):
                        pe.wait_ge(half_exp, 2 * first + 2 * b + h + 1)
                        if not (isinstance(b, int) and b == 0 and h == 0):
                            pe.wait_ge(half_copied, 2 * first + 2 * b + h)
                        for i in range(HH):
                            last = pe.transpose(by_batch(4, 2)[:, i], probs[:, HH * h + i], ident)
                        last.then_inc(half_turned, 1)

                    def weigh(b):
                        if not (isinstance(b, int) and b == 0):
                            pe.wait_ge(ctx_made, first + b)
                        for i in range(H):
                            if i % HH == 0:
                                pe.wait_ge(half_copied, 2 * first + 2 * b + i // HH + 1)
                            last = pe.matmul(bank(7)[:, i * (HD + 1):(i + 1) * (HD + 1)], probsT[:, i],
                                             values[:, bass.ds(b, 1), i], start=True, stop=True)
                        last.then_inc(pv_made, 1)

                    project(0)
                    scores(0, 0)
                    scores(0, 1)
                    project(1)
                    for b in batches(pe, 1, B - 1):
                        scores(b, 0)
                        turn(b - 1, 0)
                        scores(b, 1)
                        project(b + 1)
                        turn(b - 1, 1)
                        weigh(b - 1)
                    scores(B - 1, 0)
                    turn(B - 2, 0)
                    scores(B - 1, 1)
                    turn(B - 2, 1)
                    weigh(B - 2)
                    turn(B - 1, 0)
                    turn(B - 1, 1)
                    weigh(B - 1)

                @block.scalar
                def _(act):
                    act.preload_act_table(ACT.Exp)

                    def take(b):
                        act.wait_ge(qk_made, first + b + 1)
                        if latent is not None:
                            act.activation(flat(qT[:]), bank(6), ACT.Identity,
                                           bias=W("L0", "wqk_b")).then_inc(q_ready, 1)
                        elif q_b is None:
                            act.copy(qT[:, 0], bank(6)[:, 0:T])
                            act.copy(kT[:], bank(6)[:, T:2 * T]).then_inc(q_ready, 1)
                        else:
                            act.activation(qT[:, 0], bank(6)[:, 0:T], ACT.Identity, bias=q_b)
                            act.activation(kT[:], bank(6)[:, T:2 * T], ACT.Identity, bias=k_b).then_inc(q_ready, 1)

                    def exponential(b, h):
                        act.wait_ge(half_shifted, 2 * first + 2 * b + h + 1)
                        if not (isinstance(b, int) and b == 0):
                            act.wait_ge(half_turned, 2 * first + 2 * b + h - 1)
                        act.activation(flat(probs[:, HH * h:HH * h + HH]), flat(shifted[:, HH * h:HH * h + HH]),
                                       ACT.Exp, scale=scale if table is None else 1.0).then_inc(half_exp, 1)

                    def copy(b, h):
                        act.wait_ge(half_turned, 2 * first + 2 * b + h + 1)
                        if not (isinstance(b, int) and b == 0):
                            act.wait_ge(pv_made, first + b)
                        act.copy(flat(probsT[:, HH * h:HH * h + HH]), banks(4, 2)).then_inc(half_copied, 1)

                    def batch(b, more):
                        exponential(b, 0)
                        exponential(b, 1)
                        copy(b, 0)
                        if more:
                            take(b + 2)
                        copy(b, 1)

                    take(0)
                    take(1)
                    for b in batches(act, 0, B - 2):
                        batch(b, True)
                    batch(B - 2, False)
                    batch(B - 1, False)

                @block.gpsimd
                def _(pool):
                    for b in batches(pool, 0, B):
                        pool.wait_ge(q_ready, first + b + 1)
                        if latent is None:
                            pool.tensor_tensor(k_heads[:], kT[:].unsqueeze(1).broadcast_to([128, H, T]),
                                               W("C", "head_mask").unsqueeze(2).broadcast_to([128, H, T]),
                                               ALU.mult).then_inc(k_ready, 1)
                        else:
                            for g in range(GROUPS):
                                last = pool.tensor_tensor(
                                    k_heads[:, 4 * g:4 * g + 4],
                                    latent[1][:, g, bass.ds(b, 1)].broadcast_to([128, 4, T]),
                                    W("C", "latent_mask").unsqueeze(2).broadcast_to([128, 4, T]), ALU.mult)
                            last.then_inc(k_ready, 1)

                @block.vector
                def _(vec):
                    def shift(b, h):
                        heads = slice(HH * h, HH * h + HH)
                        peak = row_max[:, heads].unsqueeze(2).broadcast_to([128, HH, T])
                        vec.wait_ge(scores_made, 2 * first + 2 * b + h + 1)
                        if not (isinstance(b, int) and b == 0):
                            vec.wait_ge(half_exp, 2 * first + 2 * b + h - 1)
                            vec.wait_ge(half_shifted, 2 * first + 2 * b + h - 1)
                        if table is None:
                            source = heads_first(h)
                        else:
                            source = shifted[:, heads]
                            bias = (table[:, HH * h * T:(HH * h + HH) * T].rearrange("p (h k) -> p h k", k=T)
                                    if table.shape[1] > T else over_batches(table, HH))
                            vec.scalar_tensor_tensor(out=source, in0=heads_first(h), scalar=scale, in1=bias,
                                                     op0=ALU.mult, op1=ALU.add).then_inc(biased_made, 1)
                            vec.wait_ge(biased_made, 2 * first_biased + 2 * b + h + 1)
                        vec.tensor_reduce(row_max[:, heads], source, AXIS_X, ALU.max).then_inc(max_made, 1)
                        vec.wait_ge(max_made, 2 * first + 2 * b + h + 1)
                        vec.tensor_tensor(shifted[:, heads], source, peak, ALU.subtract).then_inc(half_shifted, 1)

                    def normalise(b):
                        sums = bank(7)[:, 0:H * (HD + 1)].rearrange("p (h d) -> p h d", d=HD + 1)
                        vec.wait_ge(pv_made, first + b + 1)
                        if not (isinstance(b, int) and b == 0):
                            vec.wait_ge(ctx_made, first + b)
                        vec.reciprocal(row_rec[:], sums[:, :, HD]).then_inc(rec_made, 1)
                        vec.wait_ge(rec_made, first + b + 1)
                        vec.tensor_tensor(ctx_all[:, bass.ds(b, 1)].rearrange("p b (h d) -> p (b h) d", d=HD),
                                          sums[:, :, 0:HD], row_rec[:].unsqueeze(2).broadcast_to([128, H, HD]),
                                          ALU.mult).then_inc(ctx_made, 1)

                    shift(0, 0)
                    shift(0, 1)
                    for b in batches(vec, 1, B):
                        shift(b, 0)
                        shift(b, 1)
                        normalise(b - 1)
                    normalise(B - 1)

        def attention_out(wo, bias=None, gem=None):
            ctxT = S(13)
            plan(pe=["cT0", "cT1", "o0", "o1"], vec=[] if gem is None else ["z0", "z1", "s0", "s1"],
                 act=["c0", "c1"] if gem is None else ["l0", "l1", "c0", "c1"])
            V.names += ["r0", "r1"]
            with nc.Block() as block:
                @block.tensor
                def _(pe):
                    for h in range(2):
                        for i in range(HB):
                            last = pe.transpose(by_batch(h)[:, i], normed[:, HB * h + i], ident)
                        last.then_inc(pe_done, P.step(f"cT{h}"))
                    for h in range(2):
                        if gem is None:
                            pe.wait_ge(act_done, A.after(f"c{h}"))
                        else:
                            pe.wait_ge(vec_done, V.after(f"s{h}"))
                        for i in range(HB):
                            last = pe.matmul(by_batch(2 + h)[:, i], ctxT[:, HB * h + i], wo, start=True, stop=True)
                        last.then_inc(pe_done, P.step(f"o{h}"))

                @block.scalar
                def _(act):
                    if gem is not None:
                        for h in range(2):
                            act.wait_ge(pe_done, P.after(f"cT{h}"))
                            act.activation(half(ctxT, h), by_batch(h), ACT.Ln, scale=2.0 ** LOG_LIFT).then_inc(
                                act_done, A.step(f"l{h}"))
                    for h in range(2):
                        if gem is not None:
                            act.wait_ge(vec_done, V.after(f"z{h}"))
                            act.activation(half(ctxT, h), half(ctxT, h), ACT.Exp, scale=gem[1]).then_inc(
                                act_done, A.step(f"c{h}"))
                            continue
                        act.wait_ge(pe_done, P.after(f"cT{h}"))
                        if bias is None:
                            last = act.copy(half(ctxT, h), by_batch(h))
                        else:
                            last = act.activation(half(ctxT, h), by_batch(h), ACT.Identity, bias=bias)
                        last.then_inc(act_done, A.step(f"c{h}"))

                @block.vector
                def _(vec):
                    if gem is not None:
                        for h in range(2):
                            vec.wait_ge(act_done, A.after(f"l{h}"))
                            vec.scalar_tensor_tensor(
                                out=half(ctxT, h), in0=half(ctxT, h), scalar=-LOG_LIFT * float(np.log(2.0)),
                                in1=gem[0][:, HB * h:HB * h + HB].unsqueeze(2).broadcast_to([128, HB, T]),
                                op0=ALU.add, op1=ALU.add).then_inc(vec_done, V.step(f"z{h}"))
                        for h in range(2):
                            vec.wait_ge(act_done, A.after(f"c{h}"))
                            vec.tensor_scalar(half(ctxT, h), half(ctxT, h), gem[2], None, ALU.subtract).then_inc(
                                vec_done, V.step(f"s{h}"))
                    for h in range(2):
                        vec.wait_ge(pe_done, P.after(f"o{h}"))
                        vec.tensor_tensor(half(residual, h), half(residual, h), by_batch(2 + h), ALU.add).then_inc(
                            vec_done, V.step(f"r{h}"))

        def attention_prologue(pack, wv, vb, ob, v_source):
            plan(pe=[*LN["pe"], "v0", "v1"], act=LN["act"], vec=[*LN["vec"], "v0", "v1"],
                 pool=[*LN["pool"], *(["bias"] if ob is not None else [])])
            with nc.Block() as block:
                @block.vector
                def _(vec):
                    ln_vector(vec, residual, normed)
                    vec.wait_ge(loaded[pack], 16)
                    for h in range(2):
                        target = half(values, h)[:, :, :, 0:HD].rearrange("p b h d -> p (b h) d")
                        made = bank(2 + h).rearrange("p (b d) -> p b d", d=HD)
                        vec.wait_ge(pe_done, P.after(f"v{h}"))
                        if vb is None:
                            last = vec.tensor_copy(target, made)
                        else:
                            for i in range(HB):
                                last = vec.tensor_tensor(
                                    values[:, HB * h + i, :, 0:HD],
                                    by_batch(2 + h)[:, i].rearrange("p (h d) -> p h d", d=HD),
                                    vb.rearrange("p (h d) -> p h d", d=HD), ALU.add)
                        last.then_inc(vec_done, V.step(f"v{h}"))

                @block.gpsimd
                def _(pool):
                    ln_pool(pool)
                    if ob is not None:
                        pool.wait_ge(loaded[pack], 16)
                        add_bias(pool, ob)

                @block.tensor
                def _(pe):
                    ln_tensor(pe)
                    pe.wait_ge(loaded[pack], 16)
                    for h in range(2):
                        if v_source is normedT:
                            pe.wait_ge(act_done, A.after(f"xnT{h}"))
                        for i in range(HB):
                            last = pe.matmul(by_batch(2 + h)[:, i], v_source[:, HB * h + i], wv, start=True, stop=True)
                        last.then_inc(pe_done, P.step(f"v{h}"))

                @block.scalar
                def _(act):
                    ln_scalar(act)

        def latent_prologue():
            q_rot, k_rot = scratch[:, 0:4], scratch[:, 4:8]
            lat, swapped = S(12), S(13)
            qkvT, vlat = scratch[:, 8:11], S(11)
            groups = [(x, g) for x in "qk" for g in range(GROUPS)]
            plan(pe=[*LN["pe"], "q", "k", "v", *[f"{x}{s}{g}" for x, g in groups for s in ("l", "s")],
                     *[f"v{s}{g}" for g in range(GROUPS) for s in ("l", "o")], "vT"],
                 act=[*LN["act"], "q", "k", "v", *[f"v{g}" for g in range(GROUPS)], "vo"],
                 vec=[*LN["vec"], *[f"{x}{s}{g}" for x, g in groups for s in ("c", "s", "r")], "v"],
                 pool=[*LN["pool"], "bias"])
            with nc.Block() as block:
                @block.vector
                def _(vec):
                    ln_vector(vec, residual, normed)
                    for u, (x, g) in enumerate(groups):
                        bias = "q_lat_b" if x == "q" else "kv_lat_b"
                        swap = "q_swap_b" if x == "q" else "k_swap_b"
                        vec.wait_ge(pe_done, P.after(f"{x}l{g}"))
                        if u:
                            vec.wait_ge(vec_done, V.base + len(LN["vec"]) + 3 * u)
                        vec.scalar_tensor_tensor(out=lat, in0=by_batch(4 * (u % 2), 2), scalar=W("L0", bias),
                                                 in1=over_batches(W("L0", "cos"), B), op0=ALU.add,
                                                 op1=ALU.mult).then_inc(vec_done, V.step(f"{x}c{g}"))
                        vec.wait_ge(pe_done, P.after(f"{x}s{g}"))
                        vec.scalar_tensor_tensor(out=swapped, in0=by_batch(4 * (u % 2) + 2, 2), scalar=W("L0", swap),
                                                 in1=over_batches(W("L0", "sin"), B), op0=ALU.add,
                                                 op1=ALU.mult).then_inc(vec_done, V.step(f"{x}s{g}"))
                        vec.wait_ge(vec_done, V.after(f"{x}s{g}"))
                        vec.tensor_tensor((q_rot if x == "q" else k_rot)[:, g], lat, swapped,
                                          ALU.add).then_inc(vec_done, V.step(f"{x}r{g}"))
                    vec.wait_ge(pe_done, P.after("vT"))
                    vec.tensor_copy(values[:, :, :, 0:HD].rearrange("p b h d -> p (b h) d"),
                                    banks(2, 2).rearrange("p (b d) -> p b d", d=HD)).then_inc(vec_done, V.step("v"))

                @block.gpsimd
                def _(pool):
                    ln_pool(pool)
                    pool.wait_ge(loaded["L0"], 16)
                    add_bias(pool, W("L0", "cproj_b"))

                @block.tensor
                def _(pe):
                    def product(n, weight, source, start=True, stop=True):
                        for h in range(2):
                            last = pe.matmul(bank(n + h), weight, half(source, h), start=start, stop=stop)
                        return last

                    ln_tensor(pe)
                    pe.wait_ge(loaded["L0"], 16)
                    pe.wait_ge(act_done, A.after("xnT1"))
                    for j, x in enumerate("qkv"):
                        product(2 + 2 * j, W("L0", "qkv", j * D, D), normedT).then_inc(pe_done, P.step(x))
                    pe.wait_ge(act_done, A.after("v"))
                    for u, (x, g) in enumerate(groups):
                        if u >= 2:
                            px, pg = groups[u - 2]
                            pe.wait_ge(vec_done, V.after(f"{px}s{pg}"))
                        lat_w, swap_w = ("q_lat", "q_swap") if x == "q" else ("kv_lat", "k_swap")
                        source = qkvT[:, "qk".index(x)]
                        product(4 * (u % 2), W("L0", lat_w, g * 128, 128), source).then_inc(
                            pe_done, P.step(f"{x}l{g}"))
                        product(4 * (u % 2) + 2, W("L0", swap_w, g * 128, 128), source).then_inc(
                            pe_done, P.step(f"{x}s{g}"))
                    for g in range(GROUPS):
                        if g == 0:
                            pe.wait_ge(vec_done, V.after("ks3"))
                        else:
                            pe.wait_ge(act_done, A.after(f"v{g - 1}"))
                        product(0, W("L0", "kv_lat", g * 128, 128), qkvT[:, 2]).then_inc(pe_done, P.step(f"vl{g}"))
                        pe.wait_ge(act_done, A.after(f"v{g}"))
                        product(4, W("L0", "l2o", g * 128, 128), vlat, start=g == 0, stop=g == GROUPS - 1).then_inc(
                            pe_done, P.step(f"vo{g}"))
                    pe.wait_ge(act_done, A.after("vo"))
                    for b in range(B):
                        last = pe.transpose(by_batch(2, 2)[:, b], S(12)[:, b], ident)
                    last.then_inc(pe_done, P.step("vT"))

                @block.scalar
                def _(act):
                    ln_scalar(act)
                    act.wait_ge(loaded["L0"], 16)
                    for j, x in enumerate("qkv"):
                        act.wait_ge(pe_done, P.after(x))
                        act.activation(qkvT[:, j], by_batch(2 + 2 * j, 2), ACT.Identity,
                                       bias=W("L0", "qkv_b", j, 1)).then_inc(act_done, A.step(x))
                    for g in range(GROUPS):
                        act.wait_ge(pe_done, P.after(f"vl{g}"))
                        if g:
                            act.wait_ge(pe_done, P.after(f"vo{g - 1}"))
                        act.activation(vlat, by_batch(0, 2), ACT.Identity, bias=W("L0", "kv_lat_b")).then_inc(
                            act_done, A.step(f"v{g}"))
                    act.wait_ge(pe_done, P.after("vo3"))
                    act.wait_ge(vec_done, V.after("kr3"))
                    act.copy(S(12), by_batch(4, 2)).then_inc(act_done, A.step("vo"))
            return q_rot, k_rot

        def hinge_ffn():
            steps = INNER // 2
            s, g = S(0), S(1)
            hinge = [S(2), S(3)]
            plan(pe=[*LN["pe"], "s", "o0", "o1"], act=[*LN["act"], "s", *[f"h{i}" for i in range(steps)]],
                 vec=[*LN["vec"], *[f"g{i}" for i in range(steps)], "r0", "r1"], pool=[*LN["pool"], "bias"])
            with nc.Block() as block:
                @block.vector
                def _(vec):
                    ln_vector(vec, residual, normed)
                    for i in range(steps):
                        vec.wait_ge(act_done, A.after(f"h{i}"))
                        w2 = W("L0", "w2", i, 1)
                        if i == 0:
                            last = vec.tensor_scalar(g, hinge[0], w2, W("L0", "b2"), ALU.mult, ALU.add)
                        else:
                            vec.wait_ge(vec_done, V.after(f"g{i - 1}"))
                            last = vec.scalar_tensor_tensor(out=g, in0=hinge[i % 2], scalar=w2, in1=g, op0=ALU.mult,
                                                            op1=ALU.add)
                        last.then_inc(vec_done, V.step(f"g{i}"))
                    vec.wait_ge(pool_done, G.after("bias"))
                    for h in range(2):
                        vec.wait_ge(pe_done, P.after(f"o{h}"))
                        vec.tensor_tensor(half(residual, h), half(residual, h), by_batch(4 + h), ALU.add).then_inc(
                            vec_done, V.step(f"r{h}"))

                @block.gpsimd
                def _(pool):
                    ln_pool(pool)
                    add_bias(pool, W("L0", "bout"))

                @block.tensor
                def _(pe):
                    ln_tensor(pe)
                    for h in range(2):
                        pe.wait_ge(act_done, A.after(f"xnT{h}"))
                        last = pe.matmul(bank(2 + h), W("L0", "win"), half(normedT, h), start=True, stop=True)
                    last.then_inc(pe_done, P.step("s"))
                    pe.wait_ge(vec_done, V.after(f"g{steps - 1}"))
                    for h in range(2):
                        for i in range(HB):
                            last = pe.matmul(by_batch(4 + h)[:, i], g[:, HB * h + i], W("L0", "wout"), start=True,
                                             stop=True)
                        last.then_inc(pe_done, P.step(f"o{h}"))

                @block.scalar
                def _(act):
                    ln_scalar(act)
                    act.wait_ge(pe_done, P.after("s"))
                    act.activation(s, by_batch(2, 2), ACT.Identity, bias=W("L0", "bin")).then_inc(
                        act_done, A.step("s"))
                    act.wait_ge(act_done, A.after("s"))
                    for i in range(steps):
                        if i >= 2:
                            act.wait_ge(vec_done, V.after(f"g{i - 2}"))
                        act.activation(hinge[i % 2], s, ACT.Relu, bias=W("L0", "b1", i, 1),
                                       scale=W("L0", "w1", i, 1)).then_inc(act_done, A.step(f"h{i}"))

        stages = []

        def stage(f):
            stages.append(f)

        stage(lambda: (
            attention_loop(LAT ** -0.5, table=W("L0", "causal"), latent=latent_prologue()),
            attention_out(W("L0", "cproj"), bias=W("L0", "l2o_b"))))

        def cross(pack):
            attention_prologue(pack, W(pack, "xv"), W(pack, "xv_b"), W(pack, "xo_b"), contextT)
            attention_loop(HD ** -0.5, q=W(pack, "xq"), q_b=W(pack, "xq_b"), k=W(pack, "xk"), k_b=W(pack, "xk_b"),
                           k_source=contextT, table=W("L3", "alibi") if pack == "L3" else None)
            attention_out(W(pack, "xo"))

        stage(lambda: cross("L0"))
        stage(hinge_ffn)

        def phase_memory():
            pv, keys, kv, hidden, branch, gates, logit1, diff, w_pos, w_kv, angle, sin_k, cos_k = (
                S(i) for i in range(13))
            tmp = S(13)
            sin_p, cos_p, turns, red, absolute = (shifted[:, i] for i in range(5))
            carry = probs[:, 0:B]
            a0, a1, m0, m1 = (x for x in (probs[:, B:H], probsT[:, 0:B], probsT[:, B:H], k_heads[:, 0:B]))
            m2, m3 = k_heads[:, B:H], tmp
            w = lambda name: W("L1", name)
            c1, c2 = 6.28125, float(2 * np.pi - 6.28125)
            plan(pe=[*LN["pe"], "pv", "keys", "kv", "hidden", "branch", "gate", "l0", "l1", "turn", "lnT", "out"],
                 act=[*LN["act"], "pv", "kv", "sin_p", "abs_p", "cos_p", "keys", "hidden", "branch", "l1", "gates",
                      "w_pos", "w_kv", "sin_k", "abs_k", "cos_k", "sqrt", "tokens", "ln"],
                 vec=[*LN["vec"], "const", "p0", "p1", "p2", "p3", "p4", "diff", "k0", "angle",
                      "cv", "cm", "sv", "sm", "pc", "ps", "p", "vg", "wc", "wm", "ws", "wn", "g", "gmax", "rec",
                      "kc", "ks", "k", "kn", "bp", "bk", "b", "scaled",
                      *[x + "2" for x in LN["vec"]], "r0", "r1"],
                 pool=[*LN["pool"], "bias", "input", "eps2", "rstd2"])
            with nc.Block() as block:
                @block.tensor
                def _(pe):
                    def product(n, weight, source, start=True, stop=True, rows=128):
                        for h in range(2):
                            last = pe.matmul(bank(n + h, rows=rows), weight, half(source, h), start=start, stop=stop)
                        return last

                    ln_tensor(pe)
                    pe.wait_ge(loaded["L1"], 16)
                    pe.wait_ge(act_done, A.after("xnT1"))
                    product(0, w("wpv"), normedT).then_inc(pe_done, P.step("pv"))
                    product(2, w("wk"), normedT).then_inc(pe_done, P.step("keys"))
                    product(4, w("wkv"), normedT).then_inc(pe_done, P.step("kv"))
                    product(6, w("wg1"), normedT, stop=False)
                    product(6, w("wg1_shift"), normedT_padded[:, :, 0:T], start=False).then_inc(
                        pe_done, P.step("hidden"))
                    pe.wait_ge(act_done, A.after("pv"))
                    product(0, w("wb1"), normedT, rows=64).then_inc(pe_done, P.step("branch"))
                    pe.wait_ge(act_done, A.after("hidden"))
                    product(6, w("wg2"), hidden).then_inc(pe_done, P.step("gate"))
                    pe.wait_ge(act_done, A.after("branch"))
                    product(2, W("L1", "wb2_0", rows=slice(0, 64)), branch[0:64]).then_inc(pe_done, P.step("l0"))
                    product(4, W("L1", "wb2_1", rows=slice(0, 64)), branch[0:64]).then_inc(pe_done, P.step("l1"))
                    pe.wait_ge(vec_done, V.after("scaled"))
                    for b in range(B):
                        last = pe.transpose(by_batch(0, 2)[:, b], a0[:, b], ident)
                    last.then_inc(pe_done, P.step("turn"))
                    pe.wait_ge(vec_done, V.after("xn12"))
                    for b in range(B):
                        last = pe.transpose(by_batch(2, 2)[:, b], a1[:, b], ident)
                    last.then_inc(pe_done, P.step("lnT"))
                    pe.wait_ge(act_done, A.after("ln"))
                    for b in range(B):
                        last = pe.matmul(by_batch(4, 2)[:, b], m0[:, b], w("wo"), start=True, stop=True)
                    last.then_inc(pe_done, P.step("out"))

                @block.scalar
                def _(act):
                    ln_scalar(act)
                    act.wait_ge(pe_done, P.after("pv"))
                    act.activation(pv, by_batch(0, 2), ACT.Identity, bias=w("bpv")).then_inc(act_done, A.step("pv"))
                    act.wait_ge(pe_done, P.after("kv"))
                    act.activation(kv, by_batch(4, 2), ACT.Identity, bias=w("bkv")).then_inc(act_done, A.step("kv"))
                    act.wait_ge(vec_done, V.after("p4"))
                    act.activation(sin_p, red, ACT.Sin).then_inc(act_done, A.step("sin_p"))
                    act.activation(absolute, red, ACT.Abs).then_inc(act_done, A.step("abs_p"))
                    act.wait_ge(act_done, A.after("abs_p"))
                    act.activation(cos_p, absolute, ACT.Sin, bias=half_pi[:], scale=-1.0).then_inc(
                        act_done, A.step("cos_p"))
                    act.wait_ge(pe_done, P.after("keys"))
                    act.activation(keys, by_batch(2, 2), ACT.Tanh, bias=w("bk")).then_inc(act_done, A.step("keys"))
                    act.wait_ge(pe_done, P.after("hidden"))
                    act.activation(hidden, by_batch(6, 2), ACT.Gelu, bias=w("bg1")).then_inc(
                        act_done, A.step("hidden"))
                    act.wait_ge(pe_done, P.after("branch"))
                    act.activation(branch[0:64], psum[0:64, 0:2, :].rearrange("p k (b c) -> p (k b) c", c=T), ACT.Gelu,
                                   bias=W("L1", "bb1", rows=slice(0, 64))).then_inc(act_done, A.step("branch"))
                    act.wait_ge(pe_done, P.after("l1"))
                    act.activation(logit1, by_batch(4, 2), ACT.Identity, bias=w("bb2_1")).then_inc(
                        act_done, A.step("l1"))
                    act.wait_ge(pe_done, P.after("gate"))
                    act.activation(gates, by_batch(6, 2), ACT.Sigmoid, bias=w("bg2")).then_inc(
                        act_done, A.step("gates"))
                    act.wait_ge(vec_done, V.after("diff"))
                    act.activation(w_pos, diff, ACT.Sigmoid).then_inc(act_done, A.step("w_pos"))
                    act.activation(w_kv, diff, ACT.Sigmoid, scale=-1.0).then_inc(act_done, A.step("w_kv"))
                    act.wait_ge(vec_done, V.after("angle"))
                    act.activation(sin_k, angle, ACT.Sin).then_inc(act_done, A.step("sin_k"))
                    act.wait_ge(act_done, A.after("w_kv"))
                    act.activation(tmp, angle, ACT.Abs).then_inc(act_done, A.step("abs_k"))
                    act.wait_ge(act_done, A.after("abs_k"))
                    act.activation(cos_k, tmp, ACT.Sin, bias=half_pi[:], scale=-1.0).then_inc(
                        act_done, A.step("cos_k"))
                    act.wait_ge(vec_done, V.after("gmax"))
                    act.activation(m3, m3, ACT.Sqrt).then_inc(act_done, A.step("sqrt"))
                    act.wait_ge(pe_done, P.after("turn"))
                    act.copy(a1, by_batch(0, 2)).then_inc(act_done, A.step("tokens"))
                    act.wait_ge(pe_done, P.after("lnT"))
                    act.activation(m0, by_batch(2, 2), ACT.Identity, bias=w("ln_b"), scale=w("ln_g")).then_inc(
                        act_done, A.step("ln"))

                @block.gpsimd
                def _(pool):
                    ln_pool(pool)
                    pool.wait_ge(loaded["L1"], 16)
                    add_bias(pool, w("bo"))
                    pool.wait_ge(pool_done, G.after("bias"))
                    pool.tensor_tensor(residual[:], residual[:], normed[:], ALU.add).then_inc(
                        pool_done, G.step("input"))
                    pool.wait_ge(vec_done, V.after("aggr2"))
                    pool.tensor_scalar(rstd[:], moments[:, :, 1], LN_EPS, None, ALU.add).then_inc(
                        pool_done, G.step("eps2"))
                    pool.wait_ge(pool_done, G.after("eps2"))
                    pool.tensor_tensor(rstd[:], rstd[:], minus_half[:], ALU.pow).then_inc(pool_done, G.step("rstd2"))

                @block.vector
                def _(vec):
                    tt, ts, stt = vec.tensor_tensor, vec.tensor_scalar, vec.scalar_tensor_tensor

                    ln_vector(vec, residual, normed)
                    vec.memset(carry, 1.0).then_inc(vec_done, V.step("const"))
                    vec.wait_ge(loaded["L1"], 16)
                    vec.wait_ge(vec_done, V.after("const"))
                    vec.memset(carry[:, :, 0:1], 0.0)
                    ts(turns, w("phases"), float(1 / (2 * np.pi)), ROUND, ALU.mult, ALU.add).then_inc(
                        vec_done, V.step("p0"))
                    vec.wait_ge(vec_done, V.after("p0"))
                    ts(turns, turns, ROUND, None, ALU.subtract).then_inc(vec_done, V.step("p1"))
                    vec.wait_ge(vec_done, V.after("p1"))
                    stt(out=red, in0=turns, scalar=-c1, in1=w("phases"), op0=ALU.mult, op1=ALU.add).then_inc(
                        vec_done, V.step("p2"))
                    vec.wait_ge(vec_done, V.after("p2"))
                    stt(out=red, in0=turns, scalar=-c2, in1=red, op0=ALU.mult, op1=ALU.add).then_inc(
                        vec_done, V.step("p3"))
                    vec.wait_ge(vec_done, V.after("p3"))
                    ts(red, red, PI_BELOW, -PI_BELOW, ALU.min, ALU.max).then_inc(vec_done, V.step("p4"))
                    vec.wait_ge(act_done, A.after("l1"))
                    stt(out=diff, in0=by_batch(2, 2), scalar=w("bb2_0"), in1=logit1, op0=ALU.add,
                        op1=ALU.subtract).then_inc(vec_done, V.step("diff"))
                    ts(angle, keys, PI, PI_BELOW, ALU.mult, ALU.min).then_inc(vec_done, V.step("k0"))
                    vec.wait_ge(vec_done, V.after("k0"))
                    ts(angle, angle, -PI_BELOW, None, ALU.max).then_inc(vec_done, V.step("angle"))

                    def scan(out, values, name):
                        vec.tensor_tensor_scan(flat(out), flat(carry), flat(values), 0.0, ALU.mult,
                                               ALU.add).then_inc(vec_done, V.step(name))

                    tt(a0, pv, over_batches(cos_p, B), ALU.mult).then_inc(vec_done, V.step("cv"))
                    vec.wait_ge(vec_done, V.after("cv"))
                    scan(m0, a0, "cm")
                    tt(a1, pv, over_batches(sin_p, B), ALU.mult).then_inc(vec_done, V.step("sv"))
                    vec.wait_ge(vec_done, V.after("sv"))
                    scan(m1, a1, "sm")
                    vec.wait_ge(vec_done, V.after("sm"))
                    tt(m0, m0, over_batches(cos_p, B), ALU.mult).then_inc(vec_done, V.step("pc"))
                    tt(m1, m1, over_batches(sin_p, B), ALU.mult).then_inc(vec_done, V.step("ps"))
                    vec.wait_ge(vec_done, V.after("ps"))
                    tt(pv, m0, m1, ALU.add).then_inc(vec_done, V.step("p"))
                    vec.wait_ge(act_done, A.after("cos_k"))
                    tt(kv, kv, gates, ALU.mult).then_inc(vec_done, V.step("vg"))
                    vec.wait_ge(vec_done, V.after("vg"))
                    vec.memset(a0[:, :, 0:1], 0.0)
                    vec.memset(a1[:, :, 0:1], 0.0)
                    tt(a0[:, :, 1:T], cos_k[:, :, 0:T - 1], kv[:, :, 1:T], ALU.mult).then_inc(vec_done, V.step("wc"))
                    vec.wait_ge(vec_done, V.after("wc"))
                    scan(m0, a0, "wm")
                    tt(a1[:, :, 1:T], sin_k[:, :, 0:T - 1], kv[:, :, 1:T], ALU.mult).then_inc(vec_done, V.step("ws"))
                    vec.wait_ge(vec_done, V.after("ws"))
                    scan(m1, a1, "wn")
                    scan(m2, gates, "g")
                    vec.wait_ge(vec_done, V.after("g"))
                    ts(m3, m2, 1.0, None, ALU.max).then_inc(vec_done, V.step("gmax"))
                    vec.wait_ge(act_done, A.after("sqrt"))
                    vec.reciprocal(m2, m3).then_inc(vec_done, V.step("rec"))
                    tt(m0, m0, cos_k, ALU.mult).then_inc(vec_done, V.step("kc"))
                    tt(m1, m1, sin_k, ALU.mult).then_inc(vec_done, V.step("ks"))
                    vec.wait_ge(vec_done, V.after("ks"))
                    tt(m0, m0, m1, ALU.add).then_inc(vec_done, V.step("k"))
                    vec.wait_ge(vec_done, V.after("k"))
                    tt(m0, m0, m2, ALU.mult).then_inc(vec_done, V.step("kn"))
                    tt(a0, pv, w_pos, ALU.mult).then_inc(vec_done, V.step("bp"))
                    vec.wait_ge(vec_done, V.after("bp"))
                    tt(a1, m0, w_kv, ALU.mult).then_inc(vec_done, V.step("bk"))
                    vec.wait_ge(vec_done, V.after("bk"))
                    tt(a0, a0, a1, ALU.add).then_inc(vec_done, V.step("b"))
                    vec.wait_ge(vec_done, V.after("b"))
                    ts(a0, a0, float(D) ** -0.5, None, ALU.mult).then_inc(vec_done, V.step("scaled"))
                    vec.wait_ge(act_done, A.after("tokens"))
                    for b in range(B):
                        last = vec.bn_stats(stats[:, b], a1[:, b])
                    last.then_inc(vec_done, V.step("stats2"))
                    vec.wait_ge(vec_done, V.after("stats2"))
                    for b in range(B):
                        last = vec.bn_aggr(moments[:, b], stats[:, b])
                    last.then_inc(vec_done, V.step("aggr2"))
                    vec.wait_ge(pool_done, G.after("rstd2"))
                    for h in range(2):
                        for b in range(HB * h, HB * h + HB):
                            last = ts(a1[:, b], a1[:, b], moments[:, b, 0:1], rstd[:, b:b + 1], ALU.subtract,
                                      ALU.mult)
                        last.then_inc(vec_done, V.step(f"xn{h}2"))
                    vec.wait_ge(pe_done, P.after("out"))
                    for h in range(2):
                        tt(half(residual, h), half(residual, h), by_batch(4 + h), ALU.add).then_inc(
                            vec_done, V.step(f"r{h}"))

        stage(phase_memory)
        stage(lambda: cross("L1"))

        def quantised_ffn(pack, gated):
            w = lambda name: W(pack, name)
            hidden = scratch[:, 0:4].rearrange("p a b c -> p (a b c)").rearrange("p (b f) -> p b f", f=FF)
            squares = scratch[:, 4:8].rearrange("p a b c -> p (a b c)").rearrange("p (b f) -> p b f", f=FF)
            scaled = S(8)
            xq = S(9).bitcast(BF16)[:, :, 0:D]
            xqT = S(9).bitcast(BF16)[:, :, D:2 * D]
            ternary = S(10).bitcast(BF16).rearrange("p b c -> p (b c)")
            up_q, down_q, gate_q = (ternary[:, j * FF:(j + 1) * FF] for j in range(3))
            hq = probs[:].bitcast(BF16).rearrange("p h k -> p (h k)").rearrange("p (b f) -> p b f", f=FF)
            hqT = probsT[:].bitcast(BF16).rearrange("p h k -> p (h k)").rearrange("p (b f) -> p b f", f=FF)
            temp = k_heads[:].rearrange("p h k -> p (h k)")[:, 0:FF]
            up_in = shifted[:].rearrange("p h k -> p (h k)").rearrange("p (s f) -> p s f", f=FF)
            mats = [("up", up_q), ("down", down_q)] + ([("gate", gate_q)] if gated else [])
            wsum, wscale, wrec = small[:, 0, 0:3], small[:, 1, 0:3], small[:, 2, 0:3]
            amax, inv, tok, up_s, gate_s = (small[:, 3 + j] for j in range(5))
            amax2, inv2, tok2 = (small[:, 8 + j] for j in range(3))
            last_b = B - 1
            up_at = lambda b: 2 * (b % 4) if gated else b
            plan(pe=["wsum", "xqT", *[f"u{b}" for b in range(B)], *[f"hT{b}" for b in range(B)],
                     *[f"o{b}" for b in range(B)]],
                 act=["xqT", *[f"h{b}" for b in range(B)], *[f"i{b}" for b in range(B)],
                      *[f"hT{b}" for b in range(B)]],
                 vec=[*LN["vec"], "wabs", "wclip", "wrec", *[f"{m}{j}" for m, _ in mats for j in range(3)],
                      "amax", "aclip", "inv", "sx", "tok", "x1", "x2", "xq", "scales", "scales2",
                      *([f"s{b}" for b in range(B)] if not gated else [f"{c}{b}" for b in range(B) for c in "st"]),
                      "amax2", "aclip2", "inv2", "sx2", "tok2", "tok2w",
                      *[f"{c}{b}" for b in range(B) for c in ("m", "n")],
                      *[f"r{b}" for b in range(B)]],
                 pool=[*LN["pool"], *([] if gated else ["bias"])])
            with nc.Block() as block:
                @block.vector
                def _(vec):
                    ts, stt = vec.tensor_scalar, vec.scalar_tensor_tensor

                    def chain(ins, name):
                        ins.then_inc(vec_done, V.step(name))
                        vec.wait_ge(vec_done, V.after(name))

                    vec.wait_ge(loaded[pack], 16)
                    ln_vector(vec, residual, normed)
                    for j, (name, _) in enumerate(mats):
                        last = vec.tensor_reduce(wsum[:, j:j + 1], w(name), AXIS_X, ALU.add, apply_absolute_value=True)
                    last.then_inc(vec_done, V.step("wabs"))
                    vec.wait_ge(pe_done, P.after("wsum"))
                    n = len(mats)
                    chain(ts(wscale[:, 0:n], bank(2)[:, 0:n], 1.0 / (FF * D), 1e-5, ALU.mult, ALU.max), "wclip")
                    chain(vec.reciprocal(wrec[:, 0:n], wscale[:, 0:n]), "wrec")
                    for j, (name, target) in enumerate(mats):
                        chain(ts(temp, w(name), wrec[:, j:j + 1], ROUND, ALU.mult, ALU.add), f"{name}0")
                        chain(ts(temp, temp, ROUND, 1.0, ALU.subtract, ALU.min), f"{name}1")
                        chain(ts(target, temp, -1.0, None, ALU.max), f"{name}2")
                    chain(vec.tensor_reduce(amax, normed[:], AXIS_X, ALU.max, apply_absolute_value=True), "amax")
                    chain(ts(amax, amax, 1e-5, None, ALU.max), "aclip")
                    chain(vec.reciprocal(inv, amax), "inv")
                    chain(ts(inv, inv, 127.0, None, ALU.mult), "sx")
                    ts(tok, amax, 1.0 / 127.0, None, ALU.mult).then_inc(vec_done, V.step("tok"))
                    chain(vec.tensor_tensor(scaled, normed[:], inv.unsqueeze(2).broadcast_to([128, B, D]), ALU.mult), "x1")
                    chain(ts(scaled, scaled, 127.0, -128.0, ALU.min, ALU.max), "x2")
                    chain(ts(xq, scaled, ROUND, ROUND, ALU.add, ALU.subtract), "xq")
                    chain(ts(up_s, tok, wscale[:, 0:1], None, ALU.mult), "scales")
                    chain(ts(gate_s, tok, wscale[:, n - 1:n], None, ALU.mult), "scales2")
                    for b in range(B):
                        if gated:
                            vec.wait_ge(act_done, A.after(f"h{b}"))
                            vec.wait_ge(pe_done, P.after(f"u{b}"))
                            chain(stt(out=up_in[:, b % 2], in0=bank(up_at(b)), scalar=up_s[:, b:b + 1],
                                      in1=squares[:, b], op0=ALU.mult, op1=ALU.mult), f"s{b}")
                            vec.tensor_tensor(hidden[:, b], up_in[:, b % 2], squares[:, b], ALU.mult).then_inc(
                                vec_done, V.step(f"t{b}"))
                        else:
                            vec.wait_ge(pe_done, P.after(f"u{b}"))
                            stt(out=squares[:, b], in0=bank(up_at(b)), scalar=up_s[:, b:b + 1], in1=w("up_b"),
                                op0=ALU.mult, op1=ALU.add).then_inc(vec_done, V.step(f"s{b}"))
                    if gated:
                        vec.wait_ge(vec_done, V.after(f"t{last_b}"))
                    else:
                        vec.wait_ge(act_done, A.after(f"h{last_b}"))
                    chain(vec.tensor_reduce(amax2, hidden, AXIS_X, ALU.max, apply_absolute_value=True), "amax2")
                    chain(ts(amax2, amax2, 1e-5, None, ALU.max), "aclip2")
                    chain(vec.reciprocal(inv2, amax2), "inv2")
                    chain(ts(inv2, inv2, 127.0, None, ALU.mult), "sx2")
                    chain(ts(tok2, amax2, 1.0 / 127.0, None, ALU.mult), "tok2")
                    chain(ts(tok2, tok2, wscale[:, 1:2], None, ALU.mult), "tok2w")
                    for b in range(B):
                        chain(ts(hidden[:, b], hidden[:, b], inv2[:, b:b + 1], 127.0, ALU.mult, ALU.min), f"m{b}")
                        ts(hidden[:, b], hidden[:, b], -128.0, ROUND, ALU.max, ALU.add).then_inc(
                            vec_done, V.step(f"n{b}"))
                    if not gated:
                        vec.wait_ge(pool_done, G.after("bias"))
                    for b in range(B):
                        vec.wait_ge(pe_done, P.after(f"o{b // HB * HB + HB - 1}"))
                        stt(out=residual[:, b], in0=by_batch(6, 2)[:, b], scalar=tok2[:, b:b + 1], in1=residual[:, b],
                            op0=ALU.mult, op1=ALU.add).then_inc(vec_done, V.step(f"r{b}"))

                @block.gpsimd
                def _(pool):
                    ln_pool(pool)
                    if not gated:
                        pool.wait_ge(loaded[pack], 16)
                        add_bias(pool, w("down_b"))

                @block.tensor
                def _(pe):
                    pe.wait_ge(vec_done, V.after("wabs"))
                    pe.matmul(bank(2)[:, 0:len(mats)], ones[:, 0:128], wsum[:, 0:len(mats)], start=True,
                              stop=True).then_inc(pe_done, P.step("wsum"))
                    pe.wait_ge(vec_done, V.after("xq"))
                    turned = psum[:, 0, :].bitcast(BF16).rearrange("p (b c) -> p b c", c=T)
                    for b in range(B):
                        last = pe.transpose(turned[:, b], xq[:, b], ident16[:])
                    last.then_inc(pe_done, P.step("xqT"))
                    pe.wait_ge(act_done, A.after("xqT"))
                    for b in range(B):
                        if gated:
                            if b >= 4:
                                pe.wait_ge(vec_done, V.after(f"s{b - 4}"))
                            pe.matmul(bank(up_at(b) + 1), xqT[:, b], gate_q, start=True, stop=True)
                        pe.matmul(bank(up_at(b)), xqT[:, b], up_q, start=True, stop=True).then_inc(
                            pe_done, P.step(f"u{b}"))
                    for b in range(B):
                        pe.wait_ge(act_done, A.after(f"i{b}"))
                        if b == 0:
                            pe.wait_ge(vec_done, V.after(f"s{last_b}"))
                        if b >= 2:
                            pe.wait_ge(act_done, A.after(f"hT{b - 2}"))
                        turned = psum[:, b % 2, 0:256].bitcast(BF16).rearrange("p (c k) -> p c k", k=T)
                        for c in range(4):
                            last = pe.transpose(turned[:, c], hq[:, b, c * 128:(c + 1) * 128], ident16[:])
                        last.then_inc(pe_done, P.step(f"hT{b}"))
                    for b in range(B):
                        pe.wait_ge(act_done, A.after(f"hT{b}"))
                        for c in range(4):
                            last = pe.matmul(by_batch(6, 2)[:, b], hqT[:, b, c * 128:(c + 1) * 128],
                                             down_q[:, c * 128:(c + 1) * 128], start=c == 0, stop=c == 3)
                        last.then_inc(pe_done, P.step(f"o{b}"))

                @block.scalar
                def _(act):
                    act.wait_ge(pe_done, P.after("xqT"))
                    act.copy(xqT, psum[:, 0, :].bitcast(BF16).rearrange("p (b c) -> p b c", c=T)).then_inc(
                        act_done, A.step("xqT"))
                    for b in range(B):
                        if gated:
                            act.wait_ge(pe_done, P.after(f"u{b}"))
                            act.wait_ge(vec_done, V.after("scales2"))
                            last = act.activation(squares[:, b], bank(up_at(b) + 1), ACT.Relu,
                                                  scale=gate_s[:, b:b + 1])
                        else:
                            act.wait_ge(vec_done, V.after(f"s{b}"))
                            last = act.activation(hidden[:, b], squares[:, b], ACT.Gelu)
                        last.then_inc(act_done, A.step(f"h{b}"))
                    for b in range(B):
                        act.wait_ge(vec_done, V.after(f"n{b}"))
                        act.activation(hq[:, b], hidden[:, b], ACT.Identity, bias=minus_round[:]).then_inc(
                            act_done, A.step(f"i{b}"))
                    for b in range(B):
                        act.wait_ge(pe_done, P.after(f"hT{b}"))
                        act.copy(hqT[:, b], psum[:, b % 2, 0:256].bitcast(BF16)).then_inc(act_done, A.step(f"hT{b}"))

        stage(lambda: quantised_ffn("L1", False))

        def recurrence():
            chunk = 512 // B
            banks_used = T // chunk
            states = S(0).rearrange("p b t -> p (b t)").rearrange("p (t b) -> p t b", b=B)
            UNROLL = 8
            plan(pe=[*LN["pe"], "inputs", "hT"], act=[*LN["act"]], vec=[*LN["vec"], "r"], pool=[*LN["pool"]])
            with nc.Block() as block:
                @block.vector
                def _(vec):
                    ln_vector(vec, residual, normed)
                    vec.wait_ge(pe_done, P.after("hT"))
                    vec.tensor_tensor(residual[:], residual[:], by_batch(0, 2), ALU.add).then_inc(
                        vec_done, V.step("r"))

                @block.gpsimd
                def _(pool):
                    ln_pool(pool)

                @block.tensor
                def _(pe):
                    ln_tensor(pe)
                    pe.wait_ge(loaded["L2"], 16)
                    pe.wait_ge(act_done, A.after("xnT1"))
                    for k in range(banks_used):
                        pe.matmul(bank(2 + k), W("L2", "wi"),
                                  normedT.rearrange("p b t -> p t b")[:, k * chunk:(k + 1) * chunk],
                                  start=True, stop=False, skip_group_check=True)
                        pe.matmul(bank(2 + k), W("L2", "ih_b", 0, D, rows=slice(0, 1)), ones[0:1, :], start=False,
                                  stop=False, skip_group_check=True)
                        last = pe.matmul(bank(2 + k), W("L2", "ih_b", D, D, rows=slice(0, 1)), ones[0:1, :],
                                         start=False, stop=True, skip_group_check=True)
                    last.then_inc(pe_done, P.step("inputs"))

                    def step(t):
                        pe.wait_ge(state_made, t)
                        pe.matmul(banks(2, 2)[:, bass.ds(t * B, B)], W("L2", "wh"), states[:, bass.ds(t - 1, 1)],
                                  start=False, stop=True, skip_group_check=True).then_inc(sum_made, 1)

                    for t in range(1, UNROLL):
                        step(t)
                    with pe.Fori(1, T // UNROLL) as i:
                        for j in range(UNROLL):
                            step(i * UNROLL + j)
                    pe.wait_ge(state_made, T)
                    for b in range(B):
                        last = pe.transpose(by_batch(0, 2)[:, b], states[:, :, b], ident)
                    last.then_inc(pe_done, P.step("hT"))

                @block.scalar
                def _(act):
                    ln_scalar(act)
                    act.preload_act_table(ACT.Tanh)
                    act.wait_ge(pe_done, P.after("inputs"))

                    def step(t):
                        if not (isinstance(t, int) and t == 0):
                            act.wait_ge(sum_made, t)
                        act.activation(states[:, bass.ds(t, 1)], banks(2, 2)[:, bass.ds(t * B, B)],
                                       ACT.Tanh).then_inc(state_made, 1)

                    for t in range(UNROLL):
                        step(t)
                    with act.Fori(1, T // UNROLL) as i:
                        for j in range(UNROLL):
                            step(i * UNROLL + j)

        stage(recurrence)

        peaks, p_inv = small[:, 20], small[:, 21, 0:1]

        def power_mean_prologue():
            v, z = S(0), S(1)
            p_abs, p_sign, p_used, p_moved = (small[:, 16 + j, 0:1] for j in range(4))
            plan(pe=[*LN["pe"], "v", "vT"], act=[*LN["act"], "abs", "sign", "v", "ln", "exp"],
                 vec=[*LN["vec"], "moved", "pclip", "p", "pinv", "vclip", "z", "peak", "less", "values"], pool=LN["pool"])
            with nc.Block() as block:
                @block.vector
                def _(vec):
                    ln_vector(vec, residual, normed)
                    vec.wait_ge(loaded["L2"], 16)
                    vec.tensor_scalar(p_moved, W("L2", "p"), 0.0005, None, ALU.add).then_inc(
                        vec_done, V.step("moved"))
                    vec.wait_ge(act_done, A.after("sign"))
                    vec.tensor_scalar(p_abs, p_abs, 0.001, 100.0, ALU.max, ALU.min).then_inc(
                        vec_done, V.step("pclip"))
                    vec.wait_ge(vec_done, V.after("pclip"))
                    vec.tensor_tensor(p_used, p_abs, p_sign, ALU.mult).then_inc(vec_done, V.step("p"))
                    vec.wait_ge(vec_done, V.after("p"))
                    vec.reciprocal(p_inv, p_used).then_inc(vec_done, V.step("pinv"))
                    vec.wait_ge(act_done, A.after("v"))
                    vec.tensor_scalar(v, v, 1e-10, None, ALU.max).then_inc(vec_done, V.step("vclip"))
                    vec.wait_ge(act_done, A.after("ln"))
                    vec.tensor_scalar(z, z, p_used, None, ALU.mult).then_inc(vec_done, V.step("z"))
                    vec.wait_ge(vec_done, V.after("z"))
                    vec.tensor_reduce(peaks, z, AXIS_X, ALU.max).then_inc(vec_done, V.step("peak"))
                    vec.wait_ge(vec_done, V.after("peak"))
                    vec.tensor_tensor(z, z, peaks.unsqueeze(2).broadcast_to([128, B, T]), ALU.subtract).then_inc(
                        vec_done, V.step("less"))
                    vec.wait_ge(pe_done, P.after("vT"))
                    vec.tensor_copy(values[:, :, :, 0:HD].rearrange("p b h d -> p (b h) d"),
                                    banks(2, 2).rearrange("p (b d) -> p b d", d=HD)).then_inc(
                        vec_done, V.step("values"))

                @block.gpsimd
                def _(pool):
                    ln_pool(pool)

                @block.tensor
                def _(pe):
                    ln_tensor(pe)
                    pe.wait_ge(loaded["L2"], 16)
                    for h in range(2):
                        last = pe.matmul(bank(2 + h), W("L2", "xv"), half(contextT, h), start=True, stop=True)
                    last.then_inc(pe_done, P.step("v"))
                    pe.wait_ge(act_done, A.after("exp"))
                    for b in range(B):
                        last = pe.transpose(by_batch(2, 2)[:, b], v[:, b], ident)
                    last.then_inc(pe_done, P.step("vT"))

                @block.scalar
                def _(act):
                    ln_scalar(act)
                    act.wait_ge(loaded["L2"], 16)
                    act.activation(p_abs, W("L2", "p"), ACT.Abs).then_inc(act_done, A.step("abs"))
                    act.wait_ge(vec_done, V.after("moved"))
                    act.activation(p_sign, p_moved, ACT.Sign).then_inc(act_done, A.step("sign"))
                    act.wait_ge(pe_done, P.after("v"))
                    act.activation(v, by_batch(2, 2), ACT.Abs, bias=W("L2", "shift")).then_inc(
                        act_done, A.step("v"))
                    act.wait_ge(vec_done, V.after("vclip"))
                    act.activation(z, v, ACT.Ln).then_inc(act_done, A.step("ln"))
                    act.wait_ge(vec_done, V.after("less"))
                    act.activation(v, z, ACT.Exp).then_inc(act_done, A.step("exp"))

        stage(lambda: (
            power_mean_prologue(),
            attention_loop(D ** -0.5, q=W("L2", "xq"), k=W("L2", "xk"), k_source=contextT),
            attention_out(W("L2", "xo"), gem=(peaks, p_inv, W("L2", "shift")))))

        def experts_ffn():
            weight_of = S(0)[0:EXPERTS]
            units = scratch[:, 1:3]
            sig = [S(3 + j)[:, 0:HB] for j in range(3)]
            gated = [S(6 + j)[:, 0:HB] for j in range(3)]
            part = [S(9 + j)[:, 0:HB] for j in range(3)]
            order = [(e, h, c) for e in range(EXPERTS) for h in range(2) for c in range(2)]
            row = lambda j: S(12)[:, j, 0:B * EXPERTS].rearrange("p (b e) -> p b e", e=EXPERTS)
            score, best1, best2, rank, less = (row(j) for j in range(5))
            one1, one2, weight = (S(13)[:, j, 0:B * EXPERTS].rearrange("p (b e) -> p b e", e=EXPERTS)
                                  for j in range(3))
            top, total, top1, top2, peak, denom, rec = (small[:, j] for j in range(7))
            wide = lambda col: col.unsqueeze(2).broadcast_to([128, B, EXPERTS])
            priority = over_batches(W("C", "priority"), B)
            gates = ["top", "less", "sum", "rec", "score", "m1", "e1", "rank1", "pr1", "one1", "s2", "m2", "e2",
                     "rank2", "pr2", "one2", "den", "deneps", "denrec", "w1", "w2", "w", "wn", "share"]
            plan(pe=[*LN["pe"], "gate", "wT", *[f"{x}{u}" for u in range(len(order)) for x in (["c", "h"] if u % 2 == 0 else ["h"])],
                     "out0", "out1"],
                 act=[*LN["act"], "exp", "wT", *[f"s{u}" for u in range(len(order))]],
                 vec=[*LN["vec"], *gates, *[f"{x}{u}" for u in range(len(order)) for x in "gp"],
                      *[f"b{b}" for b in range(B)], "r0", "r1"],
                 pool=[*LN["pool"], *[f"a{u}" for u in range(4, len(order))]])
            with nc.Block() as block:
                @block.vector
                def _(vec):
                    tt, ts, stt = vec.tensor_tensor, vec.tensor_scalar, vec.scalar_tensor_tensor

                    def chain(ins, name):
                        ins.then_inc(vec_done, V.step(name))
                        vec.wait_ge(vec_done, V.after(name))

                    ln_vector(vec, residual, normed)
                    logits = bank(2, B * EXPERTS).rearrange("p (b e) -> p b e", e=EXPERTS)
                    vec.wait_ge(pe_done, P.after("gate"))
                    chain(vec.tensor_reduce(top, logits, AXIS_X, ALU.max), "top")
                    chain(tt(less, logits, wide(top), ALU.subtract), "less")
                    vec.wait_ge(act_done, A.after("exp"))
                    chain(vec.tensor_reduce(total, score, AXIS_X, ALU.add), "sum")
                    chain(vec.reciprocal(rec, total), "rec")
                    chain(tt(score, score, wide(rec), ALU.mult), "score")
                    chain(vec.tensor_reduce(top1, score, AXIS_X, ALU.max), "m1")
                    chain(tt(best1, score, wide(top1), ALU.is_equal), "e1")
                    chain(tt(rank, best1, priority, ALU.mult), "rank1")
                    chain(vec.tensor_reduce(peak, rank, AXIS_X, ALU.max), "pr1")
                    chain(tt(one1, rank, wide(peak), ALU.is_equal), "one1")
                    chain(stt(out=less, in0=one1, scalar=-2.0, in1=score, op0=ALU.mult, op1=ALU.add), "s2")
                    chain(vec.tensor_reduce(top2, less, AXIS_X, ALU.max), "m2")
                    chain(tt(best2, less, wide(top2), ALU.is_equal), "e2")
                    chain(tt(rank, best2, priority, ALU.mult), "rank2")
                    chain(vec.tensor_reduce(peak, rank, AXIS_X, ALU.max), "pr2")
                    chain(tt(one2, rank, wide(peak), ALU.is_equal), "one2")
                    chain(tt(denom, top1, top2, ALU.add), "den")
                    chain(ts(total, denom, 1e-9, None, ALU.add), "deneps")
                    chain(vec.reciprocal(rec, total), "denrec")
                    chain(tt(one1, one1, wide(top1), ALU.mult), "w1")
                    chain(tt(one2, one2, wide(top2), ALU.mult), "w2")
                    chain(tt(weight, one1, one2, ALU.add), "w")
                    chain(tt(weight, weight, wide(rec), ALU.mult), "wn")
                    tt(denom, denom, rec, ALU.mult).then_inc(vec_done, V.step("share"))
                    for u, (e, h, c) in enumerate(order):
                        pair = 2 * (u % 3)
                        vec.wait_ge(act_done, A.after(f"s{u}"))
                        if u >= 3:
                            vec.wait_ge(vec_done, V.after(f"p{u - 3}"))
                        bias = W("L2", "experts_b", 4 * e + c, 1)
                        stt(out=gated[u % 3], in0=by_batch(pair), scalar=bias, in1=sig[u % 3], op0=ALU.add,
                            op1=ALU.mult).then_inc(vec_done, V.step(f"g{u}"))
                        vec.wait_ge(vec_done, V.after(f"g{u}"))
                        if u - 3 >= 4:
                            vec.wait_ge(pool_done, G.after(f"a{u - 3}"))
                        target = half(units[:, c], h) if e == 0 else part[u % 3]
                        tt(target, gated[u % 3], by_batch(6 + u // 2 % 2), ALU.mult).then_inc(
                            vec_done, V.step(f"p{u}"))
                    for b in range(B):
                        stt(out=residual[:, b], in0=W("L2", "bo"), scalar=denom[:, b:b + 1], in1=residual[:, b],
                            op0=ALU.mult, op1=ALU.add).then_inc(vec_done, V.step(f"b{b}"))
                    vec.wait_ge(vec_done, V.after(f"b{B - 1}"))
                    for h in range(2):
                        vec.wait_ge(pe_done, P.after(f"out{h}"))
                        tt(half(residual, h), half(residual, h), by_batch(h), ALU.add).then_inc(
                            vec_done, V.step(f"r{h}"))

                @block.gpsimd
                def _(pool):
                    ln_pool(pool)
                    for u, (e, h, c) in enumerate(order):
                        if e == 0:
                            continue
                        total_at = half(units[:, c], h)
                        pool.wait_ge(vec_done, V.after(f"p{u}"))
                        if u >= 8:
                            pool.wait_ge(pool_done, G.after(f"a{u - 4}"))
                        pool.tensor_tensor(total_at, total_at, part[u % 3], ALU.add).then_inc(
                            pool_done, G.step(f"a{u}"))

                @block.tensor
                def _(pe):
                    ln_tensor(pe)
                    pe.wait_ge(act_done, A.after("xnT1"))
                    pe.wait_ge(loaded["L2"], 16)
                    for b in range(B):
                        last = pe.matmul(bank(2)[:, b * EXPERTS:(b + 1) * EXPERTS], normedT[:, b], W("L2", "wg"),
                                         start=True, stop=True)
                    last.then_inc(pe_done, P.step("gate"))
                    pe.wait_ge(vec_done, V.after("wn"))
                    for b in range(B):
                        last = pe.transpose(by_batch(4, 2)[0:EXPERTS, b], weight[:, b], ident)
                    last.then_inc(pe_done, P.step("wT"))
                    pe.wait_ge(act_done, A.after("wT"))
                    for u, (e, h, c) in enumerate(order):
                        if c == 0:
                            if u >= 4:
                                pe.wait_ge(vec_done, V.after(f"p{u - 3}"))
                            pe.matmul(bank(6 + u // 2 % 2), W("C", "pick", e * 128, 128, rows=slice(0, EXPERTS)),
                                      half(weight_of, h), start=True, stop=True).then_inc(pe_done, P.step(f"c{u}"))
                        if u >= 3:
                            pe.wait_ge(vec_done, V.after(f"g{u - 3}"))
                        for j in range(2):
                            at = e * 2 * EH + j * EH + c * 128
                            last = pe.matmul(bank(2 * (u % 3) + j), W("L2", "experts", at, 128), half(normedT, h),
                                             start=True, stop=True)
                        last.then_inc(pe_done, P.step(f"h{u}"))
                    for h in range(2):
                        if h == 0:
                            pe.wait_ge(vec_done, V.after(f"g{len(order) - 1}"))
                            pe.wait_ge(pool_done, G.after(f"a{len(order) - 1}"))
                        for b in range(HB * h, HB * h + HB):
                            for c in range(2):
                                last = pe.matmul(by_batch(0, 2)[:, b], units[:, c, b], W("L2", "wo", c * D, D),
                                                 start=c == 0, stop=c == 1)
                        last.then_inc(pe_done, P.step(f"out{h}"))

                @block.scalar
                def _(act):
                    ln_scalar(act)
                    act.wait_ge(vec_done, V.after("less"))
                    act.activation(score, less, ACT.Exp).then_inc(act_done, A.step("exp"))
                    act.wait_ge(pe_done, P.after("wT"))
                    act.copy(weight_of, by_batch(4, 2)[0:EXPERTS]).then_inc(act_done, A.step("wT"))
                    for u, (e, h, c) in enumerate(order):
                        act.wait_ge(pe_done, P.after(f"h{u}"))
                        if u >= 3:
                            act.wait_ge(vec_done, V.after(f"g{u - 3}"))
                        act.activation(sig[u % 3], by_batch(2 * (u % 3) + 1), ACT.Sigmoid,
                                       bias=W("L2", "experts_b", 4 * e + 2 + c, 1)).then_inc(
                            act_done, A.step(f"s{u}"))

        stage(experts_ffn)

        stage(lambda: (
            attention_prologue("L3", W("L3", "sv"), None, None, normedT),
            attention_loop(HD ** -0.5, table=W("L3", "sparse"), q=W("L3", "sq"), k=W("L3", "sk"), k_source=normedT),
            attention_out(W("L3", "so"))))
        stage(lambda: cross("L3"))
        stage(lambda: quantised_ffn("L3", True))

        for f in stages[FIRST:STAGES]:
            f()

        with nc.Block() as block:
            @block.sync
            def _(sync):
                sync.dma_start(out_dram.rearrange("b t d -> t b d"), residual[:]).then_inc(stored, 16)
                sync.wait_ge(stored, 16)


STAGES = 12
FIRST = 0


def _columns(v, rows=128):
    return np.asarray(v).reshape(rows, 1)


def _rows(v):
    v = np.asarray(v).reshape(1, -1)
    return np.broadcast_to(v, (128, v.shape[1]))


def _stack(a):
    return a.reshape(-1, 128, a.shape[1]).transpose(1, 0, 2).reshape(128, -1)


def _latent_blocks(w):
    out = np.zeros((H, HD, GROUPS, 4, LAT), w.dtype)
    for h in range(H):
        out[h, :, h // 4, h % 4] = w.T
    return out.reshape(D, -1)


def _swap(w):
    return w.reshape(LAT // 2, 2, -1)[:, ::-1].reshape(w.shape)


def _pad(a, rows=128):
    return np.concatenate([a, np.zeros((rows - a.shape[0], a.shape[1]), a.dtype)])


def lay_out(i):
    f = np.float32
    pos = np.arange(T)
    freq = 1.0 / 10000.0 ** (np.arange(0, LAT, 2, dtype=f) / f(LAT))
    angle = np.outer(pos.astype(f), freq.astype(f)).astype(f)
    cos = np.tile(np.repeat(np.cos(angle), 2, axis=1).T, (4, 1)).astype(f)
    sign = np.tile(np.array([-1.0, 1.0], f), LAT // 2)[:, None]
    sin = np.tile(np.repeat(np.sin(angle), 2, axis=1).T * sign, (4, 1)).astype(f)
    l2o = np.zeros((4, LAT, GROUPS, H, HD), f)
    for h in range(H):
        l2o[h % 4, :, h // 4, h] = i["L0_attn_l2o_w"].T
    wqk = np.zeros((4, LAT, 4, LAT), f)
    for j in range(4):
        wqk[j, :, j] = i["L0_attn_wqk_w"].T
    per = INNER // 2

    def hinges(a):
        return a.reshape(M, 2, per).transpose(1, 0, 2).reshape(2 * M, per)

    rows, cols = pos[:, None], pos[None, :]
    causal = cols <= rows
    sparse = (causal & (cols >= rows - 31)) | (causal & ((rows - cols) % 64 == 0))
    start = 2.0 ** (-2.0 ** (-(4 - 3)))
    slopes = np.asarray([start * start ** n for n in range(H)], f)
    distance = -np.abs(rows - cols).astype(f)
    alibi = (slopes[None, :, None] * distance[:, None, :]).astype(f)

    def cross(p, q, k, v, o, turn):
        w = {n: (i[f"{p}_{m}"].T if turn else i[f"{p}_{m}"]) for n, m in (("xq", q), ("xk", k), ("xv", v), ("xo", o))}
        return w

    L0 = {
        "qkv": i["L0_attn_c_attn_w"].T, "q_lat": _latent_blocks(i["L0_attn_q2l_w"]),
        "q_swap": _latent_blocks(_swap(i["L0_attn_q2l_w"])), "kv_lat": _latent_blocks(i["L0_attn_kv2l_w"]),
        "k_swap": _latent_blocks(_swap(i["L0_attn_kv2l_w"])), "l2o": l2o.reshape(128, -1), "wqk": wqk.reshape(128, 128),
        "cproj": i["L0_attn_cproj_w"].T, "qkv_b": i["L0_attn_c_attn_b"].reshape(3, D).T,
        "q_lat_b": _columns(np.tile(i["L0_attn_q2l_b"], 4)), "q_swap_b": _columns(np.tile(_swap(i["L0_attn_q2l_b"]), 4)),
        "kv_lat_b": _columns(np.tile(i["L0_attn_kv2l_b"], 4)),
        "k_swap_b": _columns(np.tile(_swap(i["L0_attn_kv2l_b"]), 4)),
        "wqk_b": _columns(np.tile(i["L0_attn_wqk_b"], 4)), "l2o_b": _columns(np.tile(i["L0_attn_l2o_b"], H)),
        "cproj_b": _rows(i["L0_attn_cproj_b"]), "cos": cos, "sin": sin,
        "causal": np.where(causal, 0.0, MASKED).astype(f),
        **cross("L0_xattn", "wq_w", "wk_w", "wv_w", "wo_w", True),
        "xq_b": _columns(i["L0_xattn_wq_b"]), "xk_b": _columns(i["L0_xattn_wk_b"]), "xv_b": _rows(i["L0_xattn_wv_b"]),
        "xo_b": _rows(i["L0_xattn_wo_b"]),
        "win": np.tile(i["L0_ffn_Win"], (1, 2)), "wout": np.tile(i["L0_ffn_Wout"], (2, 1)),
        "bin": _columns(np.tile(i["L0_ffn_bin_"], 2)), "w1": hinges(i["L0_ffn_W1"]), "b1": hinges(i["L0_ffn_b1"]),
        "w2": hinges(i["L0_ffn_W2"]), "b2": _pad(_columns(i["L0_ffn_b2"], M)), "bout": _rows(i["L0_ffn_bout"]),
    }
    L1 = {
        "phases": i["L1_attn_pos_phases"][:T].T, "wpv": i["L1_attn_Wpv"], "wk": i["L1_attn_Wk"],
        "wkv": i["L1_attn_Wkv"], "wg1": i["L1_attn_Wg1"][:D], "wg1_shift": i["L1_attn_Wg1"][D:],
        "wg2": np.tile(i["L1_attn_Wg2"], (1, D)), "wb1": i["L1_attn_Wb1"],
        "wb2_0": _pad(np.tile(i["L1_attn_Wb2"][:, 0:1], (1, D))), "wb2_1": _pad(np.tile(i["L1_attn_Wb2"][:, 1:2], (1, D))),
        "wo": i["L1_attn_Wo"], "bpv": _columns(i["L1_attn_bpv"]), "bk": _columns(i["L1_attn_bk"]),
        "bkv": _columns(i["L1_attn_bkv"]), "bg1": _columns(i["L1_attn_bg1"]), "bg2": _rows(i["L1_attn_bg2"]),
        "bb1": _pad(_columns(i["L1_attn_bb1"], 64)), "bb2_0": _rows(i["L1_attn_bb2"][0:1]),
        "bb2_1": _rows(i["L1_attn_bb2"][1:2]), "ln_g": _columns(i["L1_attn_ln_g"]), "ln_b": _columns(i["L1_attn_ln_b"]),
        "bo": _rows(i["L1_attn_bo"]), **cross("L1_xattn", "wq", "wk", "wv", "wo", True),
        "xq_b": _columns(i["L1_xattn_bq"]), "xk_b": _columns(i["L1_xattn_bk"]), "xv_b": _rows(i["L1_xattn_bv"]),
        "xo_b": _rows(i["L1_xattn_bo"]), "up": i["L1_ffn_W1"].T, "down": _stack(i["L1_ffn_W2"].T),
        "up_b": _rows(i["L1_ffn_b1"]), "down_b": _rows(i["L1_ffn_b2"]),
    }
    L2 = {
        "wi": i["L2_attn_Wi"].T, "wh": i["L2_attn_Wh"].T,
        "ih_b": np.concatenate([_rows(i["L2_attn_bi"]), _rows(i["L2_attn_bh"])], axis=1),
        "xq": i["L2_xattn_WQ"].T, "xk": i["L2_xattn_WK"].T, "xv": i["L2_xattn_WV"].T, "xo": i["L2_xattn_Wout"].T,
        "p": _columns(i["L2_xattn_p_param"]), "shift": _columns(i["L2_xattn_shift"]), "wg": i["L2_ffn_Wg"].T,
        "experts": i["L2_ffn_W1"].transpose(2, 0, 1).reshape(D, -1),
        "experts_b": i["L2_ffn_b1"].reshape(EXPERTS, 4, 128).transpose(2, 0, 1).reshape(128, -1),
        "wo": _stack(i["L2_ffn_Wo"].T), "bo": _rows(i["L2_ffn_bo"]),
    }
    L3 = {
        "sq": i["L3_attn_Wq"].T, "sk": i["L3_attn_Wk"].T, "sv": i["L3_attn_Wv"].T, "so": i["L3_attn_Wo"].T,
        "sparse": np.where(sparse, 0.0, MASKED).astype(f), **cross("L3_xattn", "Wq", "Wk", "Wv", "Wo", False),
        "xq_b": _columns(i["L3_xattn_bq"]), "xk_b": _columns(i["L3_xattn_bk"]), "xv_b": _rows(i["L3_xattn_bv"]),
        "xo_b": _rows(i["L3_xattn_bo"]), "alibi": alibi.reshape(T, -1),
        "gate": i["L3_ffn_w_gate"].T, "up": i["L3_ffn_w_up"].T, "down": _stack(i["L3_ffn_w_down"].T),
    }
    heads = np.arange(D)[:, None] // HD
    pick = np.zeros((128, EXPERTS, 128), f)
    pick[np.arange(EXPERTS), np.arange(EXPERTS)] = 1.0
    C = {
        "identity": np.eye(128, dtype=f), "head_mask": (heads == np.arange(H)).astype(f),
        "latent_mask": (np.arange(128)[:, None] // LAT == np.arange(GROUPS)).astype(f),
        "pick": pick.reshape(128, -1), "priority": _rows(np.arange(EXPERTS, 0, -1).astype(f)),
    }
    packs = {}
    for name, parts in (("L0", L0), ("L1", L1), ("L2", L2), ("L3", L3), ("C", C)):
        assert all(parts[n].shape == (128, w) for n, w in COLUMNS[name]), [
            (n, parts[n].shape, w) for n, w in COLUMNS[name] if parts[n].shape != (128, w)]
        packs[name] = np.ascontiguousarray(np.concatenate([parts[n] for n, _ in COLUMNS[name]], axis=1))
    return packs


def kernel(**inputs):
    import concourse.bacc as bacc
    from concourse.bass_utils import run_bass_kernel_spmd

    inputs = {k: np.asarray(v) for k, v in inputs.items()}
    nc = bacc.Bacc("TRN2", target_bir_lowering=False, num_devices=1)
    packs = lay_out(inputs)
    arrays = {f"in_{p}": a for p, a in packs.items()}
    arrays["in_x"] = np.ascontiguousarray(inputs["x"])
    arrays["in_ctx"] = np.ascontiguousarray(inputs["ctx_1024"])
    drams = {n: nc.dram_tensor(n, a.shape, F32, kind="ExternalInput").ap() for n, a in arrays.items()}
    out = nc.dram_tensor("out_x", (B, T, D), F32, kind="ExternalOutput").ap()
    build(nc, {p: drams[f"in_{p}"] for p in packs}, drams["in_x"], drams["in_ctx"], out)
    result = run_bass_kernel_spmd(nc, [arrays], core_ids=[0])
    return result.results[0]["out_x"]
```

```python
from contextlib import ExitStack

import numpy as np

import concourse.bass as bass
from concourse import mybir

ALU = mybir.AluOpType
ACT = mybir.ActivationFunctionType
AXIS_X = mybir.AxisListType.X
F32 = mybir.dt.float32
BF16 = mybir.dt.bfloat16

B, T, D = 8, 128, 128
H, HD = 16, 8
HH = H // 2
LAT, GROUPS = 32, 4
HB = B // 2
FF = 512
M, INNER = 64, 16
EXPERTS, EH = 8, 256
LN_EPS = 1e-5
MASKED = -1e30
QUERY_PARTS = (0, 0, 1, 0, 2, 1)
KEY_PARTS = (0, 1, 0, 2, 0, 1)
TERMS, PARTS = 6, 3
ROUND = 12582912.0
PI = float(np.float32(np.pi))
PI_BELOW = float(np.nextafter(np.float32(np.pi), np.float32(0)))
LOG_LIFT = 60

COLUMNS = {
    "L0": [("qkv", 3 * D), ("q_lat", 4 * 128), ("q_swap", 4 * 128), ("kv_lat", 4 * 128), ("k_swap", 4 * 128),
           ("l2o", 4 * 128), ("wqk", 128), ("cproj", D), ("qkv_b", 3), ("q_lat_b", 1), ("q_swap_b", 1),
           ("kv_lat_b", 1), ("k_swap_b", 1), ("wqk_b", 1), ("l2o_b", 1), ("cproj_b", D),
           ("cos", T), ("sin", T), ("causal", T),
           ("xq", D), ("xk", D), ("xv", D), ("xo", D), ("xq_b", 1), ("xk_b", 1), ("xv_b", D), ("xo_b", D),
           ("win", 128), ("wout", D), ("bin", 1), ("w1", 8), ("b1", 8), ("w2", 8), ("b2", 1), ("bout", D),
           ("mean_v", D), ("p", 1), ("shift", 1)],
    "L1": [("phases", T), ("wpv", D), ("wk", D), ("wkv", D), ("wg1", D), ("wg1_shift", D), ("wg2", D),
           ("wb1", 64), ("wb2_0", D), ("wb2_1", D), ("wo", D), ("bpv", 1), ("bk", 1), ("bkv", 1), ("bg1", 1),
           ("bg2", 1), ("bb1", 1), ("bb2_0", 1), ("bb2_1", 1), ("ln_g", 1), ("ln_b", 1), ("bo", D),
           ("xq", D), ("xk", D), ("xv", D), ("xo", D), ("xq_b", 1), ("xk_b", 1), ("xv_b", D), ("xo_b", D),
           ("up", FF), ("down", FF), ("up_b", FF), ("down_b", D)],
    "L2": [("wi", D), ("wh", D), ("ih_b", D), ("xq", D), ("xk", D), ("xo", D),
           ("wg", EXPERTS), ("experts", EXPERTS * 2 * EH), ("experts_b", EXPERTS * 4), ("wo", 2 * D), ("bo", D)],
    "L3": [("sq", D), ("sk", D), ("sv", D), ("so", D), ("sparse", T),
           ("xq", D), ("xk", D), ("xv", D), ("xo", D), ("xq_b", 1), ("xk_b", 1), ("xv_b", D), ("xo_b", D),
           ("alibi", H * T), ("gate", FF), ("up", FF), ("down", FF)],
    "C": [("identity", 128), ("head_mask", H), ("latent_mask", GROUPS), ("minus_pick", H), ("pick", EXPERTS * 128), ("priority", EXPERTS)],
}
WIDTH = {pack: sum(w for _, w in parts) for pack, parts in COLUMNS.items()}


class Steps:

    def __init__(self):
        self.base, self.names, self.n = 0, [], 0

    def plan(self, *names):
        assert self.n == len(self.names), self.names[self.n:]
        self.base += self.n
        self.names, self.n = [x for name in names for x in ([name] if isinstance(name, str) else name)], 0

    def step(self, name):
        assert self.names[self.n] == name, (self.names[self.n], name)
        self.n += 1
        return 1

    def after(self, name):
        return self.base + self.names.index(name) + 1


def batches(engine, first, last):
    yield first
    with engine.Fori(first + 1, last) as b:
        yield b


def build(nc, packs, x_dram, ctx_dram, out_dram):
    with ExitStack() as ctx:
        def sb(name, shape, dt=F32):
            return ctx.enter_context(nc.sbuf_tensor(name, shape, dt))

        def sem(name):
            return ctx.enter_context(nc.semaphore(name))

        weights = {p: sb(f"weights_{p}", [128, WIDTH[p]]) for p in COLUMNS}
        where = {}
        for p, parts in COLUMNS.items():
            at = 0
            for name, w in parts:
                where[p, name] = (at, w)
                at += w

        def W(pack, name, start=0, width=None, rows=slice(0, 128)):
            at, w = where[pack, name]
            return weights[pack][rows, at + start:at + start + (w - start if width is None else width)]

        def over_batches(table, n):
            return table.unsqueeze(1).broadcast_to([128, n, table.shape[1]])

        residual = sb("residual", [128, B, D])
        normed = sb("normed", [128, B, D])
        normedT_padded = sb("normedT_padded", [128, B, T + 1])
        normedT = normedT_padded[:, :, 1:T + 1]
        contextT = sb("contextT", [128, B, T])
        stats = sb("stats", [128, B, 6])
        moments = sb("moments", [128, B, 2])
        rstd = sb("rstd", [128, B])
        minus_half = sb("minus_half", [128, B])
        ones = sb("ones", [128, 128])
        values = sb("values", [128, B, H, HD + 1])
        mean_values = sb("mean_values", [128, B, H, HD + 1])
        position_waves = sb("position_waves", [128, 2, T])
        ternary = {"L1": sb("ternary_L1", [128, 2, FF], BF16), "L3": sb("ternary_L3", [128, 3, FF], BF16)}
        weight_scales = sb("weight_scales", [128, 8])
        weight_inverses = sb("weight_inverses", [128, 8])
        minus_pick_space = sb("minus_pick", [128, H, T], BF16)
        qT = minus_pick_space[:].rearrange("p h t -> p (h t)").bitcast(F32)[:, 0:GROUPS * T].rearrange(
            "p (g t) -> p g t", g=GROUPS)
        probsT = sb("probsT", [128, H, T])
        row_max = sb("row_max", [128, H])
        row_rec = sb("row_rec", [128, H])
        small_sums = sb("small_sums", [128, 2, T])
        row_rest = sb("row_rest", [128, H])
        peak_parts = sb("peak_parts", [128, PARTS * H], BF16)
        peakT = sb("peakT", [128, T], BF16)
        mask16 = sb("mask16", [128, T], BF16)
        small = sb("small", [128, 24, 8])
        half_pi = sb("half_pi", [128, 1])
        minus_round = sb("minus_round", [128, 1])
        ident16 = sb("ident16", [128, 128], BF16)
        scratch = sb("scratch", [128, 20, B, T])
        k_heads, shifted, probs = (scratch[:, 14 + 2 * j:16 + 2 * j].rearrange("p a b t -> p (a b) t") for j in range(3))
        psum = ctx.enter_context(nc.psum_tensor("psum", [128, 8, 512], F32))

        ident = W("C", "identity")

        pe_done, act_done, vec_done, pool_done = (sem(x) for x in ("pe_done", "act_done", "vec_done", "pool_done"))
        P, A, V, G = Steps(), Steps(), Steps(), Steps()
        (qk_made, q_ready, k_ready, scores_made, half_shifted, half_exp, half_turned, half_copied, half_weighed,
         ctx_made, max_made, rec_made, biased_made) = (sem(x) for x in (
             "qk_made", "q_ready", "k_ready", "scores_made", "half_shifted", "half_exp", "half_turned", "half_copied",
             "half_weighed", "ctx_made", "max_made", "rec_made", "biased_made"))
        (quarter_made, quarter_max, part_made, peaks_split, peaks_turned, peaks_ready, turned_made,
         turned_biased, half_probs, half_summed, sums_inverted, results_made, half_padded, sums_taken,
         sums_turned, pads_cleared) = (sem(x) for x in (
             "quarter_made", "quarter_max", "part_made", "peaks_split", "peaks_turned", "peaks_ready",
             "turned_made", "turned_biased", "half_probs", "half_summed", "sums_inverted", "results_made",
             "half_padded", "sums_taken", "sums_turned", "pads_cleared"))
        queries_stacked, keys_stacked = sem("queries_stacked"), sem("keys_stacked")
        state_made, sum_made = sem("state_made"), sem("sum_made")
        loaded = {name: sem(f"loaded_{name}") for name in ("C", "x", "ctx", "L0", "L1", "L2", "L3")}
        stored = sem("stored")

        def plan(pe=(), act=(), vec=(), pool=()):
            P.plan(*pe), A.plan(*act), V.plan(*vec), G.plan(*pool)

        def bank(n, width=512, rows=128):
            return psum[0:rows, n, 0:width]

        def banks(n, m):
            return psum[:, n:n + m, :].rearrange("p k c -> p (k c)")

        def by_batch(n, m=1):
            return psum[:, n:n + m, :].rearrange("p k (b c) -> p (k b) c", c=128)

        def S(i):
            return scratch[:, i]

        def flat(ap):
            return ap.rearrange("p b c -> p (b c)")

        def flat_all(ap):
            return ap.rearrange("p a b c -> p (a b c)")

        plan(pe=["ctxT0", "ctxT1"], act=["ctx0", "ctx1"], vec=["const"])
        with nc.Block() as block:
            @block.sync
            def _(sync):
                sync.dma_start(weights["C"][:], packs["C"]).then_inc(loaded["C"], 16)
                sync.dma_start(residual[:], x_dram.rearrange("b t d -> t b d")).then_inc(loaded["x"], 16)
                sync.dma_start(S(0), ctx_dram.rearrange("b t d -> t b d")).then_inc(loaded["ctx"], 16)
                for p in ("L0", "L1", "L2", "L3"):
                    sync.dma_start(weights[p][:], packs[p]).then_inc(loaded[p], 16)

            @block.gpsimd
            def _(pool):
                if FIRST:
                    for x in loaded.values():
                        pool.wait_ge(x, 16)

            @block.vector
            def _(vec):
                vec.memset(ones[:], 1.0)
                vec.memset(values[:], 1.0)
                vec.memset(mean_values[:], 1.0)
                vec.memset(minus_half[:], -0.5)
                vec.memset(half_pi[:], float(np.pi / 2))
                vec.memset(minus_round[:], -ROUND)
                vec.wait_ge(loaded["C"], 16)
                vec.tensor_copy(ident16[:], ident)
                vec.memset(normedT_padded[:, :, 0:1], 0.0).then_inc(vec_done, V.step("const"))

            @block.tensor
            def _(pe):
                pe.wait_ge(loaded["C"], 16)
                pe.wait_ge(loaded["ctx"], 16)
                for h in range(2):
                    for i in range(HB):
                        last = pe.transpose(by_batch(h)[:, i], S(0)[:, HB * h + i], ident)
                    last.then_inc(pe_done, P.step(f"ctxT{h}"))

            @block.scalar
            def _(act):
                for h in range(2):
                    act.wait_ge(pe_done, P.after(f"ctxT{h}"))
                    act.copy(contextT[:, HB * h:HB * h + HB], by_batch(h)).then_inc(act_done, A.step(f"ctx{h}"))

        LN = dict(pe=["xT0", "xT1"], act=["xnT0", "xnT1"], vec=["stats", "aggr", "xn0", "xn1"], pool=["eps", "rstd"])

        def ln_vector(vec, source, target, between=None):
            vec.wait_ge(loaded["x"], 16)
            for b in range(B):
                last = vec.bn_stats(stats[:, b], source[:, b])
            last.then_inc(vec_done, V.step("stats"))
            vec.wait_ge(vec_done, V.after("stats"))
            for b in range(B):
                last = vec.bn_aggr(moments[:, b], stats[:, b])
            last.then_inc(vec_done, V.step("aggr"))
            if between is not None:
                between()
            vec.wait_ge(pool_done, G.after("rstd"))
            for h in range(2):
                for b in range(HB * h, HB * h + HB):
                    last = vec.tensor_scalar(target[:, b], source[:, b], moments[:, b, 0:1], rstd[:, b:b + 1],
                                             ALU.subtract, ALU.mult)
                last.then_inc(vec_done, V.step(f"xn{h}"))

        def ln_pool(pool):
            pool.wait_ge(vec_done, V.after("aggr"))
            pool.tensor_scalar(rstd[:], moments[:, :, 1], LN_EPS, None, ALU.add).then_inc(pool_done, G.step("eps"))
            pool.wait_ge(pool_done, G.after("eps"))
            pool.tensor_tensor(rstd[:], rstd[:], minus_half[:], ALU.pow).then_inc(pool_done, G.step("rstd"))

        def ln_tensor(pe):
            for h in range(2):
                pe.wait_ge(vec_done, V.after(f"xn{h}"))
                for i in range(HB):
                    last = pe.transpose(by_batch(h)[:, i], normed[:, HB * h + i], ident)
                last.then_inc(pe_done, P.step(f"xT{h}"))

        def ln_scalar(act):
            for h in range(2):
                act.wait_ge(pe_done, P.after(f"xT{h}"))
                act.copy(normedT[:, HB * h:HB * h + HB], by_batch(h)).then_inc(act_done, A.step(f"xnT{h}"))

        def add_bias(pool, bias):
            pool.wait_ge(vec_done, V.after("xn1"))
            pool.tensor_tensor(residual[:], residual[:], over_batches(bias, B), ALU.add).then_inc(
                pool_done, G.step("bias"))

        def half(ap, h):
            return ap[:, HB * h:HB * h + HB]

        ternary_weights = [("L1", "up"), ("L1", "down"), ("L3", "up"), ("L3", "down"), ("L3", "gate")]

        def ternary_steps(pack):
            return [f"w{m}{j}" for m, (p, _) in enumerate(ternary_weights) if p == pack for j in range(3)]

        def make_ternary(vec, pack, temp):
            for m, (p, name) in enumerate(ternary_weights):
                if p != pack:
                    continue
                target = ternary[pack][:, ("up", "down", "gate").index(name)]
                vec.tensor_scalar(temp, W(pack, name), weight_inverses[:, m:m + 1], ROUND, ALU.mult, ALU.add).then_inc(
                    vec_done, V.step(f"w{m}0"))
                vec.wait_ge(vec_done, V.after(f"w{m}0"))
                vec.tensor_scalar(temp, temp, ROUND, 1.0, ALU.subtract, ALU.min).then_inc(vec_done, V.step(f"w{m}1"))
                vec.wait_ge(vec_done, V.after(f"w{m}1"))
                vec.tensor_scalar(target, temp, -1.0, None, ALU.max).then_inc(vec_done, V.step(f"w{m}2"))
                vec.wait_ge(vec_done, V.after(f"w{m}2"))

        def heads_first(h):
            return by_batch(2 * h, 2)

        def latent_attention(scale, causal, q_rot, k_rot):
            ctx_all = normed

            with nc.Block() as block:
                @block.tensor
                def _(pe):
                    def project(b):
                        if not (isinstance(b, int) and b == 0):
                            pe.wait_ge(q_ready, b)
                        for g in range(GROUPS):
                            last = pe.matmul(bank(6)[:, g * T:(g + 1) * T], W("L0", "wqk"),
                                             q_rot[:, g, bass.ds(b, 1)], start=True, stop=True)
                        last.then_inc(qk_made, 1)

                    def scores(b, h):
                        pe.wait_ge(k_ready, 2 * b + h + 1)
                        if h == 0:
                            pe.wait_ge(q_ready, b + 1)
                        if not (isinstance(b, int) and b == 0):
                            pe.wait_ge(half_shifted, 2 * b + h - 1)
                        for g in range(2):
                            quad = 2 * h + g
                            last = pe.matmul(bank(quad), qT[:, quad],
                                             k_heads[:, 4 * quad:4 * quad + 4], start=True, stop=True)
                        last.then_inc(scores_made, 1)

                    def turn_and_weigh(turned=None, weighed=None):
                        if turned is not None:
                            b, h = turned
                            pe.wait_ge(half_exp, 2 * b + h + 1)
                            if not (isinstance(b, int) and b == 0 and h == 0):
                                pe.wait_ge(half_copied, 2 * b + h)
                        if weighed is not None:
                            b, h = weighed
                            if h == 0 and not (isinstance(b, int) and b == 0):
                                pe.wait_ge(ctx_made, b)
                            pe.wait_ge(half_copied, 2 * b + h + 1)
                        for i in range(HH):
                            if turned is not None:
                                last = pe.transpose(by_batch(4, 2)[:, i], probs[:, HH * turned[1] + i], ident)
                                if i == HH - 1:
                                    last.then_inc(half_turned, 1)
                            if weighed is not None:
                                head = HH * weighed[1] + i
                                last = pe.matmul(bank(7)[:, head * (HD + 1):(head + 1) * (HD + 1)], probsT[:, head],
                                                 values[:, bass.ds(weighed[0], 1), head], start=True, stop=True)
                                if i == HH - 1:
                                    last.then_inc(half_weighed, 1)

                    project(0)
                    scores(0, 0)
                    scores(0, 1)
                    project(1)
                    scores(1, 0)
                    turn_and_weigh((0, 0))
                    scores(1, 1)
                    project(2)
                    turn_and_weigh((0, 1), (0, 0))
                    for b in batches(pe, 2, B - 1):
                        scores(b, 0)
                        turn_and_weigh((b - 1, 0), (b - 2, 1))
                        scores(b, 1)
                        project(b + 1)
                        turn_and_weigh((b - 1, 1), (b - 1, 0))
                    scores(B - 1, 0)
                    turn_and_weigh((B - 2, 0), (B - 3, 1))
                    scores(B - 1, 1)
                    turn_and_weigh((B - 2, 1), (B - 2, 0))
                    turn_and_weigh((B - 1, 0), (B - 2, 1))
                    turn_and_weigh((B - 1, 1), (B - 1, 0))
                    turn_and_weigh(None, (B - 1, 1))

                @block.scalar
                def _(act):
                    act.preload_act_table(ACT.Exp)

                    def take(b):
                        act.wait_ge(qk_made, b + 1)
                        act.activation(flat(qT), bank(6), ACT.Identity, bias=W("L0", "wqk_b")).then_inc(q_ready, 1)

                    def exponential(b, h):
                        act.wait_ge(half_shifted, 2 * b + h + 1)
                        if not (isinstance(b, int) and b == 0):
                            act.wait_ge(half_turned, 2 * b + h - 1)
                        act.activation(flat(probs[:, HH * h:HH * h + HH]), flat(shifted[:, HH * h:HH * h + HH]),
                                       ACT.Exp).then_inc(half_exp, 1)

                    def copy(b, h):
                        act.wait_ge(half_turned, 2 * b + h + 1)
                        if not (isinstance(b, int) and b == 0):
                            act.wait_ge(half_weighed, 2 * b + h - 1)
                        act.copy(flat(probsT[:, HH * h:HH * h + HH]), banks(4, 2)).then_inc(half_copied, 1)

                    def batch(b, more):
                        exponential(b, 0)
                        copy(b, 0)
                        exponential(b, 1)
                        if more:
                            take(b + 2)
                        copy(b, 1)

                    take(0)
                    take(1)
                    for b in batches(act, 0, B - 2):
                        batch(b, True)
                    batch(B - 2, False)
                    batch(B - 1, False)

                @block.gpsimd
                def _(pool):
                    for b in batches(pool, 0, B):
                        for g in range(GROUPS):
                            if g % 2 == 0 and not (isinstance(b, int) and b == 0):
                                pool.wait_ge(scores_made, 2 * b + g // 2 - 1)
                            last = pool.tensor_tensor(
                                k_heads[:, 4 * g:4 * g + 4], k_rot[:, g, bass.ds(b, 1)].broadcast_to([128, 4, T]),
                                W("C", "latent_mask").unsqueeze(2).broadcast_to([128, 4, T]), ALU.mult)
                            if g % 2:
                                last.then_inc(k_ready, 1)

                @block.vector
                def _(vec):
                    def shift(b, h):
                        heads = slice(HH * h, HH * h + HH)
                        peak = row_max[:, heads].unsqueeze(2).broadcast_to([128, HH, T])
                        vec.wait_ge(scores_made, 2 * b + h + 1)
                        if not (isinstance(b, int) and b == 0):
                            vec.wait_ge(half_exp, 2 * b + h - 1)
                            vec.wait_ge(half_shifted, 2 * b + h - 1)
                        source = shifted[:, heads]
                        vec.scalar_tensor_tensor(out=source, in0=heads_first(h), scalar=scale,
                                                 in1=over_batches(causal, HH), op0=ALU.mult,
                                                 op1=ALU.add).then_inc(biased_made, 1)
                        vec.wait_ge(biased_made, 2 * b + h + 1)
                        vec.tensor_reduce(row_max[:, heads], source, AXIS_X, ALU.max).then_inc(max_made, 1)
                        vec.wait_ge(max_made, 2 * b + h + 1)
                        vec.tensor_tensor(shifted[:, heads], source, peak, ALU.subtract).then_inc(half_shifted, 1)

                    def normalise(b):
                        sums = bank(7)[:, 0:H * (HD + 1)].rearrange("p (h d) -> p h d", d=HD + 1)
                        vec.wait_ge(half_weighed, 2 * b + 2)
                        if not (isinstance(b, int) and b == 0):
                            vec.wait_ge(ctx_made, b)
                        vec.reciprocal(row_rec[:], sums[:, :, HD]).then_inc(rec_made, 1)
                        vec.wait_ge(rec_made, b + 1)
                        vec.tensor_tensor(ctx_all[:, bass.ds(b, 1)].rearrange("p b (h d) -> p (b h) d", d=HD),
                                          sums[:, :, 0:HD], row_rec[:].unsqueeze(2).broadcast_to([128, H, HD]),
                                          ALU.mult).then_inc(ctx_made, 1)

                    for b in range(2):
                        shift(b, 0)
                        shift(b, 1)
                    for b in batches(vec, 2, B):
                        shift(b, 0)
                        normalise(b - 2)
                        shift(b, 1)
                    normalise(B - 2)
                    normalise(B - 1)

        def attention_out(wo, bias=None, gem=None):
            ctxT = S(13)
            plan(pe=["cT0", "cT1", "o0", "o1"], vec=[] if gem is None else ["z0", "z1", "s0", "s1"],
                 act=["c0", "c1"] if gem is None else ["l0", "l1", "c0", "c1"])
            V.names += ["r0", "r1"]
            with nc.Block() as block:
                @block.tensor
                def _(pe):
                    for h in range(2):
                        for i in range(HB):
                            last = pe.transpose(by_batch(h)[:, i], normed[:, HB * h + i], ident)
                        last.then_inc(pe_done, P.step(f"cT{h}"))
                    for h in range(2):
                        if gem is None:
                            pe.wait_ge(act_done, A.after(f"c{h}"))
                        else:
                            pe.wait_ge(vec_done, V.after(f"s{h}"))
                        for i in range(HB):
                            last = pe.matmul(by_batch(2 + h)[:, i], ctxT[:, HB * h + i], wo, start=True, stop=True)
                        last.then_inc(pe_done, P.step(f"o{h}"))

                @block.scalar
                def _(act):
                    if gem is not None:
                        for h in range(2):
                            act.wait_ge(pe_done, P.after(f"cT{h}"))
                            act.activation(half(ctxT, h), by_batch(h), ACT.Ln, scale=2.0 ** LOG_LIFT).then_inc(
                                act_done, A.step(f"l{h}"))
                    for h in range(2):
                        if gem is not None:
                            act.wait_ge(vec_done, V.after(f"z{h}"))
                            act.activation(half(ctxT, h), half(ctxT, h), ACT.Exp, scale=gem[1]).then_inc(
                                act_done, A.step(f"c{h}"))
                            continue
                        act.wait_ge(pe_done, P.after(f"cT{h}"))
                        if bias is None:
                            last = act.copy(half(ctxT, h), by_batch(h))
                        else:
                            last = act.activation(half(ctxT, h), by_batch(h), ACT.Identity, bias=bias)
                        last.then_inc(act_done, A.step(f"c{h}"))

                @block.vector
                def _(vec):
                    if gem is not None:
                        for h in range(2):
                            vec.wait_ge(act_done, A.after(f"l{h}"))
                            vec.scalar_tensor_tensor(
                                out=half(ctxT, h), in0=half(ctxT, h), scalar=-LOG_LIFT * float(np.log(2.0)),
                                in1=gem[0][:, HB * h:HB * h + HB].unsqueeze(2).broadcast_to([128, HB, T]),
                                op0=ALU.add, op1=ALU.add).then_inc(vec_done, V.step(f"z{h}"))
                        for h in range(2):
                            vec.wait_ge(act_done, A.after(f"c{h}"))
                            vec.tensor_scalar(half(ctxT, h), half(ctxT, h), gem[2], None, ALU.subtract).then_inc(
                                vec_done, V.step(f"s{h}"))
                    for h in range(2):
                        vec.wait_ge(pe_done, P.after(f"o{h}"))
                        vec.tensor_tensor(half(residual, h), half(residual, h), by_batch(2 + h), ALU.add).then_inc(
                            vec_done, V.step(f"r{h}"))

        stacked_so_far = {"all": 0, "biased": 0}
        stack_rows = TERMS * HD
        peak_rows = PARTS * H
        query_stack, key_stack = (flat_all(scratch[:, 8 * j:8 * j + 8]).bitcast(BF16).rearrange(
            "p (h b t) -> p h b t", h=H, b=B) for j in range(2))
        query_parts, key_parts = (flat_all(scratch[:, 16:19]).bitcast(BF16)[
            :, PARTS * B * T * j:PARTS * B * T * (j + 1)].rearrange("p (m b t) -> p m b t", m=PARTS, b=B) for j in range(2))
        query_rest, key_rest = normed, S(19)
        minus_pick = minus_pick_space[0:peak_rows]
        WH = HH * (HD + 1)
        after_parts = flat_all(scratch[:, 18:20])
        padded = after_parts[:, 0:2 * HH * (WH + HD + 1)].rearrange("p (h c) -> p h c", h=2)
        sumsT = small_sums[0:WH]
        bias16 = flat(contextT[:]).bitcast(BF16)

        def stacked_attention(scale, values=values, mask=None, bias=None):
            first = B * stacked_so_far["all"]
            first_biased = B * stacked_so_far["biased"]
            stacked_so_far["all"] += 1
            stacked_so_far["biased"] += bias is not None
            ctx_all = normed

            def at_start(b, below=1):
                return isinstance(b, int) and b < below

            def of_head(stack, b, head):
                return stack[0:stack_rows, head, bass.ds(b, 1)]

            with nc.Block() as block:
                @block.tensor
                def _(pe):
                    def quarter(b, g):
                        if not (at_start(b) and g < 2):
                            pe.wait_ge(quarter_max, 4 * first + 4 * b + g - 1)
                        if mask is not None:
                            pe.matmul(by_batch(g % 2), ident16[:], over_batches(mask16[:], 4), start=True, stop=False)
                        if bias is not None:
                            pe.matmul(bank(g % 2), ident16[:], bias16[:, 4 * g * T:(4 * g + 4) * T], start=True, stop=False)
                        for i in range(4):
                            last = pe.matmul(by_batch(g % 2)[:, i], of_head(query_stack, b, 4 * g + i),
                                             of_head(key_stack, b, 4 * g + i), start=mask is None and bias is None,
                                             stop=i == 3 or (mask is None and bias is None))
                        last.then_inc(quarter_made, 1)

                    def turn_peaks(b):
                        pe.wait_ge(peaks_split, first + b + 1)
                        pe.matmul(bank(1, T, rows=peak_rows), peak_parts[:], ident16[:], start=True,
                                  stop=True).then_inc(peaks_turned, 1)

                    def turned(b, h):
                        if h == 0:
                            pe.wait_ge(peaks_ready, first + b + 1)
                        if not at_start(b):
                            pe.wait_ge(half_probs, 2 * first + 2 * b + h - 1)
                            if bias is not None:
                                pe.wait_ge(turned_biased, 2 * first_biased + 2 * b + h - 1)
                        for i in range(HH):
                            head, out = HH * h + i, by_batch(2 + 2 * h, 2)[:, i]
                            pe.matmul(out, of_head(key_stack, b, head), of_head(query_stack, b, head), start=True,
                                      stop=False)
                            if mask is not None:
                                pe.matmul(out, mask16[:], ident16[:], start=False, stop=False)
                            last = pe.matmul(out, minus_pick[:, head], peakT[0:peak_rows], start=False, stop=True)
                        last.then_inc(turned_made, 1)

                    def weigh(b, h, between=None):
                        if h == 0 and not at_start(b):
                            pe.wait_ge(sums_taken, first + b)
                        pe.wait_ge(half_padded, 2 * first + 2 * b + h + 1)
                        pe.wait_ge(half_probs, 2 * first + 2 * b + h + 1)
                        for i in range(HH):
                            if between is not None and i == 5:
                                turn_peaks(between)
                            last = pe.matmul(psum[0:WH, 6, h * T:(h + 1) * T], padded[:, h, i * WH:(i + 1) * WH],
                                             probsT[:, HH * h + i], start=i == 0, stop=i == HH - 1)
                        last.then_inc(half_summed, 1)

                    def turn_sums(b):
                        pe.wait_ge(sums_taken, first + b + 1)
                        if not at_start(b):
                            pe.wait_ge(results_made, first + b)
                        for h in range(2):
                            last = pe.transpose(bank(7)[:, h * WH:(h + 1) * WH], sumsT[:, h], ident[0:WH, 0:WH])
                        last.then_inc(sums_turned, 1)

                    def batch(b, before=True, more=True):
                        turned(b, 0)
                        if more:
                            quarter(b + 1, 0)
                            quarter(b + 1, 1)
                        if before:
                            weigh(b - 1, 1)
                        if more:
                            quarter(b + 1, 2)
                            quarter(b + 1, 3)
                        turned(b, 1)
                        if before:
                            turn_sums(b - 1)
                        weigh(b, 0, between=b + 1 if more else None)

                    for g in range(4):
                        quarter(0, g)
                    turn_peaks(0)
                    batch(0, before=False)
                    for b in range(1, B - 1):
                        batch(b)
                    batch(B - 1, more=False)
                    weigh(B - 1, 1)
                    turn_sums(B - 1)

                @block.scalar
                def _(act):
                    act.preload_act_table(ACT.Exp)

                    def take_peaks(b):
                        act.wait_ge(peaks_turned, first + b + 1)
                        if not at_start(b):
                            act.wait_ge(turned_made, 2 * first + 2 * b)
                        act.copy(peakT[0:peak_rows], bank(1, T, rows=peak_rows)).then_inc(peaks_ready, 1)

                    def exponential(b, h):
                        if bias is None:
                            act.wait_ge(turned_made, 2 * first + 2 * b + h + 1)
                        else:
                            act.wait_ge(turned_biased, 2 * first_biased + 2 * b + h + 1)
                        if not at_start(b):
                            act.wait_ge(half_summed, 2 * first + 2 * b + h - 1)
                        half_heads = slice(HH * h, HH * h + HH)
                        act.activation(flat(probsT[:, half_heads]),
                                       banks(2 + 2 * h, 2) if bias is None else flat(shifted[:, half_heads]),
                                       ACT.Exp, scale=scale if bias is None else 1.0).then_inc(half_probs, 1)

                    def take_sums(b):
                        act.wait_ge(half_summed, 2 * first + 2 * b + 2)
                        if not at_start(b):
                            act.wait_ge(sums_turned, first + b)
                        act.copy(flat(sumsT), bank(6, 2 * T, rows=WH)).then_inc(sums_taken, 1)

                    def second_half(b):
                        if bias is None:
                            exponential(b, 1)
                        take_peaks(b + 1)
                        if bias is not None:
                            exponential(b, 1)

                    take_peaks(0)
                    exponential(0, 0)
                    second_half(0)
                    for b in batches(act, 1, B - 1):
                        exponential(b, 0)
                        take_sums(b - 1)
                        second_half(b)
                    exponential(B - 1, 0)
                    take_sums(B - 2)
                    exponential(B - 1, 1)
                    take_sums(B - 1)

                @block.gpsimd
                def _(pool):
                    pool.memset(padded, 0.0).then_inc(pads_cleared, 1)
                    pool.wait_ge(pads_cleared, first // B + 1)
                    for b in batches(pool, 0, B):
                        for h in range(2):
                            if not at_start(b):
                                pool.wait_ge(half_summed, 2 * first + 2 * b + h - 1)
                            pool.tensor_copy(padded[:, h].rearrange("p (i c) -> p i c", i=HH)[:, :, 0:HD + 1],
                                             values[:, bass.ds(b, 1), HH * h:HH * h + HH].rearrange(
                                                 "p b h d -> p (b h) d")).then_inc(half_padded, 1)

                @block.vector
                def _(vec):
                    def bias_of(start, n):
                        return bias[:, start * T:(start + n) * T].rearrange("p (h k) -> p h k", k=T)

                    def largest(b, g):
                        heads = slice(4 * g, 4 * g + 4)
                        source = by_batch(g % 2)
                        vec.wait_ge(quarter_made, 4 * first + 4 * b + g + 1)
                        if not at_start(b):
                            vec.wait_ge(peaks_split, first + b)
                        vec.tensor_reduce(row_max[:, heads], source, AXIS_X, ALU.max).then_inc(quarter_max, 1)

                    def split(b):
                        high, mid, low = (peak_parts[:, H * j:H * j + H] for j in range(PARTS))
                        n = 3 * (first + b)
                        vec.wait_ge(quarter_max, 4 * first + 4 * b + 4)
                        if not at_start(b):
                            vec.wait_ge(peaks_turned, first + b)
                        vec.tensor_copy(high, row_max[:]).then_inc(part_made, 1)
                        vec.wait_ge(part_made, n + 1)
                        vec.tensor_tensor(row_rest[:], row_max[:], high, ALU.subtract).then_inc(part_made, 1)
                        vec.wait_ge(part_made, n + 2)
                        vec.tensor_copy(mid, row_rest[:]).then_inc(part_made, 1)
                        vec.wait_ge(part_made, n + 3)
                        vec.tensor_tensor(low, row_rest[:], mid, ALU.subtract).then_inc(peaks_split, 1)

                    def bias_turned(b, h):
                        vec.wait_ge(turned_made, 2 * first + 2 * b + h + 1)
                        if not at_start(b):
                            vec.wait_ge(half_probs, 2 * first + 2 * b + h - 1)
                        vec.scalar_tensor_tensor(out=shifted[:, HH * h:HH * h + HH], in0=by_batch(2 + 2 * h, 2),
                                                 scalar=scale, in1=bias_of(HH * h, HH), op0=ALU.mult,
                                                 op1=ALU.add).then_inc(turned_biased, 1)

                    def normalise(b):
                        sums = bank(7)[:, 0:H * (HD + 1)].rearrange("p (h d) -> p h d", d=HD + 1)
                        vec.wait_ge(sums_turned, first + b + 1)
                        if not at_start(b):
                            vec.wait_ge(results_made, first + b)
                        vec.reciprocal(row_rec[:], sums[:, :, HD]).then_inc(sums_inverted, 1)
                        vec.wait_ge(sums_inverted, first + b + 1)
                        vec.tensor_tensor(ctx_all[:, bass.ds(b, 1)].rearrange("p b (h d) -> p (b h) d", d=HD),
                                          sums[:, :, 0:HD], row_rec[:].unsqueeze(2).broadcast_to([128, H, HD]),
                                          ALU.mult).then_inc(results_made, 1)

                    def batch(b, before=True, more=True):
                        if bias is not None:
                            bias_turned(b, 0)
                        if more:
                            for g in range(4):
                                largest(b + 1, g)
                        if more:
                            split(b + 1)
                        if bias is not None:
                            bias_turned(b, 1)
                        if before:
                            normalise(b - 1)

                    for g in range(4):
                        largest(0, g)
                    split(0)
                    batch(0, before=False)
                    for b in batches(vec, 1, B - 1):
                        batch(b)
                    batch(B - 1, more=False)
                    normalise(B - 1)

        def stacked_prologue(pack, q, k, q_b=None, k_b=None, wv=None, vb=None, ob=None, self_attention=False, mask=None,
                             bias=None, scale=None):
            made = [] if wv is None else ["v0", "v1"]
            source = normedT if self_attention else contextT
            n = stacked_so_far["all"]
            plan(pe=["k", *made, *LN["pe"], "q0", "q1"] if not self_attention else [*LN["pe"], "q0", "q1", "k", *made],
                 act=(["khigh", "kmid", *LN["act"], "qhigh0", "qhigh1", "qmid0", "qmid1"] if not self_attention else
                      [*LN["act"], "qhigh0", "qhigh1", "qmid0", "qmid1", "khigh", "kmid"]),
                 vec=(["stats", "aggr", "krest", "xn0", "xn1", "qrest0", "qrest1", "qlow0", "qlow1", *made,
                       *(ternary_steps("L1") if n == 0 else [])]
                      if not self_attention else
                      [*LN["vec"], "qrest0", "qrest1", "qlow0", "qlow1", "krest", *made]),
                 pool=[*LN["pool"], "klow", *(["bias"] if ob is not None else []), *(["pick"] if n == 0 else []),
                       *(["bias16"] if bias is not None else [])])

            def k_product(pe):
                for h in range(2):
                    last = pe.matmul(bank(4 + h), k, half(source, h), start=True, stop=True)
                last.then_inc(pe_done, P.step("k"))

            def v_product(pe):
                for h in range(len(made)):
                    for i in range(HB):
                        last = pe.matmul(by_batch(2 + h)[:, i], source[:, HB * h + i], wv, start=True, stop=True)
                    last.then_inc(pe_done, P.step(f"v{h}"))

            def part(act, out, source, bias):
                return act.copy(out, source) if bias is None else act.activation(out, source, ACT.Identity, bias=bias)

            def rest(vec, out, source, bias, high):
                return vec.scalar_tensor_tensor(out=out, in0=source, scalar=0.0 if bias is None else bias, in1=high,
                                                op0=ALU.add, op1=ALU.subtract)

            with nc.Block() as block:
                @block.sync
                def _(sync):
                    def stack(parts, target, order, ready, signal):
                        for m in range(PARTS):
                            ready(m)
                            for t in range(TERMS):
                                if order[t] == m:
                                    sync.dma_start(target[HD * t:HD * t + HD], parts[:, m]).then_inc(signal, 16)

                    def key_ready(m):
                        if m == 2:
                            sync.wait_ge(pool_done, G.after("klow"))
                        else:
                            sync.wait_ge(act_done, A.after(("khigh", "kmid")[m]))

                    def query_ready(m):
                        if m == 2:
                            sync.wait_ge(vec_done, V.after("qlow1"))
                        else:
                            sync.wait_ge(act_done, A.after(("qhigh1", "qmid1")[m]))

                    stacks = [(key_parts, key_stack, KEY_PARTS, key_ready, keys_stacked),
                              (query_parts, query_stack, QUERY_PARTS, query_ready, queries_stacked)]
                    for args in reversed(stacks) if self_attention else stacks:
                        stack(*args)
                    dmas = 16 * TERMS * (n + 1)
                    sync.wait_ge(keys_stacked, dmas)
                    sync.wait_ge(queries_stacked, dmas)

                @block.vector
                def _(vec):
                    def key_rest_step():
                        vec.wait_ge(act_done, A.after("khigh"))
                        rest(vec, key_rest, by_batch(4, 2), k_b, key_parts[:, 0]).then_inc(vec_done, V.step("krest"))

                    if self_attention:
                        ln_vector(vec, residual, normed)
                    else:
                        ln_vector(vec, residual, normed, between=key_rest_step)
                    for h in range(2):
                        vec.wait_ge(act_done, A.after(f"qhigh{h}"))
                        rest(vec, half(query_rest, h), by_batch(6 + h), q_b, half(query_parts[:, 0], h)).then_inc(
                            vec_done, V.step(f"qrest{h}"))
                    for h in range(2):
                        vec.wait_ge(act_done, A.after(f"qmid{h}"))
                        vec.tensor_tensor(half(query_parts[:, 2], h), half(query_rest, h), half(query_parts[:, 1], h),
                                          ALU.subtract).then_inc(vec_done, V.step(f"qlow{h}"))
                    if self_attention:
                        key_rest_step()
                    if mask is not None:
                        vec.tensor_copy(mask16[:], mask)
                    for h in range(len(made)):
                        vec.wait_ge(pe_done, P.after(f"v{h}"))
                        target = half(values, h)[:, :, :, 0:HD].rearrange("p b h d -> p (b h) d")
                        if vb is None:
                            last = vec.tensor_copy(target, bank(2 + h).rearrange("p (b d) -> p b d", d=HD))
                        else:
                            for i in range(HB):
                                last = vec.tensor_tensor(
                                    values[:, HB * h + i, :, 0:HD],
                                    by_batch(2 + h)[:, i].rearrange("p (h d) -> p h d", d=HD),
                                    vb.rearrange("p (h d) -> p h d", d=HD), ALU.add)
                        last.then_inc(vec_done, V.step(f"v{h}"))
                    if n == 0:
                        vec.wait_ge(pool_done, G.after("klow"))
                        make_ternary(vec, "L1", flat(key_rest[:, 0:HB]))

                @block.gpsimd
                def _(pool):
                    ln_pool(pool)
                    pool.wait_ge(vec_done, V.after("krest"))
                    pool.wait_ge(act_done, A.after("kmid"))
                    pool.tensor_tensor(key_parts[:, 2], key_rest, key_parts[:, 1], ALU.subtract).then_inc(
                        pool_done, G.step("klow"))
                    pool.wait_ge(loaded[pack], 16)
                    if ob is not None:
                        add_bias(pool, ob)
                    if n == 0:
                        pool.tensor_tensor(minus_pick, ones[0:peak_rows, 0:T].unsqueeze(1).broadcast_to([peak_rows, H, T]),
                                       W("C", "minus_pick", rows=slice(0, peak_rows)).unsqueeze(2).broadcast_to(
                                           [peak_rows, H, T]), ALU.mult).then_inc(pool_done, G.step("pick"))
                    if bias is not None:
                        pool.wait_ge(pe_done, P.after("v1"))
                        pool.tensor_scalar(bias16, bias, 1.0 / scale, None, ALU.mult).then_inc(
                            pool_done, G.step("bias16"))

                @block.tensor
                def _(pe):
                    pe.wait_ge(loaded[pack], 16)
                    if not self_attention:
                        k_product(pe)
                        v_product(pe)
                    ln_tensor(pe)
                    for h in range(2):
                        pe.wait_ge(act_done, A.after(f"xnT{h}"))
                        pe.matmul(bank(6 + h), q, half(normedT, h), start=True, stop=True).then_inc(
                            pe_done, P.step(f"q{h}"))
                    if self_attention:
                        k_product(pe)
                        v_product(pe)

                @block.scalar
                def _(act):
                    def keys():
                        act.wait_ge(pe_done, P.after("k"))
                        part(act, key_parts[:, 0], by_batch(4, 2), k_b).then_inc(act_done, A.step("khigh"))
                        act.wait_ge(vec_done, V.after("krest"))
                        act.copy(key_parts[:, 1], key_rest).then_inc(act_done, A.step("kmid"))

                    act.wait_ge(loaded[pack], 16)
                    if not self_attention:
                        keys()
                    ln_scalar(act)
                    for h in range(2):
                        act.wait_ge(pe_done, P.after(f"q{h}"))
                        part(act, half(query_parts[:, 0], h), by_batch(6 + h), q_b).then_inc(
                            act_done, A.step(f"qhigh{h}"))
                    for h in range(2):
                        act.wait_ge(vec_done, V.after(f"qrest{h}"))
                        act.copy(half(query_parts[:, 1], h), half(query_rest, h)).then_inc(
                            act_done, A.step(f"qmid{h}"))
                    if self_attention:
                        keys()

        peaks, p_inv = small[:, 20], small[:, 21, 0:1]
        def latent_prologue():
            q_rot, k_rot = scratch[:, 0:4], scratch[:, 4:8]
            lat, swapped = S(12), S(13)
            qkvT, vlat = scratch[:, 8:11], [S(11), S(14)]
            mean_v, mean_z = probs[:, 0:B], probs[:, B:H]
            p_abs, p_sign, p_used, p_moved = (small[:, 16 + j, 0:1] for j in range(4))
            turns, red, absolute = shifted[:, 0], shifted[:, 1], shifted[:, 2]
            sums = small[:, 0]
            n_mats = len(ternary_weights)
            c1, c2 = 6.28125, float(2 * np.pi - 6.28125)
            groups = [(x, g) for x in "qk" for g in range(GROUPS)]
            at_bank = lambda u: 4 * ((u + 1) % 2)
            plan(pe=[*LN["pe"], "q", "k", "v", "mean", *[f"{x}{s}{g}" for x, g in groups for s in ("l", "s")],
                     "vl0", *[x for g in range(1, GROUPS) for x in (f"vl{g}", f"vo{g - 1}")], "vo3", "meanT", "vT", "wsum"],
                 act=[*LN["act"], "q", "k", "v", "mean", "abs", "sign", "ln", "exp", *[f"v{g}" for g in range(GROUPS)],
                      "vo", "sin_p", "abs_p", "cos_p"],
                 vec=[*LN["vec"], "moved", "qc0", "qs0", "qr0", "pclip", "p", "pinv", "vclip",
                      *[f"{x}{s}{g}" for x, g in groups[1:4] for s in ("c", "s", "r")], "z", "peak", "less",
                      *[f"{x}{s}{g}" for x, g in groups[4:] for s in ("c", "s", "r")],
                      "wabs", "p0", "p1", "p2", "p3", "p4", "mean_values", "v", "wclip", "wrec"],
                 pool=[*LN["pool"], "bias"])
            with nc.Block() as block:
                @block.vector
                def _(vec):
                    ts, stt = vec.tensor_scalar, vec.scalar_tensor_tensor

                    def chain(ins, name):
                        ins.then_inc(vec_done, V.step(name))
                        vec.wait_ge(vec_done, V.after(name))

                    def rotate(u):
                        x, g = groups[u]
                        bias = "q_lat_b" if x == "q" else "kv_lat_b"
                        swap = "q_swap_b" if x == "q" else "k_swap_b"
                        vec.wait_ge(pe_done, P.after(f"{x}l{g}"))
                        if u:
                            px, pg = groups[u - 1]
                            vec.wait_ge(vec_done, V.after(f"{px}r{pg}"))
                        stt(out=lat, in0=by_batch(at_bank(u), 2), scalar=W("L0", bias),
                            in1=over_batches(W("L0", "cos"), B), op0=ALU.add,
                            op1=ALU.mult).then_inc(vec_done, V.step(f"{x}c{g}"))
                        vec.wait_ge(pe_done, P.after(f"{x}s{g}"))
                        chain(stt(out=swapped, in0=by_batch(at_bank(u) + 2, 2), scalar=W("L0", swap),
                                  in1=over_batches(W("L0", "sin"), B), op0=ALU.add, op1=ALU.mult), f"{x}s{g}")
                        vec.tensor_tensor((q_rot if x == "q" else k_rot)[:, g], lat, swapped,
                                          ALU.add).then_inc(vec_done, V.step(f"{x}r{g}"))

                    ln_vector(vec, residual, normed)
                    vec.wait_ge(loaded["L0"], 16)
                    ts(p_moved, W("L0", "p"), 0.0005, None, ALU.add).then_inc(vec_done, V.step("moved"))
                    rotate(0)
                    vec.wait_ge(act_done, A.after("sign"))
                    chain(ts(p_abs, p_abs, 0.001, 100.0, ALU.max, ALU.min), "pclip")
                    chain(vec.tensor_tensor(p_used, p_abs, p_sign, ALU.mult), "p")
                    vec.reciprocal(p_inv, p_used).then_inc(vec_done, V.step("pinv"))
                    ts(mean_v, mean_v, 1e-10, None, ALU.max).then_inc(vec_done, V.step("vclip"))
                    for u in range(1, 4):
                        rotate(u)
                    vec.wait_ge(act_done, A.after("ln"))
                    chain(ts(mean_z, mean_z, p_used, None, ALU.mult), "z")
                    chain(vec.tensor_reduce(peaks, mean_z, AXIS_X, ALU.max), "peak")
                    vec.tensor_tensor(mean_z, mean_z, peaks.unsqueeze(2).broadcast_to([128, B, T]),
                                      ALU.subtract).then_inc(vec_done, V.step("less"))
                    for u in range(4, 8):
                        rotate(u)
                    vec.wait_ge(loaded["L1"], 16)
                    vec.wait_ge(loaded["L3"], 16)
                    for m, (pack, name) in enumerate(ternary_weights):
                        last = vec.tensor_reduce(sums[:, m:m + 1], W(pack, name), AXIS_X, ALU.add,
                                                 apply_absolute_value=True)
                    last.then_inc(vec_done, V.step("wabs"))
                    chain(ts(turns, W("L1", "phases"), float(1 / (2 * np.pi)), ROUND, ALU.mult, ALU.add), "p0")
                    chain(ts(turns, turns, ROUND, None, ALU.subtract), "p1")
                    chain(stt(out=red, in0=turns, scalar=-c1, in1=W("L1", "phases"), op0=ALU.mult, op1=ALU.add), "p2")
                    chain(stt(out=red, in0=turns, scalar=-c2, in1=red, op0=ALU.mult, op1=ALU.add), "p3")
                    ts(red, red, PI_BELOW, -PI_BELOW, ALU.min, ALU.max).then_inc(vec_done, V.step("p4"))
                    for source, target, n, name in ((6, mean_values, "meanT", "mean_values"), (2, values, "vT", "v")):
                        vec.wait_ge(pe_done, P.after(n))
                        vec.tensor_copy(target[:, :, :, 0:HD].rearrange("p b h d -> p (b h) d"),
                                        banks(source, 2).rearrange("p (b d) -> p b d", d=HD)).then_inc(
                            vec_done, V.step(name))
                    vec.wait_ge(pe_done, P.after("wsum"))
                    chain(ts(weight_scales[:, 0:n_mats], bank(0, n_mats), 1.0 / (FF * D), 1e-5, ALU.mult, ALU.max),
                          "wclip")
                    vec.reciprocal(weight_inverses[:, 0:n_mats], weight_scales[:, 0:n_mats]).then_inc(
                        vec_done, V.step("wrec"))

                @block.gpsimd
                def _(pool):
                    ln_pool(pool)
                    pool.wait_ge(loaded["L0"], 16)
                    add_bias(pool, W("L0", "cproj_b"))

                @block.tensor
                def _(pe):
                    def product(n, weight, source, start=True, stop=True):
                        for h in range(2):
                            last = pe.matmul(bank(n + h), weight, half(source, h), start=start, stop=stop)
                        return last

                    ln_tensor(pe)
                    pe.wait_ge(loaded["L0"], 16)
                    pe.wait_ge(act_done, A.after("xnT1"))
                    for j, x in enumerate("qkv"):
                        product(2 + 2 * j, W("L0", "qkv", j * D, D), normedT).then_inc(pe_done, P.step(x))
                    product(0, W("L0", "mean_v"), contextT).then_inc(pe_done, P.step("mean"))
                    pe.wait_ge(act_done, A.after("v"))
                    for u, (x, g) in enumerate(groups):
                        if u == 1:
                            pe.wait_ge(act_done, A.after("mean"))
                        if u >= 2:
                            px, pg = groups[u - 2]
                            pe.wait_ge(vec_done, V.after(f"{px}s{pg}"))
                        lat_w, swap_w = ("q_lat", "q_swap") if x == "q" else ("kv_lat", "k_swap")
                        source = qkvT[:, "qk".index(x)]
                        product(at_bank(u), W("L0", lat_w, g * 128, 128), source).then_inc(
                            pe_done, P.step(f"{x}l{g}"))
                        product(at_bank(u) + 2, W("L0", swap_w, g * 128, 128), source).then_inc(
                            pe_done, P.step(f"{x}s{g}"))
                    pe.wait_ge(vec_done, V.after("ks3"))
                    for g in range(GROUPS + 1):
                        if g < GROUPS:
                            if g >= 2:
                                pe.wait_ge(act_done, A.after(f"v{g - 2}"))
                            product(2 * (g % 2), W("L0", "kv_lat", g * 128, 128), qkvT[:, 2]).then_inc(
                                pe_done, P.step(f"vl{g}"))
                        if g:
                            pe.wait_ge(act_done, A.after(f"v{g - 1}"))
                            product(4, W("L0", "l2o", (g - 1) * 128, 128), vlat[(g - 1) % 2], start=g == 1,
                                    stop=g == GROUPS).then_inc(pe_done, P.step(f"vo{g - 1}"))
                    pe.wait_ge(act_done, A.after("exp"))
                    for b in range(B):
                        last = pe.transpose(by_batch(6, 2)[:, b], mean_v[:, b], ident)
                    last.then_inc(pe_done, P.step("meanT"))
                    pe.wait_ge(act_done, A.after("vo"))
                    for b in range(B):
                        last = pe.transpose(by_batch(2, 2)[:, b], S(12)[:, b], ident)
                    last.then_inc(pe_done, P.step("vT"))
                    pe.wait_ge(vec_done, V.after("wabs"))
                    pe.matmul(bank(0, n_mats), ones[:, 0:128], sums[:, 0:n_mats], start=True, stop=True).then_inc(
                        pe_done, P.step("wsum"))

                @block.scalar
                def _(act):
                    ln_scalar(act)
                    act.wait_ge(loaded["L0"], 16)
                    for j, x in enumerate("qkv"):
                        act.wait_ge(pe_done, P.after(x))
                        act.activation(qkvT[:, j], by_batch(2 + 2 * j, 2), ACT.Identity,
                                       bias=W("L0", "qkv_b", j, 1)).then_inc(act_done, A.step(x))
                    act.wait_ge(pe_done, P.after("mean"))
                    act.activation(mean_v, by_batch(0, 2), ACT.Abs, bias=W("L0", "shift")).then_inc(
                        act_done, A.step("mean"))
                    act.activation(p_abs, W("L0", "p"), ACT.Abs).then_inc(act_done, A.step("abs"))
                    act.wait_ge(vec_done, V.after("moved"))
                    act.activation(p_sign, p_moved, ACT.Sign).then_inc(act_done, A.step("sign"))
                    act.wait_ge(vec_done, V.after("vclip"))
                    act.activation(mean_z, mean_v, ACT.Ln).then_inc(act_done, A.step("ln"))
                    act.wait_ge(vec_done, V.after("less"))
                    act.activation(mean_v, mean_z, ACT.Exp).then_inc(act_done, A.step("exp"))
                    for g in range(GROUPS):
                        act.wait_ge(pe_done, P.after(f"vl{g}"))
                        if g >= 2:
                            act.wait_ge(pe_done, P.after(f"vo{g - 2}"))
                        act.activation(vlat[g % 2], by_batch(2 * (g % 2), 2), ACT.Identity, bias=W("L0", "kv_lat_b")).then_inc(
                            act_done, A.step(f"v{g}"))
                    act.wait_ge(pe_done, P.after("vo3"))
                    act.wait_ge(vec_done, V.after("kr3"))
                    act.copy(S(12), by_batch(4, 2)).then_inc(act_done, A.step("vo"))
                    act.wait_ge(vec_done, V.after("p4"))
                    act.activation(position_waves[:, 0], red, ACT.Sin).then_inc(act_done, A.step("sin_p"))
                    act.activation(absolute, red, ACT.Abs).then_inc(act_done, A.step("abs_p"))
                    act.wait_ge(act_done, A.after("abs_p"))
                    act.activation(position_waves[:, 1], absolute, ACT.Sin, bias=half_pi[:], scale=-1.0).then_inc(
                        act_done, A.step("cos_p"))
            return q_rot, k_rot

        def hinge_ffn():
            steps = INNER // 2
            s, g = S(0), S(1)
            hinge = [S(2), S(3)]
            plan(pe=[*LN["pe"], "s", "o0", "o1"], act=[*LN["act"], "s", *[f"h{i}" for i in range(steps)]],
                 vec=[*LN["vec"], *[f"g{i}" for i in range(steps)], "r0", "r1"], pool=[*LN["pool"], "bias"])
            with nc.Block() as block:
                @block.vector
                def _(vec):
                    ln_vector(vec, residual, normed)
                    for i in range(steps):
                        vec.wait_ge(act_done, A.after(f"h{i}"))
                        w2 = W("L0", "w2", i, 1)
                        if i == 0:
                            last = vec.tensor_scalar(g, hinge[0], w2, W("L0", "b2"), ALU.mult, ALU.add)
                        else:
                            vec.wait_ge(vec_done, V.after(f"g{i - 1}"))
                            last = vec.scalar_tensor_tensor(out=g, in0=hinge[i % 2], scalar=w2, in1=g, op0=ALU.mult,
                                                            op1=ALU.add)
                        last.then_inc(vec_done, V.step(f"g{i}"))
                    vec.wait_ge(pool_done, G.after("bias"))
                    for h in range(2):
                        vec.wait_ge(pe_done, P.after(f"o{h}"))
                        vec.tensor_tensor(half(residual, h), half(residual, h), by_batch(4 + h), ALU.add).then_inc(
                            vec_done, V.step(f"r{h}"))

                @block.gpsimd
                def _(pool):
                    ln_pool(pool)
                    add_bias(pool, W("L0", "bout"))

                @block.tensor
                def _(pe):
                    ln_tensor(pe)
                    for h in range(2):
                        pe.wait_ge(act_done, A.after(f"xnT{h}"))
                        last = pe.matmul(bank(2 + h), W("L0", "win"), half(normedT, h), start=True, stop=True)
                    last.then_inc(pe_done, P.step("s"))
                    pe.wait_ge(vec_done, V.after(f"g{steps - 1}"))
                    for h in range(2):
                        for i in range(HB):
                            last = pe.matmul(by_batch(4 + h)[:, i], g[:, HB * h + i], W("L0", "wout"), start=True,
                                             stop=True)
                        last.then_inc(pe_done, P.step(f"o{h}"))

                @block.scalar
                def _(act):
                    ln_scalar(act)
                    act.wait_ge(pe_done, P.after("s"))
                    act.activation(s, by_batch(2, 2), ACT.Identity, bias=W("L0", "bin")).then_inc(
                        act_done, A.step("s"))
                    act.wait_ge(act_done, A.after("s"))
                    for i in range(steps):
                        if i >= 2:
                            act.wait_ge(vec_done, V.after(f"g{i - 2}"))
                        act.activation(hinge[i % 2], s, ACT.Relu, bias=W("L0", "b1", i, 1),
                                       scale=W("L0", "w1", i, 1)).then_inc(act_done, A.step(f"h{i}"))

        stages = []

        def stage(f):
            stages.append(f)

        stage(lambda: (
            latent_attention(LAT ** -0.5, W("L0", "causal"), *latent_prologue()),
            attention_out(W("L0", "cproj"), bias=W("L0", "l2o_b"))))

        def cross(pack):
            bias = W("L3", "alibi") if pack == "L3" else None
            stacked_prologue(pack, W(pack, "xq"), W(pack, "xk"), W(pack, "xq_b"), W(pack, "xk_b"), W(pack, "xv"),
                             W(pack, "xv_b"), W(pack, "xo_b"), bias=bias, scale=HD ** -0.5)
            stacked_attention(HD ** -0.5, bias=bias)
            attention_out(W(pack, "xo"))

        stage(lambda: cross("L0"))
        stage(hinge_ffn)

        def phase_memory():
            pv, keys, kv, hidden, branch, gates, logit1, diff, w_pos, w_kv, angle, sin_k, cos_k = (
                S(i) for i in range(13))
            tmp = S(13)
            sin_p, cos_p = position_waves[:, 0], position_waves[:, 1]
            carry = probs[:, 0:B]
            a0, a1, m0, m1 = (x for x in (probs[:, B:H], probsT[:, 0:B], probsT[:, B:H], k_heads[:, 0:B]))
            m2, m3 = k_heads[:, B:H], tmp
            w = lambda name: W("L1", name)
            plan(pe=[*LN["pe"], "pv", "keys", "kv", "hidden", "branch", "gate", "l0", "l1", "turn", "lnT", "out"],
                 act=[*LN["act"], "pv", "keys", "kv", "hidden", "branch", "l1", "gates",
                      "w_pos", "w_kv", "abs_k", "sin_k", "cos_k", "sqrt", "tokens", "ln"],
                 vec=[*LN["vec"], "const", "carry", "cv", "cm", "sv", "sm", "pc", "ps", "p", "k0", "angle", "diff",
                      "g", "gmax", "vg", "wc", "wm", "ws", "wn", "rec",
                      "kc", "ks", "k", "kn", "bp", "bk", "b", "scaled",
                      *[x + "2" for x in LN["vec"]], "r0", "r1"],
                 pool=[*LN["pool"], "bias", "input", "eps2", "rstd2"])
            with nc.Block() as block:
                @block.tensor
                def _(pe):
                    def product(n, weight, source, start=True, stop=True, rows=128):
                        for h in range(2):
                            last = pe.matmul(bank(n + h, rows=rows), weight, half(source, h), start=start, stop=stop)
                        return last

                    ln_tensor(pe)
                    pe.wait_ge(loaded["L1"], 16)
                    pe.wait_ge(act_done, A.after("xnT1"))
                    product(0, w("wpv"), normedT).then_inc(pe_done, P.step("pv"))
                    product(2, w("wk"), normedT).then_inc(pe_done, P.step("keys"))
                    product(4, w("wkv"), normedT).then_inc(pe_done, P.step("kv"))
                    product(6, w("wg1"), normedT, stop=False)
                    product(6, w("wg1_shift"), normedT_padded[:, :, 0:T], start=False).then_inc(
                        pe_done, P.step("hidden"))
                    pe.wait_ge(act_done, A.after("pv"))
                    product(0, w("wb1"), normedT, rows=64).then_inc(pe_done, P.step("branch"))
                    pe.wait_ge(act_done, A.after("hidden"))
                    product(6, w("wg2"), hidden).then_inc(pe_done, P.step("gate"))
                    pe.wait_ge(act_done, A.after("branch"))
                    product(2, W("L1", "wb2_0", rows=slice(0, 64)), branch[0:64]).then_inc(pe_done, P.step("l0"))
                    product(4, W("L1", "wb2_1", rows=slice(0, 64)), branch[0:64]).then_inc(pe_done, P.step("l1"))
                    pe.wait_ge(vec_done, V.after("scaled"))
                    for b in range(B):
                        last = pe.transpose(by_batch(0, 2)[:, b], a0[:, b], ident)
                    last.then_inc(pe_done, P.step("turn"))
                    pe.wait_ge(vec_done, V.after("xn12"))
                    for b in range(B):
                        last = pe.transpose(by_batch(2, 2)[:, b], a1[:, b], ident)
                    last.then_inc(pe_done, P.step("lnT"))
                    pe.wait_ge(act_done, A.after("ln"))
                    for b in range(B):
                        last = pe.matmul(by_batch(4, 2)[:, b], m0[:, b], w("wo"), start=True, stop=True)
                    last.then_inc(pe_done, P.step("out"))

                @block.scalar
                def _(act):
                    ln_scalar(act)
                    act.wait_ge(pe_done, P.after("pv"))
                    act.activation(pv, by_batch(0, 2), ACT.Identity, bias=w("bpv")).then_inc(act_done, A.step("pv"))
                    act.wait_ge(pe_done, P.after("keys"))
                    act.activation(keys, by_batch(2, 2), ACT.Tanh, bias=w("bk")).then_inc(act_done, A.step("keys"))
                    act.wait_ge(pe_done, P.after("kv"))
                    act.activation(kv, by_batch(4, 2), ACT.Identity, bias=w("bkv")).then_inc(act_done, A.step("kv"))
                    act.wait_ge(pe_done, P.after("hidden"))
                    act.activation(hidden, by_batch(6, 2), ACT.Gelu, bias=w("bg1")).then_inc(
                        act_done, A.step("hidden"))
                    act.wait_ge(pe_done, P.after("branch"))
                    act.activation(branch[0:64], psum[0:64, 0:2, :].rearrange("p k (b c) -> p (k b) c", c=T), ACT.Gelu,
                                   bias=W("L1", "bb1", rows=slice(0, 64))).then_inc(act_done, A.step("branch"))
                    act.wait_ge(pe_done, P.after("l1"))
                    act.activation(logit1, by_batch(4, 2), ACT.Identity, bias=w("bb2_1")).then_inc(
                        act_done, A.step("l1"))
                    act.wait_ge(pe_done, P.after("gate"))
                    act.activation(gates, by_batch(6, 2), ACT.Sigmoid, bias=w("bg2")).then_inc(
                        act_done, A.step("gates"))
                    act.wait_ge(vec_done, V.after("diff"))
                    act.activation(w_pos, diff, ACT.Sigmoid).then_inc(act_done, A.step("w_pos"))
                    act.activation(w_kv, diff, ACT.Sigmoid, scale=-1.0).then_inc(act_done, A.step("w_kv"))
                    act.wait_ge(vec_done, V.after("angle"))
                    act.wait_ge(act_done, A.after("w_kv"))
                    act.activation(diff, angle, ACT.Abs).then_inc(act_done, A.step("abs_k"))
                    act.activation(sin_k, angle, ACT.Sin).then_inc(act_done, A.step("sin_k"))
                    act.wait_ge(act_done, A.after("abs_k"))
                    act.activation(cos_k, diff, ACT.Sin, bias=half_pi[:], scale=-1.0).then_inc(
                        act_done, A.step("cos_k"))
                    act.wait_ge(vec_done, V.after("gmax"))
                    act.activation(m3, m3, ACT.Sqrt).then_inc(act_done, A.step("sqrt"))
                    act.wait_ge(pe_done, P.after("turn"))
                    act.copy(a1, by_batch(0, 2)).then_inc(act_done, A.step("tokens"))
                    act.wait_ge(pe_done, P.after("lnT"))
                    act.activation(m0, by_batch(2, 2), ACT.Identity, bias=w("ln_b"), scale=w("ln_g")).then_inc(
                        act_done, A.step("ln"))

                @block.gpsimd
                def _(pool):
                    ln_pool(pool)
                    pool.wait_ge(loaded["L1"], 16)
                    add_bias(pool, w("bo"))
                    pool.wait_ge(pool_done, G.after("bias"))
                    pool.tensor_tensor(residual[:], residual[:], normed[:], ALU.add).then_inc(
                        pool_done, G.step("input"))
                    pool.wait_ge(vec_done, V.after("aggr2"))
                    pool.tensor_scalar(rstd[:], moments[:, :, 1], LN_EPS, None, ALU.add).then_inc(
                        pool_done, G.step("eps2"))
                    pool.wait_ge(pool_done, G.after("eps2"))
                    pool.tensor_tensor(rstd[:], rstd[:], minus_half[:], ALU.pow).then_inc(pool_done, G.step("rstd2"))

                @block.vector
                def _(vec):
                    tt, ts, stt = vec.tensor_tensor, vec.tensor_scalar, vec.scalar_tensor_tensor

                    ln_vector(vec, residual, normed)
                    vec.memset(carry, 1.0).then_inc(vec_done, V.step("const"))
                    vec.wait_ge(vec_done, V.after("const"))
                    vec.memset(carry[:, :, 0:1], 0.0).then_inc(vec_done, V.step("carry"))
                    vec.wait_ge(vec_done, V.after("carry"))

                    def scan(out, values, name):
                        vec.tensor_tensor_scan(flat(out), flat(carry), flat(values), 0.0, ALU.mult,
                                               ALU.add).then_inc(vec_done, V.step(name))

                    vec.wait_ge(act_done, A.after("pv"))
                    tt(a0, pv, over_batches(cos_p, B), ALU.mult).then_inc(vec_done, V.step("cv"))
                    vec.wait_ge(vec_done, V.after("cv"))
                    scan(m0, a0, "cm")
                    tt(a1, pv, over_batches(sin_p, B), ALU.mult).then_inc(vec_done, V.step("sv"))
                    vec.wait_ge(vec_done, V.after("sv"))
                    scan(m1, a1, "sm")
                    vec.wait_ge(vec_done, V.after("sm"))
                    tt(m0, m0, over_batches(cos_p, B), ALU.mult).then_inc(vec_done, V.step("pc"))
                    tt(m1, m1, over_batches(sin_p, B), ALU.mult).then_inc(vec_done, V.step("ps"))
                    vec.wait_ge(vec_done, V.after("ps"))
                    tt(pv, m0, m1, ALU.add).then_inc(vec_done, V.step("p"))
                    vec.wait_ge(act_done, A.after("keys"))
                    ts(angle, keys, PI, PI_BELOW, ALU.mult, ALU.min).then_inc(vec_done, V.step("k0"))
                    vec.wait_ge(vec_done, V.after("k0"))
                    ts(angle, angle, -PI_BELOW, None, ALU.max).then_inc(vec_done, V.step("angle"))
                    vec.wait_ge(act_done, A.after("l1"))
                    stt(out=diff, in0=by_batch(2, 2), scalar=w("bb2_0"), in1=logit1, op0=ALU.add,
                        op1=ALU.subtract).then_inc(vec_done, V.step("diff"))
                    vec.wait_ge(act_done, A.after("gates"))
                    scan(m2, gates, "g")
                    vec.wait_ge(vec_done, V.after("g"))
                    ts(m3, m2, 1.0, None, ALU.max).then_inc(vec_done, V.step("gmax"))
                    vec.wait_ge(act_done, A.after("cos_k"))
                    tt(kv, kv, gates, ALU.mult).then_inc(vec_done, V.step("vg"))
                    vec.wait_ge(vec_done, V.after("vg"))
                    vec.memset(a0[:, :, 0:1], 0.0)
                    vec.memset(a1[:, :, 0:1], 0.0)
                    tt(a0[:, :, 1:T], cos_k[:, :, 0:T - 1], kv[:, :, 1:T], ALU.mult).then_inc(vec_done, V.step("wc"))
                    vec.wait_ge(vec_done, V.after("wc"))
                    scan(m0, a0, "wm")
                    tt(a1[:, :, 1:T], sin_k[:, :, 0:T - 1], kv[:, :, 1:T], ALU.mult).then_inc(vec_done, V.step("ws"))
                    vec.wait_ge(vec_done, V.after("ws"))
                    scan(m1, a1, "wn")
                    vec.wait_ge(act_done, A.after("sqrt"))
                    vec.reciprocal(m2, m3).then_inc(vec_done, V.step("rec"))
                    tt(m0, m0, cos_k, ALU.mult).then_inc(vec_done, V.step("kc"))
                    vec.wait_ge(vec_done, V.after("wn"))
                    tt(m1, m1, sin_k, ALU.mult).then_inc(vec_done, V.step("ks"))
                    vec.wait_ge(vec_done, V.after("ks"))
                    tt(m0, m0, m1, ALU.add).then_inc(vec_done, V.step("k"))
                    vec.wait_ge(vec_done, V.after("k"))
                    tt(m0, m0, m2, ALU.mult).then_inc(vec_done, V.step("kn"))
                    tt(a0, pv, w_pos, ALU.mult).then_inc(vec_done, V.step("bp"))
                    vec.wait_ge(vec_done, V.after("bp"))
                    tt(a1, m0, w_kv, ALU.mult).then_inc(vec_done, V.step("bk"))
                    vec.wait_ge(vec_done, V.after("bk"))
                    tt(a0, a0, a1, ALU.add).then_inc(vec_done, V.step("b"))
                    vec.wait_ge(vec_done, V.after("b"))
                    ts(a0, a0, float(D) ** -0.5, None, ALU.mult).then_inc(vec_done, V.step("scaled"))
                    vec.wait_ge(act_done, A.after("tokens"))
                    for b in range(B):
                        last = vec.bn_stats(stats[:, b], a1[:, b])
                    last.then_inc(vec_done, V.step("stats2"))
                    vec.wait_ge(vec_done, V.after("stats2"))
                    for b in range(B):
                        last = vec.bn_aggr(moments[:, b], stats[:, b])
                    last.then_inc(vec_done, V.step("aggr2"))
                    vec.wait_ge(pool_done, G.after("rstd2"))
                    for h in range(2):
                        for b in range(HB * h, HB * h + HB):
                            last = ts(a1[:, b], a1[:, b], moments[:, b, 0:1], rstd[:, b:b + 1], ALU.subtract,
                                      ALU.mult)
                        last.then_inc(vec_done, V.step(f"xn{h}2"))
                    vec.wait_ge(pe_done, P.after("out"))
                    for h in range(2):
                        tt(half(residual, h), half(residual, h), by_batch(4 + h), ALU.add).then_inc(
                            vec_done, V.step(f"r{h}"))

        stage(phase_memory)
        stage(lambda: cross("L1"))

        def quantised_ffn(pack, gated):
            w = lambda name: W(pack, name)
            hidden = scratch[:, 0:4].rearrange("p a b c -> p (a b c)").rearrange("p (b f) -> p b f", f=FF)
            squares = scratch[:, 4:8].rearrange("p a b c -> p (a b c)").rearrange("p (b f) -> p b f", f=FF)
            scaled = S(8)
            xq = S(9).bitcast(BF16)[:, :, 0:D]
            xqT = S(9).bitcast(BF16)[:, :, D:2 * D]
            up_q, down_q = ternary[pack][:, 0], ternary[pack][:, 1]
            gate_q = ternary[pack][:, 2] if gated else None
            up_scale, down_scale, gate_scale = (weight_scales[:, j:j + 1] for j in ((2, 3, 4) if gated else (0, 1, 0)))
            hq = probs.bitcast(BF16).rearrange("p h k -> p (h k)").rearrange("p (b f) -> p b f", f=FF)
            hqT = probsT[:].bitcast(BF16).rearrange("p h k -> p (h k)").rearrange("p (b f) -> p b f", f=FF)
            up_in = shifted.rearrange("p h k -> p (h k)").rearrange("p (s f) -> p s f", f=FF)
            amax, inv, tok, up_s, gate_s = (small[:, 3 + j] for j in range(5))
            amax2, inv2, tok2 = (small[:, 8 + j] for j in range(3))
            last_b = B - 1
            up_at = lambda b: 2 * (b % 4) if gated else b
            plan(pe=["xqT", *[f"u{b}" for b in range(B)], *[f"hT{b}" for b in range(B)],
                     *[f"o{b}" for b in range(B)]],
                 act=["xqT", *[f"h{b}" for b in range(B)], "i0", *[x for b in range(1, B) for x in (f"i{b}", f"hT{b - 1}")],
                      f"hT{B - 1}"],
                 vec=[*LN["vec"], "amax", "aclip", "inv", "sx", "x1", "x2", "xq", "tok", "scales", "scales2",
                      *[f"s{b}" for b in range(B)],
                      *[x for h in range(2) for x in (
                          *[f"{c}{h}" for c in ("amax2", "aclip2", "inv2", "sx2")],
                          *[f"m{b}" for b in range(HB * h, HB * h + HB)])],
                      "tok2", "tok2w", *[f"r{b}" for b in range(B)]],
                 pool=[*LN["pool"], *([] if gated else ["bias"]),
                       *([f"t{b}" for b in range(B)] if gated else []), *[f"n{b}" for b in range(B)]])
            with nc.Block() as block:
                @block.vector
                def _(vec):
                    ts, stt = vec.tensor_scalar, vec.scalar_tensor_tensor

                    def chain(ins, name):
                        ins.then_inc(vec_done, V.step(name))
                        vec.wait_ge(vec_done, V.after(name))

                    vec.wait_ge(loaded[pack], 16)
                    ln_vector(vec, residual, normed)
                    vec.wait_ge(vec_done, V.after("xn1"))
                    chain(vec.tensor_reduce(amax, normed[:], AXIS_X, ALU.max, apply_absolute_value=True), "amax")
                    chain(ts(amax, amax, 1e-5, None, ALU.max), "aclip")
                    chain(vec.reciprocal(inv, amax), "inv")
                    chain(ts(inv, inv, 127.0, None, ALU.mult), "sx")
                    chain(vec.tensor_tensor(scaled, normed[:], inv.unsqueeze(2).broadcast_to([128, B, D]), ALU.mult), "x1")
                    chain(ts(scaled, scaled, 127.0, -128.0, ALU.min, ALU.max), "x2")
                    chain(ts(xq, scaled, ROUND, ROUND, ALU.add, ALU.subtract), "xq")
                    chain(ts(tok, amax, 1.0 / 127.0, None, ALU.mult), "tok")
                    chain(ts(up_s, tok, up_scale, None, ALU.mult), "scales")
                    chain(ts(gate_s, tok, gate_scale, None, ALU.mult), "scales2")
                    for b in range(B):
                        vec.wait_ge(pe_done, P.after(f"u{b}"))
                        if gated:
                            vec.wait_ge(act_done, A.after(f"h{b}"))
                            if b >= 2:
                                vec.wait_ge(pool_done, G.after(f"t{b - 2}"))
                            stt(out=up_in[:, b % 2], in0=bank(up_at(b)), scalar=up_s[:, b:b + 1],
                                in1=squares[:, b], op0=ALU.mult, op1=ALU.mult).then_inc(vec_done, V.step(f"s{b}"))
                        else:
                            stt(out=squares[:, b], in0=bank(up_at(b)), scalar=up_s[:, b:b + 1], in1=w("up_b"),
                                op0=ALU.mult, op1=ALU.add).then_inc(vec_done, V.step(f"s{b}"))
                    for h in range(2):
                        half_b = slice(HB * h, HB * h + HB)
                        if gated:
                            vec.wait_ge(pool_done, G.after(f"t{HB * h + HB - 1}"))
                        else:
                            vec.wait_ge(act_done, A.after(f"h{HB * h + HB - 1}"))
                        chain(vec.tensor_reduce(amax2[:, half_b], hidden[:, half_b], AXIS_X, ALU.max,
                                                apply_absolute_value=True), f"amax2{h}")
                        chain(ts(amax2[:, half_b], amax2[:, half_b], 1e-5, None, ALU.max), f"aclip2{h}")
                        chain(vec.reciprocal(inv2[:, half_b], amax2[:, half_b]), f"inv2{h}")
                        chain(ts(inv2[:, half_b], inv2[:, half_b], 127.0, None, ALU.mult), f"sx2{h}")
                        for b in range(HB * h, HB * h + HB):
                            ts(hidden[:, b], hidden[:, b], inv2[:, b:b + 1], 127.0, ALU.mult, ALU.min).then_inc(
                                vec_done, V.step(f"m{b}"))
                    chain(ts(tok2, amax2, 1.0 / 127.0, None, ALU.mult), "tok2")
                    chain(ts(tok2, tok2, down_scale, None, ALU.mult), "tok2w")
                    if not gated:
                        vec.wait_ge(pool_done, G.after("bias"))
                    for b in range(B):
                        vec.wait_ge(pe_done, P.after(f"o{b // HB * HB + HB - 1}"))
                        stt(out=residual[:, b], in0=by_batch(6, 2)[:, b], scalar=tok2[:, b:b + 1], in1=residual[:, b],
                            op0=ALU.mult, op1=ALU.add).then_inc(vec_done, V.step(f"r{b}"))

                @block.gpsimd
                def _(pool):
                    ln_pool(pool)
                    if not gated:
                        pool.wait_ge(loaded[pack], 16)
                        add_bias(pool, w("down_b"))
                    for b in range(B if gated else 0):
                        pool.wait_ge(vec_done, V.after(f"s{b}"))
                        pool.tensor_tensor(hidden[:, b], up_in[:, b % 2], squares[:, b], ALU.mult).then_inc(
                            pool_done, G.step(f"t{b}"))
                    for b in range(B):
                        pool.wait_ge(vec_done, V.after(f"m{b}"))
                        pool.tensor_scalar(hidden[:, b], hidden[:, b], -128.0, ROUND, ALU.max, ALU.add).then_inc(
                            pool_done, G.step(f"n{b}"))

                @block.tensor
                def _(pe):
                    pe.wait_ge(vec_done, V.after("xq"))
                    turned = psum[:, 0, :].bitcast(BF16).rearrange("p (b c) -> p b c", c=T)
                    for b in range(B):
                        last = pe.transpose(turned[:, b], xq[:, b], ident16[:])
                    last.then_inc(pe_done, P.step("xqT"))
                    pe.wait_ge(act_done, A.after("xqT"))
                    for b in range(B):
                        if gated:
                            if b >= 4:
                                pe.wait_ge(vec_done, V.after(f"s{b - 4}"))
                            pe.matmul(bank(up_at(b) + 1), xqT[:, b], gate_q, start=True, stop=True)
                        pe.matmul(bank(up_at(b)), xqT[:, b], up_q, start=True, stop=True).then_inc(
                            pe_done, P.step(f"u{b}"))
                    for b in range(B):
                        pe.wait_ge(act_done, A.after(f"i{b}"))
                        if b == 0:
                            pe.wait_ge(vec_done, V.after(f"s{last_b}"))
                        if b >= 2:
                            pe.wait_ge(act_done, A.after(f"hT{b - 2}"))
                        turned = psum[:, b % 2, 0:256].bitcast(BF16).rearrange("p (c k) -> p c k", k=T)
                        for c in range(4):
                            last = pe.transpose(turned[:, c], hq[:, b, c * 128:(c + 1) * 128], ident16[:])
                        last.then_inc(pe_done, P.step(f"hT{b}"))
                    for b in range(B):
                        pe.wait_ge(act_done, A.after(f"hT{b}"))
                        for c in range(4):
                            last = pe.matmul(by_batch(6, 2)[:, b], hqT[:, b, c * 128:(c + 1) * 128],
                                             down_q[:, c * 128:(c + 1) * 128], start=c == 0, stop=c == 3)
                        last.then_inc(pe_done, P.step(f"o{b}"))

                @block.scalar
                def _(act):
                    act.wait_ge(pe_done, P.after("xqT"))
                    act.copy(xqT, psum[:, 0, :].bitcast(BF16).rearrange("p (b c) -> p b c", c=T)).then_inc(
                        act_done, A.step("xqT"))
                    for b in range(B):
                        if gated:
                            act.wait_ge(pe_done, P.after(f"u{b}"))
                            act.wait_ge(vec_done, V.after("scales2"))
                            last = act.activation(squares[:, b], bank(up_at(b) + 1), ACT.Relu,
                                                  scale=gate_s[:, b:b + 1])
                        else:
                            act.wait_ge(vec_done, V.after(f"s{b}"))
                            last = act.activation(hidden[:, b], squares[:, b], ACT.Gelu)
                        last.then_inc(act_done, A.step(f"h{b}"))

                    def copy(b):
                        act.wait_ge(pe_done, P.after(f"hT{b}"))
                        act.copy(hqT[:, b], psum[:, b % 2, 0:256].bitcast(BF16)).then_inc(act_done, A.step(f"hT{b}"))

                    for b in range(B):
                        act.wait_ge(pool_done, G.after(f"n{b}"))
                        act.activation(hq[:, b], hidden[:, b], ACT.Identity, bias=minus_round[:]).then_inc(
                            act_done, A.step(f"i{b}"))
                        if b:
                            copy(b - 1)
                    copy(B - 1)

        stage(lambda: quantised_ffn("L1", False))

        def recurrence():
            chunk = 512 // B
            banks_used = T // chunk
            states = S(0).rearrange("p b t -> p (b t)").rearrange("p (t b) -> p t b", b=B)
            plan(pe=[*LN["pe"], "inputs", "hT"], act=[*LN["act"]], vec=[*LN["vec"], *ternary_steps("L3"), "r"], pool=[*LN["pool"]])
            with nc.Block() as block:
                @block.vector
                def _(vec):
                    ln_vector(vec, residual, normed)
                    make_ternary(vec, "L3", flat(S(1)[:, 0:HB]))
                    vec.wait_ge(pe_done, P.after("hT"))
                    vec.tensor_tensor(residual[:], residual[:], by_batch(0, 2), ALU.add).then_inc(
                        vec_done, V.step("r"))

                @block.gpsimd
                def _(pool):
                    ln_pool(pool)

                @block.tensor
                def _(pe):
                    ln_tensor(pe)
                    pe.wait_ge(loaded["L2"], 16)
                    pe.wait_ge(act_done, A.after("xnT1"))
                    by_step = normedT.rearrange("p b t -> p t b")

                    def from_inputs(start, steps):
                        return pe.matmul(banks(2, banks_used)[:, start * B:(start + steps) * B], W("L2", "wi"),
                                         by_step[:, start:start + steps], start=True, stop=False,
                                         skip_group_check=True)

                    def from_biases(start, steps):
                        return pe.matmul(banks(2, banks_used)[:, start * B:(start + steps) * B],
                                         W("L2", "ih_b", rows=slice(0, 2)),
                                         ones[0:2, 0:B].unsqueeze(1).broadcast_to([2, steps, B]), start=False,
                                         stop=True, skip_group_check=True)

                    from_inputs(0, chunk)
                    from_biases(0, chunk).then_inc(pe_done, P.step("inputs"))

                    def step(t):
                        pe.wait_ge(state_made, t)
                        pe.matmul(banks(2, 2)[:, t * B:(t + 1) * B], W("L2", "wh"), states[:, t - 1],
                                  start=False, stop=True, skip_group_check=True).then_inc(sum_made, 1)

                    for t in range(1, T):
                        step(t)
                        start = (t // chunk + 1) * chunk
                        if start < T and t % chunk in (8, 16):
                            (from_inputs if t % chunk == 8 else from_biases)(start, chunk)
                    pe.wait_ge(state_made, T)
                    for b in range(B):
                        last = pe.transpose(by_batch(0, 2)[:, b], states[:, :, b], ident)
                    last.then_inc(pe_done, P.step("hT"))

                @block.scalar
                def _(act):
                    ln_scalar(act)
                    act.preload_act_table(ACT.Tanh)
                    act.wait_ge(pe_done, P.after("inputs"))

                    def step(t):
                        if t:
                            act.wait_ge(sum_made, t)
                        act.activation(states[:, t], banks(2, 2)[:, t * B:(t + 1) * B],
                                       ACT.Tanh).then_inc(state_made, 1)

                    for t in range(T):
                        step(t)

        stage(recurrence)

        stage(lambda: (
            stacked_prologue("L2", W("L2", "xq"), W("L2", "xk")),
            stacked_attention(D ** -0.5, values=mean_values),
            attention_out(W("L2", "xo"), gem=(peaks, p_inv, W("L0", "shift")))))

        def experts_ffn():
            rows = PARTS * EXPERTS
            weight_of = S(0).bitcast(BF16)[0:rows, 0:HB].rearrange("p b t -> p (b t)").rearrange(
                "p (b t) -> p b t", b=B)
            pick16 = flat(S(0).bitcast(BF16)[0:rows, HB:B])
            parts = flat(S(13)[:, 3:4]).bitcast(BF16)[:, 0:B * rows].rearrange("p (b m e) -> p b m e", b=B, m=PARTS)
            units = scratch[:, 1:3]
            sig = [S(3 + j)[:, 0:HB] for j in range(3)]
            gated = [S(6 + j)[:, 0:HB] for j in range(3)]
            part = [S(9 + j)[:, 0:HB] for j in range(3)]
            order = [(e, h, c) for e in range(EXPERTS) for h in range(2) for c in range(2)]
            row = lambda j: S(12)[:, j, 0:B * EXPERTS].rearrange("p (b e) -> p b e", e=EXPERTS)
            score, best1, best2, rank, less = (row(j) for j in range(5))
            one1, one2, weight = (S(13)[:, j, 0:B * EXPERTS].rearrange("p (b e) -> p b e", e=EXPERTS)
                                  for j in range(3))
            top, total, top1, top2, peak, denom, rec = (small[:, j] for j in range(7))
            wide = lambda col: col.unsqueeze(2).broadcast_to([128, B, EXPERTS])
            priority = over_batches(W("C", "priority"), B)
            gates = ["top", "less", "sum", "rec", "score", "m1", "e1", "rank1", "pr1", "one1", "s2", "m2", "e2",
                     "rank2", "pr2", "one2", "den", "deneps", "denrec", "w1", "w2", "w", "wn", "high", "rest", "mid", "low", "share"]
            plan(pe=[*LN["pe"], "gate", "h0", "h1", "h2", "wT", "c0", "c2",
                     *[f"{x}{u}" for u in range(3, len(order)) for x in (["c", "h"] if u % 2 == 0 else ["h"])],
                     "out0", "out1"],
                 act=[*LN["act"], "exp", "s0", "s1", "s2", "wT", *[f"s{u}" for u in range(3, len(order))]],
                 vec=[*LN["vec"], *gates, *[f"{x}{u}" for u in range(len(order)) for x in "gp"],
                      *[f"b{b}" for b in range(B)], "r0", "r1"],
                 pool=[*LN["pool"], "pick", *[f"a{u}" for u in range(4, len(order))]])
            with nc.Block() as block:
                @block.vector
                def _(vec):
                    tt, ts, stt = vec.tensor_tensor, vec.tensor_scalar, vec.scalar_tensor_tensor

                    def chain(ins, name):
                        ins.then_inc(vec_done, V.step(name))
                        vec.wait_ge(vec_done, V.after(name))

                    ln_vector(vec, residual, normed)
                    logits = bank(7, B * EXPERTS).rearrange("p (b e) -> p b e", e=EXPERTS)
                    vec.wait_ge(pe_done, P.after("gate"))
                    chain(vec.tensor_reduce(top, logits, AXIS_X, ALU.max), "top")
                    chain(tt(less, logits, wide(top), ALU.subtract), "less")
                    vec.wait_ge(act_done, A.after("exp"))
                    chain(vec.tensor_reduce(total, score, AXIS_X, ALU.add), "sum")
                    chain(vec.reciprocal(rec, total), "rec")
                    chain(tt(score, score, wide(rec), ALU.mult), "score")
                    chain(vec.tensor_reduce(top1, score, AXIS_X, ALU.max), "m1")
                    chain(tt(best1, score, wide(top1), ALU.is_equal), "e1")
                    chain(tt(rank, best1, priority, ALU.mult), "rank1")
                    chain(vec.tensor_reduce(peak, rank, AXIS_X, ALU.max), "pr1")
                    chain(tt(one1, rank, wide(peak), ALU.is_equal), "one1")
                    chain(stt(out=less, in0=one1, scalar=-2.0, in1=score, op0=ALU.mult, op1=ALU.add), "s2")
                    chain(vec.tensor_reduce(top2, less, AXIS_X, ALU.max), "m2")
                    chain(tt(best2, less, wide(top2), ALU.is_equal), "e2")
                    chain(tt(rank, best2, priority, ALU.mult), "rank2")
                    chain(vec.tensor_reduce(peak, rank, AXIS_X, ALU.max), "pr2")
                    chain(tt(one2, rank, wide(peak), ALU.is_equal), "one2")
                    chain(tt(denom, top1, top2, ALU.add), "den")
                    chain(ts(total, denom, 1e-9, None, ALU.add), "deneps")
                    chain(vec.reciprocal(rec, total), "denrec")
                    chain(tt(one1, one1, wide(top1), ALU.mult), "w1")
                    chain(tt(one2, one2, wide(top2), ALU.mult), "w2")
                    chain(tt(weight, one1, one2, ALU.add), "w")
                    chain(tt(weight, weight, wide(rec), ALU.mult), "wn")
                    chain(vec.tensor_copy(parts[:, :, 0], weight), "high")
                    chain(tt(weight, weight, parts[:, :, 0], ALU.subtract), "rest")
                    chain(vec.tensor_copy(parts[:, :, 1], weight), "mid")
                    tt(parts[:, :, 2], weight, parts[:, :, 1], ALU.subtract).then_inc(vec_done, V.step("low"))
                    tt(denom, denom, rec, ALU.mult).then_inc(vec_done, V.step("share"))
                    for u, (e, h, c) in enumerate(order):
                        pair = 2 * (u % 3)
                        vec.wait_ge(act_done, A.after(f"s{u}"))
                        if u >= 3:
                            vec.wait_ge(vec_done, V.after(f"p{u - 3}"))
                        bias = W("L2", "experts_b", 4 * e + c, 1)
                        stt(out=gated[u % 3], in0=by_batch(pair), scalar=bias, in1=sig[u % 3], op0=ALU.add,
                            op1=ALU.mult).then_inc(vec_done, V.step(f"g{u}"))
                        vec.wait_ge(vec_done, V.after(f"g{u}"))
                        if u - 3 >= 4:
                            vec.wait_ge(pool_done, G.after(f"a{u - 3}"))
                        target = half(units[:, c], h) if e == 0 else part[u % 3]
                        vec.wait_ge(pe_done, P.after(f"c{u - c}"))
                        tt(target, gated[u % 3], by_batch(6 + u // 2 % 2), ALU.mult).then_inc(
                            vec_done, V.step(f"p{u}"))
                    for b in range(B):
                        stt(out=residual[:, b], in0=W("L2", "bo"), scalar=denom[:, b:b + 1], in1=residual[:, b],
                            op0=ALU.mult, op1=ALU.add).then_inc(vec_done, V.step(f"b{b}"))
                    vec.wait_ge(vec_done, V.after(f"b{B - 1}"))
                    for h in range(2):
                        vec.wait_ge(pe_done, P.after(f"out{h}"))
                        tt(half(residual, h), half(residual, h), by_batch(h), ALU.add).then_inc(
                            vec_done, V.step(f"r{h}"))

                @block.gpsimd
                def _(pool):
                    ln_pool(pool)
                    pool.tensor_copy(pick16, W("C", "pick", rows=slice(0, rows))).then_inc(pool_done, G.step("pick"))
                    for u, (e, h, c) in enumerate(order):
                        if e == 0:
                            continue
                        total_at = half(units[:, c], h)
                        pool.wait_ge(vec_done, V.after(f"p{u}"))
                        if u >= 8:
                            pool.wait_ge(pool_done, G.after(f"a{u - 4}"))
                        pool.tensor_tensor(total_at, total_at, part[u % 3], ALU.add).then_inc(
                            pool_done, G.step(f"a{u}"))

                @block.tensor
                def _(pe):
                    ln_tensor(pe)
                    pe.wait_ge(act_done, A.after("xnT1"))
                    pe.wait_ge(loaded["L2"], 16)
                    for b in range(B):
                        last = pe.matmul(bank(7)[:, b * EXPERTS:(b + 1) * EXPERTS], normedT[:, b], W("L2", "wg"),
                                         start=True, stop=True)
                    last.then_inc(pe_done, P.step("gate"))

                    def hidden(u):
                        e, h, c = order[u]
                        if u >= 3:
                            pe.wait_ge(vec_done, V.after(f"g{u - 3}"))
                        for j in range(2):
                            at = e * 2 * EH + j * EH + c * 128
                            last = pe.matmul(bank(2 * (u % 3) + j), W("L2", "experts", at, 128), half(normedT, h),
                                             start=True, stop=True)
                        last.then_inc(pe_done, P.step(f"h{u}"))

                    def spread(u):
                        e, h, c = order[u]
                        if u >= 4:
                            pe.wait_ge(vec_done, V.after(f"p{u - 3}"))
                        pe.matmul(bank(6 + u // 2 % 2), pick16[:, e * 128:(e + 1) * 128], half(weight_of, h),
                                  start=True, stop=True).then_inc(pe_done, P.step(f"c{u}"))

                    for u in range(3):
                        hidden(u)
                    pe.wait_ge(vec_done, V.after("low"))
                    for b in range(B):
                        last = pe.matmul(by_batch(6, 2)[0:rows, b], parts[:, b].rearrange("p m e -> p (m e)"), ident16[:],
                                         start=True, stop=True)
                    last.then_inc(pe_done, P.step("wT"))
                    pe.wait_ge(act_done, A.after("wT"))
                    pe.wait_ge(pool_done, G.after("pick"))
                    spread(0)
                    spread(2)
                    for u in range(3, len(order)):
                        if u % 2 == 0:
                            spread(u)
                        hidden(u)
                    for h in range(2):
                        if h == 0:
                            pe.wait_ge(vec_done, V.after(f"g{len(order) - 1}"))
                            pe.wait_ge(pool_done, G.after(f"a{len(order) - 1}"))
                        for b in range(HB * h, HB * h + HB):
                            for c in range(2):
                                last = pe.matmul(by_batch(0, 2)[:, b], units[:, c, b], W("L2", "wo", c * D, D),
                                                 start=c == 0, stop=c == 1)
                        last.then_inc(pe_done, P.step(f"out{h}"))

                @block.scalar
                def _(act):
                    ln_scalar(act)
                    act.wait_ge(vec_done, V.after("less"))
                    act.activation(score, less, ACT.Exp).then_inc(act_done, A.step("exp"))

                    def sigmoid(u):
                        e, h, c = order[u]
                        act.wait_ge(pe_done, P.after(f"h{u}"))
                        if u >= 3:
                            act.wait_ge(vec_done, V.after(f"g{u - 3}"))
                        act.activation(sig[u % 3], by_batch(2 * (u % 3) + 1), ACT.Sigmoid,
                                       bias=W("L2", "experts_b", 4 * e + 2 + c, 1)).then_inc(
                            act_done, A.step(f"s{u}"))

                    for u in range(3):
                        sigmoid(u)
                    act.wait_ge(pe_done, P.after("wT"))
                    act.copy(weight_of, by_batch(6, 2)[0:rows]).then_inc(act_done, A.step("wT"))
                    for u in range(3, len(order)):
                        sigmoid(u)

        stage(experts_ffn)

        stage(lambda: (
            stacked_prologue("L3", W("L3", "sq"), W("L3", "sk"), wv=W("L3", "sv"), self_attention=True,
                             mask=W("L3", "sparse")),
            stacked_attention(HD ** -0.5, mask=True),
            attention_out(W("L3", "so"))))
        stage(lambda: cross("L3"))
        stage(lambda: quantised_ffn("L3", True))

        for f in stages[FIRST:STAGES]:
            f()

        with nc.Block() as block:
            @block.sync
            def _(sync):
                sync.dma_start(out_dram.rearrange("b t d -> t b d"), residual[:]).then_inc(stored, 16)
                sync.wait_ge(stored, 16)


STAGES = 12
FIRST = 0


def _columns(v, rows=128):
    return np.asarray(v).reshape(rows, 1)


def _rows(v):
    v = np.asarray(v).reshape(1, -1)
    return np.broadcast_to(v, (128, v.shape[1]))


def _stack(a):
    return a.reshape(-1, 128, a.shape[1]).transpose(1, 0, 2).reshape(128, -1)


def _latent_blocks(w):
    out = np.zeros((H, HD, GROUPS, 4, LAT), w.dtype)
    for h in range(H):
        out[h, :, h // 4, h % 4] = w.T
    return out.reshape(D, -1)


def _stacked(w):
    return np.swapaxes(w.reshape(*w.shape[:-1], H, HD), -2, -1).reshape(w.shape)


def _swap(w):
    return w.reshape(LAT // 2, 2, -1)[:, ::-1].reshape(w.shape)


def _pad(a, rows=128):
    return np.concatenate([a, np.zeros((rows - a.shape[0], a.shape[1]), a.dtype)])


def lay_out(i):
    f = np.float32
    pos = np.arange(T)
    freq = 1.0 / 10000.0 ** (np.arange(0, LAT, 2, dtype=f) / f(LAT))
    angle = np.outer(pos.astype(f), freq.astype(f)).astype(f)
    cos = np.tile(np.repeat(np.cos(angle), 2, axis=1).T, (4, 1)).astype(f)
    sign = np.tile(np.array([-1.0, 1.0], f), LAT // 2)[:, None]
    sin = np.tile(np.repeat(np.sin(angle), 2, axis=1).T * sign, (4, 1)).astype(f)
    l2o = np.zeros((4, LAT, GROUPS, H, HD), f)
    for h in range(H):
        l2o[h % 4, :, h // 4, h] = i["L0_attn_l2o_w"].T
    wqk = np.zeros((4, LAT, 4, LAT), f)
    for j in range(4):
        wqk[j, :, j] = i["L0_attn_wqk_w"].T
    per = INNER // 2

    def hinges(a):
        return a.reshape(M, 2, per).transpose(1, 0, 2).reshape(2 * M, per)

    rows, cols = pos[:, None], pos[None, :]
    causal = cols <= rows
    sparse = (causal & (cols >= rows - 31)) | (causal & ((rows - cols) % 64 == 0))
    start = 2.0 ** (-2.0 ** (-(4 - 3)))
    slopes = np.asarray([start * start ** n for n in range(H)], f)
    distance = -np.abs(rows - cols).astype(f)
    alibi = (slopes[None, :, None] * distance[:, None, :]).astype(f)

    def cross(p, q, k, v, o, turn):
        w = {n: (i[f"{p}_{m}"].T if turn else i[f"{p}_{m}"]) for n, m in (("xq", q), ("xk", k), ("xv", v), ("xo", o))}
        return {n: _stacked(a) if n in ("xq", "xk") else a for n, a in w.items()}

    L0 = {
        "qkv": i["L0_attn_c_attn_w"].T, "q_lat": _latent_blocks(i["L0_attn_q2l_w"]),
        "q_swap": _latent_blocks(_swap(i["L0_attn_q2l_w"])), "kv_lat": _latent_blocks(i["L0_attn_kv2l_w"]),
        "k_swap": _latent_blocks(_swap(i["L0_attn_kv2l_w"])), "l2o": l2o.reshape(128, -1), "wqk": wqk.reshape(128, 128),
        "cproj": i["L0_attn_cproj_w"].T, "qkv_b": i["L0_attn_c_attn_b"].reshape(3, D).T,
        "q_lat_b": _columns(np.tile(i["L0_attn_q2l_b"], 4)), "q_swap_b": _columns(np.tile(_swap(i["L0_attn_q2l_b"]), 4)),
        "kv_lat_b": _columns(np.tile(i["L0_attn_kv2l_b"], 4)),
        "k_swap_b": _columns(np.tile(_swap(i["L0_attn_kv2l_b"]), 4)),
        "wqk_b": _columns(np.tile(i["L0_attn_wqk_b"], 4)), "l2o_b": _columns(np.tile(i["L0_attn_l2o_b"], H)),
        "cproj_b": _rows(i["L0_attn_cproj_b"]), "cos": cos, "sin": sin,
        "causal": np.where(causal, 0.0, MASKED).astype(f),
        **cross("L0_xattn", "wq_w", "wk_w", "wv_w", "wo_w", True),
        "xq_b": _columns(_stacked(i["L0_xattn_wq_b"])), "xk_b": _columns(_stacked(i["L0_xattn_wk_b"])), "xv_b": _rows(i["L0_xattn_wv_b"]),
        "xo_b": _rows(i["L0_xattn_wo_b"]),
        "win": np.tile(i["L0_ffn_Win"], (1, 2)), "wout": np.tile(i["L0_ffn_Wout"], (2, 1)),
        "bin": _columns(np.tile(i["L0_ffn_bin_"], 2)), "w1": hinges(i["L0_ffn_W1"]), "b1": hinges(i["L0_ffn_b1"]),
        "w2": hinges(i["L0_ffn_W2"]), "b2": _pad(_columns(i["L0_ffn_b2"], M)), "bout": _rows(i["L0_ffn_bout"]),
        "mean_v": i["L2_xattn_WV"].T, "p": _columns(i["L2_xattn_p_param"]), "shift": _columns(i["L2_xattn_shift"]),
    }
    L1 = {
        "phases": i["L1_attn_pos_phases"][:T].T, "wpv": i["L1_attn_Wpv"], "wk": i["L1_attn_Wk"],
        "wkv": i["L1_attn_Wkv"], "wg1": i["L1_attn_Wg1"][:D], "wg1_shift": i["L1_attn_Wg1"][D:],
        "wg2": np.tile(i["L1_attn_Wg2"], (1, D)), "wb1": i["L1_attn_Wb1"],
        "wb2_0": _pad(np.tile(i["L1_attn_Wb2"][:, 0:1], (1, D))), "wb2_1": _pad(np.tile(i["L1_attn_Wb2"][:, 1:2], (1, D))),
        "wo": i["L1_attn_Wo"], "bpv": _columns(i["L1_attn_bpv"]), "bk": _columns(i["L1_attn_bk"]),
        "bkv": _columns(i["L1_attn_bkv"]), "bg1": _columns(i["L1_attn_bg1"]), "bg2": _rows(i["L1_attn_bg2"]),
        "bb1": _pad(_columns(i["L1_attn_bb1"], 64)), "bb2_0": _rows(i["L1_attn_bb2"][0:1]),
        "bb2_1": _rows(i["L1_attn_bb2"][1:2]), "ln_g": _columns(i["L1_attn_ln_g"]), "ln_b": _columns(i["L1_attn_ln_b"]),
        "bo": _rows(i["L1_attn_bo"]), **cross("L1_xattn", "wq", "wk", "wv", "wo", True),
        "xq_b": _columns(_stacked(i["L1_xattn_bq"])), "xk_b": _columns(_stacked(i["L1_xattn_bk"])), "xv_b": _rows(i["L1_xattn_bv"]),
        "xo_b": _rows(i["L1_xattn_bo"]), "up": i["L1_ffn_W1"].T, "down": _stack(i["L1_ffn_W2"].T),
        "up_b": _rows(i["L1_ffn_b1"]), "down_b": _rows(i["L1_ffn_b2"]),
    }
    L2 = {
        "wi": i["L2_attn_Wi"].T, "wh": i["L2_attn_Wh"].T,
        "ih_b": _pad(np.stack([i["L2_attn_bi"], i["L2_attn_bh"]])),
        "xq": _stacked(i["L2_xattn_WQ"].T), "xk": _stacked(i["L2_xattn_WK"].T), "xo": i["L2_xattn_Wout"].T, "wg": i["L2_ffn_Wg"].T,
        "experts": i["L2_ffn_W1"].transpose(2, 0, 1).reshape(D, -1),
        "experts_b": i["L2_ffn_b1"].reshape(EXPERTS, 4, 128).transpose(2, 0, 1).reshape(128, -1),
        "wo": _stack(i["L2_ffn_Wo"].T), "bo": _rows(i["L2_ffn_bo"]),
    }
    L3 = {
        "sq": _stacked(i["L3_attn_Wq"].T), "sk": _stacked(i["L3_attn_Wk"].T), "sv": i["L3_attn_Wv"].T, "so": i["L3_attn_Wo"].T,
        "sparse": np.where(sparse, 0.0, MASKED).astype(f), **cross("L3_xattn", "Wq", "Wk", "Wv", "Wo", False),
        "xq_b": _columns(_stacked(i["L3_xattn_bq"])), "xk_b": _columns(_stacked(i["L3_xattn_bk"])), "xv_b": _rows(i["L3_xattn_bv"]),
        "xo_b": _rows(i["L3_xattn_bo"]), "alibi": alibi.reshape(T, -1),
        "gate": i["L3_ffn_w_gate"].T, "up": i["L3_ffn_w_up"].T, "down": _stack(i["L3_ffn_w_down"].T),
    }
    heads = np.arange(D)[:, None] // HD
    pick = np.zeros((128, EXPERTS, 128), f)
    for m in range(PARTS):
        pick[m * EXPERTS + np.arange(EXPERTS), np.arange(EXPERTS)] = 1.0
    minus_pick = np.zeros((128, H), f)
    minus_pick[:PARTS * H] = -np.tile(np.eye(H, dtype=f), (PARTS, 1))
    C = {
        "identity": np.eye(128, dtype=f), "head_mask": (heads == np.arange(H)).astype(f),
        "latent_mask": (np.arange(128)[:, None] // LAT == np.arange(GROUPS)).astype(f),
        "minus_pick": minus_pick,
        "pick": pick.reshape(128, -1), "priority": _rows(np.arange(EXPERTS, 0, -1).astype(f)),
    }
    packs = {}
    for name, parts in (("L0", L0), ("L1", L1), ("L2", L2), ("L3", L3), ("C", C)):
        assert all(parts[n].shape == (128, w) for n, w in COLUMNS[name]), [
            (n, parts[n].shape, w) for n, w in COLUMNS[name] if parts[n].shape != (128, w)]
        packs[name] = np.ascontiguousarray(np.concatenate([parts[n] for n, _ in COLUMNS[name]], axis=1))
    return packs


def kernel(**inputs):
    import concourse.bacc as bacc
    from concourse.bass_utils import run_bass_kernel_spmd

    inputs = {k: np.asarray(v) for k, v in inputs.items()}
    nc = bacc.Bacc("TRN2", target_bir_lowering=False, num_devices=1)
    packs = lay_out(inputs)
    arrays = {f"in_{p}": a for p, a in packs.items()}
    arrays["in_x"] = np.ascontiguousarray(inputs["x"])
    arrays["in_ctx"] = np.ascontiguousarray(inputs["ctx_1024"])
    drams = {n: nc.dram_tensor(n, a.shape, F32, kind="ExternalInput").ap() for n, a in arrays.items()}
    out = nc.dram_tensor("out_x", (B, T, D), F32, kind="ExternalOutput").ap()
    build(nc, {p: drams[f"in_{p}"] for p in packs}, drams["in_x"], drams["in_ctx"], out)
    result = run_bass_kernel_spmd(nc, [arrays], core_ids=[0])
    return result.results[0]["out_x"]
```

```python
from contextlib import ExitStack

import numpy as np

import concourse.bass as bass
from concourse import mybir

ALU = mybir.AluOpType
ACT = mybir.ActivationFunctionType
AXIS_X = mybir.AxisListType.X
F32 = mybir.dt.float32
BF16 = mybir.dt.bfloat16

B, T, D = 8, 128, 128
H, HD = 16, 8
HH = H // 2
LAT, GROUPS = 32, 4
HB = B // 2
FF = 512
M, INNER = 64, 16
EXPERTS, EH = 8, 256
LN_EPS = 1e-5
MASKED = -1e30
QUERY_PARTS = (0, 0, 1, 0, 2, 1)
KEY_PARTS = (0, 1, 0, 2, 0, 1)
TERMS, PARTS = 6, 3
ROUND = 12582912.0
PI = float(np.float32(np.pi))
PI_BELOW = float(np.nextafter(np.float32(np.pi), np.float32(0)))
LOG_LIFT = 60

COLUMNS = {
    "L0": [("qkv", 3 * D), ("q_lat", 4 * 128), ("q_swap", 4 * 128), ("kv_lat", 4 * 128), ("k_swap", 4 * 128),
           ("l2o", 4 * 128), ("wqk", 128), ("cproj", D), ("qkv_b", 3), ("q_lat_b", 1), ("q_swap_b", 1),
           ("kv_lat_b", 1), ("k_swap_b", 1), ("wqk_b", 1), ("l2o_b", 1), ("cproj_b", D),
           ("cos", T), ("sin", T), ("causal", T),
           ("xq", D), ("xk", D), ("xv", D), ("xo", D), ("xq_b", 1), ("xk_b", 1), ("xv_b", D), ("xo_b", D),
           ("win", 128), ("wout", D), ("bin", 1), ("w1", 8), ("b1", 8), ("w2", 8), ("b2", 1), ("bout", D),
           ("mean_v", D), ("p", 1), ("shift", 1)],
    "L1": [("phases", T), ("wpv", D), ("wk", D), ("wkv", D), ("wg1", D), ("wg1_shift", D), ("wg2", D),
           ("wb1", 64), ("wb2_0", D), ("wb2_1", D), ("wo", D), ("bpv", 1), ("bk", 1), ("bkv", 1), ("bg1", 1),
           ("bg2", 1), ("bb1", 1), ("bb2_0", 1), ("bb2_1", 1), ("ln_g", 1), ("ln_b", 1), ("bo", D),
           ("xq", D), ("xk", D), ("xv", D), ("xo", D), ("xq_b", 1), ("xk_b", 1), ("xv_b", D), ("xo_b", D),
           ("up", FF), ("down", FF), ("up_b", FF), ("down_b", D)],
    "L2": [("wi", D), ("wh", D), ("ih_b", D), ("xq", D), ("xk", D), ("xo", D),
           ("wg", EXPERTS), ("experts", EXPERTS * 2 * EH), ("experts_b", EXPERTS * 4), ("wo", 2 * D), ("bo", D)],
    "L3": [("sq", D), ("sk", D), ("sv", D), ("so", D), ("sparse", T),
           ("xq", D), ("xk", D), ("xv", D), ("xo", D), ("xq_b", 1), ("xk_b", 1), ("xv_b", D), ("xo_b", D),
           ("alibi", H * T), ("gate", FF), ("up", FF), ("down", FF)],
    "C": [("identity", 128), ("latent_mask", GROUPS), ("minus_pick", H), ("pick", EXPERTS * 128),
          ("priority", EXPERTS)],
}
WIDTH = {pack: sum(w for _, w in parts) for pack, parts in COLUMNS.items()}


class Steps:

    def __init__(self):
        self.base, self.names, self.n = 0, [], 0

    def plan(self, *names):
        assert self.n == len(self.names), self.names[self.n:]
        self.base += self.n
        self.names, self.n = [x for name in names for x in ([name] if isinstance(name, str) else name)], 0

    def step(self, name):
        assert self.names[self.n] == name, (self.names[self.n], name)
        self.n += 1
        return 1

    def after(self, name):
        return self.base + self.names.index(name) + 1


def batches(engine, first, last):
    yield first
    with engine.Fori(first + 1, last) as b:
        yield b


def build(nc, packs, x_dram, ctx_dram, out_dram):
    with ExitStack() as ctx:
        def sb(name, shape, dt=F32):
            return ctx.enter_context(nc.sbuf_tensor(name, shape, dt))

        def sem(name):
            return ctx.enter_context(nc.semaphore(name))

        weights = {p: sb(f"weights_{p}", [128, WIDTH[p]]) for p in COLUMNS}
        where = {}
        for p, parts in COLUMNS.items():
            at = 0
            for name, w in parts:
                where[p, name] = (at, w)
                at += w

        def W(pack, name, start=0, width=None, rows=slice(0, 128)):
            at, w = where[pack, name]
            return weights[pack][rows, at + start:at + start + (w - start if width is None else width)]

        def over_batches(table, n):
            return table.unsqueeze(1).broadcast_to([128, n, table.shape[1]])

        residual = sb("residual", [128, B, D])
        normed = sb("normed", [128, B, D])
        normedT_padded = sb("normedT_padded", [128, B, T + 1])
        normedT = normedT_padded[:, :, 1:T + 1]
        contextT = sb("contextT", [128, B, T])
        stats = sb("stats", [128, B, 6])
        moments = sb("moments", [128, B, 2])
        rstd = sb("rstd", [128, B])
        ln_eps = sb("ln_eps", [128, 1])
        ones = sb("ones", [128, 128])
        values = sb("values", [128, B, H, HD + 1])
        mean_values = sb("mean_values", [128, B, H, HD + 1])
        position_waves = sb("position_waves", [128, 2, T])
        ternary = {"L1": sb("ternary_L1", [128, 2, FF], BF16), "L3": sb("ternary_L3", [128, 3, FF], BF16)}
        weight_scales = sb("weight_scales", [128, 8])
        weight_inverses = sb("weight_inverses", [128, 8])
        minus_pick_space = sb("minus_pick", [128, H, T], BF16)
        qT = minus_pick_space[:].rearrange("p h t -> p (h t)").bitcast(F32)[:, 0:GROUPS * T].rearrange(
            "p (g t) -> p g t", g=GROUPS)
        probsT = sb("probsT", [128, H, T])
        row_max = sb("row_max", [128, H])
        row_rec = sb("row_rec", [128, H])
        small_sums = sb("small_sums", [128, 2, T])
        row_rest = sb("row_rest", [128, H])
        peak_parts = sb("peak_parts", [128, PARTS * H], BF16)
        peakT = sb("peakT", [128, T], BF16)
        mask16 = sb("mask16", [128, T], BF16)
        small = sb("small", [128, 24, 8])
        half_pi = sb("half_pi", [128, 1])
        minus_round = sb("minus_round", [128, 1])
        ident16 = sb("ident16", [128, 128], BF16)
        scratch = sb("scratch", [128, 20, B, T])
        k_heads, shifted, probs = (scratch[:, j:j + 2].rearrange("p a b t -> p (a b) t") for j in (14, 16, 18))
        resultsT = scratch[:, 0]
        psum = ctx.enter_context(nc.psum_tensor("psum", [128, 8, 512], F32))

        ident = W("C", "identity")

        pe_done, act_done, vec_done, pool_done = (sem(x) for x in ("pe_done", "act_done", "vec_done", "pool_done"))
        P, A, V, G = Steps(), Steps(), Steps(), Steps()
        (qk_made, q_ready, k_ready, scores_made, half_shifted, half_exp, half_turned, half_copied, half_weighed,
         ctx_made, max_made, rec_made, biased_made) = (sem(x) for x in (
             "qk_made", "q_ready", "k_ready", "scores_made", "half_shifted", "half_exp", "half_turned", "half_copied",
             "half_weighed", "ctx_made", "max_made", "rec_made", "biased_made"))
        (quarter_made, quarter_max, part_made, peaks_split, peaks_turned, peaks_ready, turned_made,
         turned_biased, half_probs, half_summed, sums_inverted, results_made, half_padded, sums_taken,
         sums_turned, pads_cleared) = (sem(x) for x in (
             "quarter_made", "quarter_max", "part_made", "peaks_split", "peaks_turned", "peaks_ready",
             "turned_made", "turned_biased", "half_probs", "half_summed", "sums_inverted", "results_made",
             "half_padded", "sums_taken", "sums_turned", "pads_cleared"))
        queries_stacked, keys_stacked = sem("queries_stacked"), sem("keys_stacked")
        state_made, sum_made = sem("state_made"), sem("sum_made")
        loaded = {name: sem(f"loaded_{name}") for name in ("C", "x", "ctx", "L0", "L1", "L2", "L3")}
        stored = sem("stored")

        output = {"next": None, "here": None}

        def plan(pe=(), act=(), vec=(), pool=()):
            output["here"], output["next"] = output["next"], None
            if output["here"] is not None:
                gem = output["here"]["gem"] is not None
                pe = ["ctxT0", "ctxT1", "proj0", "proj1", *pe]
                act = [*(["log0", "log1"] if gem else []), "ctx0", "ctx1", *act]
                vec = [*(["lifted0", "lifted1", "unshifted0", "unshifted1"] if gem else []), "added0", "added1", *vec]
            P.plan(*pe), A.plan(*act), V.plan(*vec), G.plan(*pool)

        def bank(n, width=512, rows=128):
            return psum[0:rows, n, 0:width]

        def banks(n, m):
            return psum[:, n:n + m, :].rearrange("p k c -> p (k c)")

        def by_batch(n, m=1):
            return psum[:, n:n + m, :].rearrange("p k (b c) -> p (k b) c", c=128)

        def S(i):
            return scratch[:, i]

        def flat(ap):
            return ap.rearrange("p b c -> p (b c)")

        def flat_all(ap):
            return ap.rearrange("p a b c -> p (a b c)")

        plan(pe=["ctxT0", "ctxT1"], act=["ctx0", "ctx1"], vec=["const"])
        with nc.Block() as block:
            @block.sync
            def _(sync):
                sync.dma_start(weights["C"][:], packs["C"]).then_inc(loaded["C"], 16)
                sync.dma_start(residual[:], x_dram.rearrange("b t d -> t b d")).then_inc(loaded["x"], 16)
                sync.dma_start(S(0), ctx_dram.rearrange("b t d -> t b d")).then_inc(loaded["ctx"], 16)
                for p in ("L0", "L1", "L2", "L3"):
                    sync.dma_start(weights[p][:], packs[p]).then_inc(loaded[p], 16)

            @block.vector
            def _(vec):
                vec.memset(ones[:], 1.0)
                vec.memset(values[:], 1.0)
                vec.memset(mean_values[:], 1.0)
                vec.memset(ln_eps[:], LN_EPS)
                vec.memset(half_pi[:], float(np.pi / 2))
                vec.memset(minus_round[:], -ROUND)
                vec.wait_ge(loaded["C"], 16)
                vec.tensor_copy(ident16[:], ident)
                vec.memset(normedT_padded[:, :, 0:1], 0.0).then_inc(vec_done, V.step("const"))

            @block.tensor
            def _(pe):
                pe.wait_ge(loaded["C"], 16)
                pe.wait_ge(loaded["ctx"], 16)
                for h in range(2):
                    for i in range(HB):
                        last = pe.transpose(by_batch(h)[:, i], S(0)[:, HB * h + i], ident)
                    last.then_inc(pe_done, P.step(f"ctxT{h}"))

            @block.scalar
            def _(act):
                for h in range(2):
                    act.wait_ge(pe_done, P.after(f"ctxT{h}"))
                    act.copy(contextT[:, HB * h:HB * h + HB], by_batch(h)).then_inc(act_done, A.step(f"ctx{h}"))

        def attention_out(wo, bias=None, gem=None):
            output["next"] = {"wo": wo, "bias": bias, "gem": gem}

        def out_tensor(pe):
            if output["here"] is None:
                return
            for h in range(2):
                for i in range(HB):
                    last = pe.transpose(by_batch(h)[:, i], normed[:, HB * h + i], ident)
                last.then_inc(pe_done, P.step(f"ctxT{h}"))
            for h in range(2):
                if output["here"]["gem"] is None:
                    pe.wait_ge(act_done, A.after(f"ctx{h}"))
                else:
                    pe.wait_ge(vec_done, V.after(f"unshifted{h}"))
                for i in range(HB):
                    last = pe.matmul(by_batch(2 + h)[:, i], resultsT[:, HB * h + i], output["here"]["wo"], start=True,
                                     stop=True)
                last.then_inc(pe_done, P.step(f"proj{h}"))

        def out_scalar(act):
            if output["here"] is None:
                return
            bias, gem = output["here"]["bias"], output["here"]["gem"]
            if gem is not None:
                for h in range(2):
                    act.wait_ge(pe_done, P.after(f"ctxT{h}"))
                    act.activation(half(resultsT, h), by_batch(h), ACT.Ln, scale=2.0 ** LOG_LIFT).then_inc(
                        act_done, A.step(f"log{h}"))
            for h in range(2):
                if gem is not None:
                    act.wait_ge(vec_done, V.after(f"lifted{h}"))
                    act.activation(half(resultsT, h), half(resultsT, h), ACT.Exp, scale=gem[1]).then_inc(
                        act_done, A.step(f"ctx{h}"))
                    continue
                act.wait_ge(pe_done, P.after(f"ctxT{h}"))
                if bias is None:
                    last = act.copy(half(resultsT, h), by_batch(h))
                else:
                    last = act.activation(half(resultsT, h), by_batch(h), ACT.Identity, bias=bias)
                last.then_inc(act_done, A.step(f"ctx{h}"))

        def out_vector_gem(vec):
            gem = output["here"]["gem"]
            for h in range(2):
                vec.wait_ge(act_done, A.after(f"log{h}"))
                vec.scalar_tensor_tensor(
                    out=half(resultsT, h), in0=half(resultsT, h), scalar=-LOG_LIFT * float(np.log(2.0)),
                    in1=gem[0][:, HB * h:HB * h + HB].unsqueeze(2).broadcast_to([128, HB, T]),
                    op0=ALU.add, op1=ALU.add).then_inc(vec_done, V.step(f"lifted{h}"))
            for h in range(2):
                vec.wait_ge(act_done, A.after(f"ctx{h}"))
                vec.tensor_scalar(half(resultsT, h), half(resultsT, h), gem[2], None, ALU.subtract).then_inc(
                    vec_done, V.step(f"unshifted{h}"))

        LN = dict(pe=["xT0", "xT1"], act=["root", "xnT0", "xnT1"], vec=["stats", "aggr", "rstd", "xn0", "xn1"])

        def ln_vector(vec, source, target, again=""):
            vec.wait_ge(loaded["x"], 16)
            attention_here = output["here"] is not None and not again
            if attention_here and output["here"]["gem"] is not None:
                out_vector_gem(vec)
            for h in range(2):
                if attention_here:
                    vec.wait_ge(pe_done, P.after(f"proj{h}"))
                    vec.tensor_tensor(half(residual, h), half(residual, h), by_batch(2 + h), ALU.add).then_inc(
                        vec_done, V.step(f"added{h}"))
                    vec.wait_ge(vec_done, V.after(f"added{h}"))
                for b in range(HB * h, HB * h + HB):
                    last = vec.bn_stats(stats[:, b], source[:, b])
            last.then_inc(vec_done, V.step("stats" + again))
            vec.wait_ge(vec_done, V.after("stats" + again))
            for b in range(B):
                last = vec.bn_aggr(moments[:, b], stats[:, b])
            last.then_inc(vec_done, V.step("aggr" + again))
            vec.wait_ge(act_done, A.after("root" + again))
            vec.reciprocal(rstd[:], rstd[:]).then_inc(vec_done, V.step("rstd" + again))
            vec.wait_ge(vec_done, V.after("rstd" + again))
            for h in range(2):
                for b in range(HB * h, HB * h + HB):
                    last = vec.tensor_scalar(target[:, b], source[:, b], moments[:, b, 0:1], rstd[:, b:b + 1],
                                             ALU.subtract, ALU.mult)
                last.then_inc(vec_done, V.step(f"xn{h}{again}"))

        def ln_root(act, again=""):
            if not again:
                out_scalar(act)
            act.preload_act_table(ACT.Sqrt)
            act.wait_ge(vec_done, V.after("aggr" + again))
            act.activation(rstd[:], moments[:, :, 1], ACT.Sqrt, bias=ln_eps[:]).then_inc(
                act_done, A.step("root" + again))

        def ln_tensor(pe):
            for h in range(2):
                pe.wait_ge(vec_done, V.after(f"xn{h}"))
                for i in range(HB):
                    last = pe.transpose(by_batch(h)[:, i], normed[:, HB * h + i], ident)
                last.then_inc(pe_done, P.step(f"xT{h}"))

        def ln_scalar(act):
            for h in range(2):
                act.wait_ge(pe_done, P.after(f"xT{h}"))
                act.copy(normedT[:, HB * h:HB * h + HB], by_batch(h)).then_inc(act_done, A.step(f"xnT{h}"))

        def add_bias(pool, bias):
            pool.wait_ge(vec_done, V.after("xn1"))
            pool.tensor_tensor(residual[:], residual[:], over_batches(bias, B), ALU.add).then_inc(
                pool_done, G.step("bias"))

        def half(ap, h):
            return ap[:, HB * h:HB * h + HB]

        ternary_weights = [("L1", "up"), ("L1", "down"), ("L3", "up"), ("L3", "down"), ("L3", "gate")]

        def ternary_steps(pack):
            return [f"w{m}{j}" for m, (p, _) in enumerate(ternary_weights) if p == pack for j in range(3)]

        def make_ternary(vec, pack, temp):
            for m, (p, name) in enumerate(ternary_weights):
                if p != pack:
                    continue
                target = ternary[pack][:, ("up", "down", "gate").index(name)]
                vec.tensor_scalar(temp, W(pack, name), weight_inverses[:, m:m + 1], ROUND, ALU.mult, ALU.add).then_inc(
                    vec_done, V.step(f"w{m}0"))
                vec.wait_ge(vec_done, V.after(f"w{m}0"))
                vec.tensor_scalar(temp, temp, ROUND, 1.0, ALU.subtract, ALU.min).then_inc(vec_done, V.step(f"w{m}1"))
                vec.wait_ge(vec_done, V.after(f"w{m}1"))
                vec.tensor_scalar(target, temp, -1.0, None, ALU.max).then_inc(vec_done, V.step(f"w{m}2"))
                vec.wait_ge(vec_done, V.after(f"w{m}2"))

        def heads_first(h):
            return by_batch(2 * h, 2)

        def latent_attention(scale, causal, q_rot, k_rot):
            ctx_all = normed

            with nc.Block() as block:
                @block.tensor
                def _(pe):
                    def project(b):
                        if not (isinstance(b, int) and b == 0):
                            pe.wait_ge(q_ready, b)
                        for g in range(GROUPS):
                            last = pe.matmul(bank(6)[:, g * T:(g + 1) * T], W("L0", "wqk"),
                                             q_rot[:, g, bass.ds(b, 1)], start=True, stop=True)
                        last.then_inc(qk_made, 1)

                    def scores(b, h):
                        pe.wait_ge(k_ready, 2 * b + h + 1)
                        if h == 0:
                            pe.wait_ge(q_ready, b + 1)
                        if not (isinstance(b, int) and b == 0):
                            pe.wait_ge(half_shifted, 2 * b + h - 1)
                        for g in range(2):
                            quad = 2 * h + g
                            last = pe.matmul(bank(quad), qT[:, quad],
                                             k_heads[:, 4 * quad:4 * quad + 4], start=True, stop=True)
                        last.then_inc(scores_made, 1)

                    def turn_and_weigh(turned=None, weighed=None):
                        if turned is not None:
                            b, h = turned
                            pe.wait_ge(half_exp, 2 * b + h + 1)
                            if not (isinstance(b, int) and b == 0 and h == 0):
                                pe.wait_ge(half_copied, 2 * b + h)
                        if weighed is not None:
                            b, h = weighed
                            if h == 0 and not (isinstance(b, int) and b == 0):
                                pe.wait_ge(ctx_made, b)
                            pe.wait_ge(half_copied, 2 * b + h + 1)
                        for i in range(HH):
                            if turned is not None:
                                last = pe.transpose(by_batch(4, 2)[:, i], probs[:, HH * turned[1] + i], ident)
                                if i == HH - 1:
                                    last.then_inc(half_turned, 1)
                            if weighed is not None:
                                head = HH * weighed[1] + i
                                last = pe.matmul(bank(7)[:, head * (HD + 1):(head + 1) * (HD + 1)], probsT[:, head],
                                                 values[:, bass.ds(weighed[0], 1), head], start=True, stop=True)
                                if i == HH - 1:
                                    last.then_inc(half_weighed, 1)

                    project(0)
                    scores(0, 0)
                    scores(0, 1)
                    project(1)
                    scores(1, 0)
                    turn_and_weigh((0, 0))
                    scores(1, 1)
                    project(2)
                    turn_and_weigh((0, 1), (0, 0))
                    for b in batches(pe, 2, B - 1):
                        scores(b, 0)
                        turn_and_weigh((b - 1, 0), (b - 2, 1))
                        scores(b, 1)
                        project(b + 1)
                        turn_and_weigh((b - 1, 1), (b - 1, 0))
                    scores(B - 1, 0)
                    turn_and_weigh((B - 2, 0), (B - 3, 1))
                    scores(B - 1, 1)
                    turn_and_weigh((B - 2, 1), (B - 2, 0))
                    turn_and_weigh((B - 1, 0), (B - 2, 1))
                    turn_and_weigh((B - 1, 1), (B - 1, 0))
                    turn_and_weigh(None, (B - 1, 1))

                @block.scalar
                def _(act):
                    act.preload_act_table(ACT.Exp)

                    def take(b):
                        act.wait_ge(qk_made, b + 1)
                        act.activation(flat(qT), bank(6), ACT.Identity, bias=W("L0", "wqk_b")).then_inc(q_ready, 1)

                    def exponential(b, h):
                        act.wait_ge(half_shifted, 2 * b + h + 1)
                        if not (isinstance(b, int) and b == 0):
                            act.wait_ge(half_turned, 2 * b + h - 1)
                        act.activation(flat(probs[:, HH * h:HH * h + HH]), flat(shifted[:, HH * h:HH * h + HH]),
                                       ACT.Exp).then_inc(half_exp, 1)

                    def copy(b, h):
                        act.wait_ge(half_turned, 2 * b + h + 1)
                        if not (isinstance(b, int) and b == 0):
                            act.wait_ge(half_weighed, 2 * b + h - 1)
                        act.copy(flat(probsT[:, HH * h:HH * h + HH]), banks(4, 2)).then_inc(half_copied, 1)

                    def batch(b, more):
                        exponential(b, 0)
                        copy(b, 0)
                        exponential(b, 1)
                        if more:
                            take(b + 2)
                        copy(b, 1)

                    take(0)
                    take(1)
                    for b in batches(act, 0, B - 2):
                        batch(b, True)
                    batch(B - 2, False)
                    batch(B - 1, False)

                @block.gpsimd
                def _(pool):
                    for b in batches(pool, 0, B):
                        for g in range(GROUPS):
                            if g % 2 == 0 and not (isinstance(b, int) and b == 0):
                                pool.wait_ge(scores_made, 2 * b + g // 2 - 1)
                            last = pool.tensor_tensor(
                                k_heads[:, 4 * g:4 * g + 4], k_rot[:, g, bass.ds(b, 1)].broadcast_to([128, 4, T]),
                                W("C", "latent_mask").unsqueeze(2).broadcast_to([128, 4, T]), ALU.mult)
                            if g % 2:
                                last.then_inc(k_ready, 1)

                @block.vector
                def _(vec):
                    def shift(b, h):
                        heads = slice(HH * h, HH * h + HH)
                        peak = row_max[:, heads].unsqueeze(2).broadcast_to([128, HH, T])
                        vec.wait_ge(scores_made, 2 * b + h + 1)
                        if not (isinstance(b, int) and b == 0):
                            vec.wait_ge(half_exp, 2 * b + h - 1)
                            vec.wait_ge(half_shifted, 2 * b + h - 1)
                        source = shifted[:, heads]
                        vec.scalar_tensor_tensor(out=source, in0=heads_first(h), scalar=scale,
                                                 in1=over_batches(causal, HH), op0=ALU.mult,
                                                 op1=ALU.add).then_inc(biased_made, 1)
                        vec.wait_ge(biased_made, 2 * b + h + 1)
                        vec.tensor_reduce(row_max[:, heads], source, AXIS_X, ALU.max).then_inc(max_made, 1)
                        vec.wait_ge(max_made, 2 * b + h + 1)
                        vec.tensor_tensor(shifted[:, heads], source, peak, ALU.subtract).then_inc(half_shifted, 1)

                    def normalise(b):
                        sums = bank(7)[:, 0:H * (HD + 1)].rearrange("p (h d) -> p h d", d=HD + 1)
                        vec.wait_ge(half_weighed, 2 * b + 2)
                        if not (isinstance(b, int) and b == 0):
                            vec.wait_ge(ctx_made, b)
                        vec.reciprocal(row_rec[:], sums[:, :, HD]).then_inc(rec_made, 1)
                        vec.wait_ge(rec_made, b + 1)
                        vec.tensor_tensor(ctx_all[:, bass.ds(b, 1)].rearrange("p b (h d) -> p (b h) d", d=HD),
                                          sums[:, :, 0:HD], row_rec[:].unsqueeze(2).broadcast_to([128, H, HD]),
                                          ALU.mult).then_inc(ctx_made, 1)

                    for b in range(2):
                        shift(b, 0)
                        shift(b, 1)
                    for b in batches(vec, 2, B):
                        shift(b, 0)
                        normalise(b - 2)
                        shift(b, 1)
                    normalise(B - 2)
                    normalise(B - 1)

        stacked_so_far = {"all": 0, "biased": 0}
        stack_rows = TERMS * HD
        peak_rows = PARTS * H
        query_stack, key_stack = (flat_all(scratch[:, 8 * j:8 * j + 8]).bitcast(BF16).rearrange(
            "p (h b t) -> p h b t", h=H, b=B) for j in range(2))
        query_parts, key_parts = (flat_all(scratch[:, 16:19]).bitcast(BF16)[
            :, PARTS * B * T * j:PARTS * B * T * (j + 1)].rearrange("p (m b t) -> p m b t", m=PARTS, b=B) for j in range(2))
        query_rest, key_rest = normed, S(19)
        minus_pick = minus_pick_space[0:peak_rows]
        WH = HH * (HD + 1)
        after_parts = flat_all(scratch[:, 18:20])
        padded = after_parts[:, 0:2 * HH * (WH + HD + 1)].rearrange("p (h c) -> p h c", h=2)
        sumsT = small_sums[0:WH]
        bias16 = flat(contextT[:]).bitcast(BF16)

        def stacked_attention(scale, values=values, mask=None, bias=None):
            first = B * stacked_so_far["all"]
            first_biased = B * stacked_so_far["biased"]
            stacked_so_far["all"] += 1
            stacked_so_far["biased"] += bias is not None
            ctx_all = normed

            def at_start(b, below=1):
                return isinstance(b, int) and b < below

            def of_head(stack, b, head):
                return stack[0:stack_rows, head, bass.ds(b, 1)]

            with nc.Block() as block:
                @block.tensor
                def _(pe):
                    def quarter(b, g):
                        if not (at_start(b) and g < 2):
                            pe.wait_ge(quarter_max, 4 * first + 4 * b + g - 1)
                        if mask is not None:
                            pe.matmul(by_batch(g % 2), ident16[:], over_batches(mask16[:], 4), start=True, stop=False)
                        if bias is not None:
                            pe.matmul(bank(g % 2), ident16[:], bias16[:, 4 * g * T:(4 * g + 4) * T], start=True,
                                      stop=False)
                        for i in range(4):
                            last = pe.matmul(by_batch(g % 2)[:, i], of_head(query_stack, b, 4 * g + i),
                                             of_head(key_stack, b, 4 * g + i), start=mask is None and bias is None,
                                             stop=i == 3 or (mask is None and bias is None))
                        last.then_inc(quarter_made, 1)

                    def turn_peaks(b):
                        pe.wait_ge(peaks_split, first + b + 1)
                        pe.matmul(bank(1, T, rows=peak_rows), peak_parts[:], ident16[:], start=True,
                                  stop=True).then_inc(peaks_turned, 1)

                    def turned(b, h):
                        if h == 0:
                            pe.wait_ge(peaks_ready, first + b + 1)
                        if not at_start(b):
                            pe.wait_ge(half_probs, 2 * first + 2 * b + h - 1)
                            if bias is not None:
                                pe.wait_ge(turned_biased, 2 * first_biased + 2 * b + h - 1)
                        for i in range(HH):
                            head, out = HH * h + i, by_batch(2 + 2 * h, 2)[:, i]
                            pe.matmul(out, of_head(key_stack, b, head), of_head(query_stack, b, head), start=True,
                                      stop=False)
                            if mask is not None:
                                pe.matmul(out, mask16[:], ident16[:], start=False, stop=False)
                            last = pe.matmul(out, minus_pick[:, head], peakT[0:peak_rows], start=False, stop=True)
                        last.then_inc(turned_made, 1)

                    def weigh(b, h, between=None):
                        if h == 0 and not at_start(b):
                            pe.wait_ge(sums_taken, first + b)
                        pe.wait_ge(half_padded, 2 * first + 2 * b + h + 1)
                        pe.wait_ge(half_probs, 2 * first + 2 * b + h + 1)
                        for i in range(HH):
                            if between is not None and i == 5:
                                turn_peaks(between)
                            last = pe.matmul(psum[0:WH, 6, h * T:(h + 1) * T], padded[:, h, i * WH:(i + 1) * WH],
                                             probsT[:, HH * h + i], start=i == 0, stop=i == HH - 1)
                        last.then_inc(half_summed, 1)

                    def turn_sums(b):
                        pe.wait_ge(sums_taken, first + b + 1)
                        if not at_start(b):
                            pe.wait_ge(results_made, first + b)
                        for h in range(2):
                            last = pe.transpose(bank(7)[:, h * WH:(h + 1) * WH], sumsT[:, h], ident[0:WH, 0:WH])
                        last.then_inc(sums_turned, 1)

                    def batch(b, before=True, more=True):
                        turned(b, 0)
                        if more:
                            quarter(b + 1, 0)
                            quarter(b + 1, 1)
                        if before:
                            weigh(b - 1, 1)
                        if more:
                            quarter(b + 1, 2)
                            quarter(b + 1, 3)
                        turned(b, 1)
                        if before:
                            turn_sums(b - 1)
                        weigh(b, 0, between=b + 1 if more else None)

                    for g in range(4):
                        quarter(0, g)
                    turn_peaks(0)
                    batch(0, before=False)
                    for b in range(1, B - 1):
                        batch(b)
                    batch(B - 1, more=False)
                    weigh(B - 1, 1)
                    turn_sums(B - 1)

                @block.scalar
                def _(act):
                    act.preload_act_table(ACT.Exp)

                    def take_peaks(b):
                        act.wait_ge(peaks_turned, first + b + 1)
                        if not at_start(b):
                            act.wait_ge(turned_made, 2 * first + 2 * b)
                        act.copy(peakT[0:peak_rows], bank(1, T, rows=peak_rows)).then_inc(peaks_ready, 1)

                    def exponential(b, h):
                        if bias is None:
                            act.wait_ge(turned_made, 2 * first + 2 * b + h + 1)
                        else:
                            act.wait_ge(turned_biased, 2 * first_biased + 2 * b + h + 1)
                        if not at_start(b):
                            act.wait_ge(half_summed, 2 * first + 2 * b + h - 1)
                        half_heads = slice(HH * h, HH * h + HH)
                        act.activation(flat(probsT[:, half_heads]),
                                       banks(2 + 2 * h, 2) if bias is None else flat(shifted[:, half_heads]),
                                       ACT.Exp, scale=scale if bias is None else 1.0).then_inc(half_probs, 1)

                    def take_sums(b):
                        act.wait_ge(half_summed, 2 * first + 2 * b + 2)
                        if not at_start(b):
                            act.wait_ge(sums_turned, first + b)
                        act.copy(flat(sumsT), bank(6, 2 * T, rows=WH)).then_inc(sums_taken, 1)

                    def second_half(b):
                        if bias is None:
                            exponential(b, 1)
                        take_peaks(b + 1)
                        if bias is not None:
                            exponential(b, 1)

                    take_peaks(0)
                    exponential(0, 0)
                    second_half(0)
                    for b in batches(act, 1, B - 1):
                        exponential(b, 0)
                        take_sums(b - 1)
                        second_half(b)
                    exponential(B - 1, 0)
                    take_sums(B - 2)
                    exponential(B - 1, 1)
                    take_sums(B - 1)

                @block.gpsimd
                def _(pool):
                    pool.memset(padded, 0.0).then_inc(pads_cleared, 1)
                    pool.wait_ge(pads_cleared, first // B + 1)
                    for b in batches(pool, 0, B):
                        for h in range(2):
                            if not at_start(b):
                                pool.wait_ge(half_summed, 2 * first + 2 * b + h - 1)
                            pool.tensor_copy(padded[:, h].rearrange("p (i c) -> p i c", i=HH)[:, :, 0:HD + 1],
                                             values[:, bass.ds(b, 1), HH * h:HH * h + HH].rearrange(
                                                 "p b h d -> p (b h) d")).then_inc(half_padded, 1)

                @block.vector
                def _(vec):
                    def bias_of(start, n):
                        return bias[:, start * T:(start + n) * T].rearrange("p (h k) -> p h k", k=T)

                    def largest(b, g):
                        heads = slice(4 * g, 4 * g + 4)
                        source = by_batch(g % 2)
                        vec.wait_ge(quarter_made, 4 * first + 4 * b + g + 1)
                        if not at_start(b):
                            vec.wait_ge(peaks_split, first + b)
                        vec.tensor_reduce(row_max[:, heads], source, AXIS_X, ALU.max).then_inc(quarter_max, 1)

                    def split(b):
                        high, mid, low = (peak_parts[:, H * j:H * j + H] for j in range(PARTS))
                        n = 3 * (first + b)
                        vec.wait_ge(quarter_max, 4 * first + 4 * b + 4)
                        if not at_start(b):
                            vec.wait_ge(peaks_turned, first + b)
                        vec.tensor_copy(high, row_max[:]).then_inc(part_made, 1)
                        vec.wait_ge(part_made, n + 1)
                        vec.tensor_tensor(row_rest[:], row_max[:], high, ALU.subtract).then_inc(part_made, 1)
                        vec.wait_ge(part_made, n + 2)
                        vec.tensor_copy(mid, row_rest[:]).then_inc(part_made, 1)
                        vec.wait_ge(part_made, n + 3)
                        vec.tensor_tensor(low, row_rest[:], mid, ALU.subtract).then_inc(peaks_split, 1)

                    def bias_turned(b, h):
                        vec.wait_ge(turned_made, 2 * first + 2 * b + h + 1)
                        if not at_start(b):
                            vec.wait_ge(half_probs, 2 * first + 2 * b + h - 1)
                        vec.scalar_tensor_tensor(out=shifted[:, HH * h:HH * h + HH], in0=by_batch(2 + 2 * h, 2),
                                                 scalar=scale, in1=bias_of(HH * h, HH), op0=ALU.mult,
                                                 op1=ALU.add).then_inc(turned_biased, 1)

                    def normalise(b):
                        sums = bank(7)[:, 0:H * (HD + 1)].rearrange("p (h d) -> p h d", d=HD + 1)
                        vec.wait_ge(sums_turned, first + b + 1)
                        if not at_start(b):
                            vec.wait_ge(results_made, first + b)
                        vec.reciprocal(row_rec[:], sums[:, :, HD]).then_inc(sums_inverted, 1)
                        vec.wait_ge(sums_inverted, first + b + 1)
                        vec.tensor_tensor(ctx_all[:, bass.ds(b, 1)].rearrange("p b (h d) -> p (b h) d", d=HD),
                                          sums[:, :, 0:HD], row_rec[:].unsqueeze(2).broadcast_to([128, H, HD]),
                                          ALU.mult).then_inc(results_made, 1)

                    def batch(b, before=True, more=True):
                        if bias is not None:
                            bias_turned(b, 0)
                        if more:
                            for g in range(4):
                                largest(b + 1, g)
                        if more:
                            split(b + 1)
                        if bias is not None:
                            bias_turned(b, 1)
                        if before:
                            normalise(b - 1)

                    for g in range(4):
                        largest(0, g)
                    split(0)
                    batch(0, before=False)
                    for b in batches(vec, 1, B - 1):
                        batch(b)
                    batch(B - 1, more=False)
                    normalise(B - 1)

        def stacked_prologue(pack, q, k, q_b=None, k_b=None, wv=None, vb=None, ob=None, self_attention=False, mask=None,
                             bias=None, scale=None):
            made = [] if wv is None else ["v0", "v1"]
            source = normedT if self_attention else contextT
            n = stacked_so_far["all"]
            plan(pe=["k", *made, *LN["pe"], "q0", "q1"] if not self_attention else [*LN["pe"], "q0", "q1", "k", *made],
                 act=(["root", "khigh", *LN["act"][1:], "kmid", "qhigh0", "qhigh1", "qmid0", "qmid1"] if not self_attention else
                      [*LN["act"], "qhigh0", "qhigh1", "qmid0", "qmid1", "khigh", "kmid"]),
                 vec=([*LN["vec"], "krest", "qrest0", "qrest1", "qlow0", "qlow1", *made]
                      if not self_attention else
                      [*LN["vec"], "qrest0", "qrest1", "qlow0", "qlow1", "krest", *made]),
                 pool=["klow", *(["bias"] if ob is not None else []), *(["pick"] if n == 0 else []),
                       *(["bias16"] if bias is not None else [])])

            def k_product(pe):
                for h in range(2):
                    last = pe.matmul(bank(4 + h), k, half(source, h), start=True, stop=True)
                last.then_inc(pe_done, P.step("k"))

            def v_product(pe):
                for h in range(len(made)):
                    for i in range(HB):
                        last = pe.matmul(by_batch(2 + h)[:, i], source[:, HB * h + i], wv, start=True, stop=True)
                    last.then_inc(pe_done, P.step(f"v{h}"))

            def part(act, out, source, bias):
                return act.copy(out, source) if bias is None else act.activation(out, source, ACT.Identity, bias=bias)

            def rest(vec, out, source, bias, high):
                return vec.scalar_tensor_tensor(out=out, in0=source, scalar=0.0 if bias is None else bias, in1=high,
                                                op0=ALU.add, op1=ALU.subtract)

            with nc.Block() as block:
                @block.sync
                def _(sync):
                    def stack_keys(m):
                        if m == 2:
                            sync.wait_ge(pool_done, G.after("klow"))
                        else:
                            sync.wait_ge(act_done, A.after(("khigh", "kmid")[m]))
                        for t in range(TERMS):
                            if KEY_PARTS[t] == m:
                                sync.dma_start(key_stack[HD * t:HD * t + HD], key_parts[:, m]).then_inc(keys_stacked, 16)

                    def stack_queries(m):
                        if m == 2:
                            sync.wait_ge(vec_done, V.after("qlow1"))
                        else:
                            sync.wait_ge(act_done, A.after(("qhigh1", "qmid1")[m]))
                        for t in range(TERMS):
                            if QUERY_PARTS[t] == m:
                                sync.dma_start(query_stack[HD * t:HD * t + HD], query_parts[:, m]).then_inc(
                                    queries_stacked, 16)

                    if self_attention:
                        for m in range(PARTS):
                            stack_queries(m)
                        for m in range(PARTS):
                            stack_keys(m)
                    else:
                        stack_keys(0)
                        stack_keys(1)
                        stack_queries(0)
                        stack_keys(2)
                        stack_queries(1)
                        stack_queries(2)
                    dmas = 16 * TERMS * (n + 1)
                    sync.wait_ge(keys_stacked, dmas)
                    sync.wait_ge(queries_stacked, dmas)

                @block.vector
                def _(vec):
                    def key_rest_step():
                        vec.wait_ge(act_done, A.after("khigh"))
                        rest(vec, key_rest, by_batch(4, 2), k_b, key_parts[:, 0]).then_inc(vec_done, V.step("krest"))

                    ln_vector(vec, residual, normed)
                    if not self_attention:
                        key_rest_step()
                    for h in range(2):
                        vec.wait_ge(act_done, A.after(f"qhigh{h}"))
                        rest(vec, half(query_rest, h), by_batch(6 + h), q_b, half(query_parts[:, 0], h)).then_inc(
                            vec_done, V.step(f"qrest{h}"))
                    for h in range(2):
                        vec.wait_ge(act_done, A.after(f"qmid{h}"))
                        vec.tensor_tensor(half(query_parts[:, 2], h), half(query_rest, h), half(query_parts[:, 1], h),
                                          ALU.subtract).then_inc(vec_done, V.step(f"qlow{h}"))
                    if self_attention:
                        key_rest_step()
                    if mask is not None:
                        vec.tensor_copy(mask16[:], mask)
                    for h in range(len(made)):
                        vec.wait_ge(pe_done, P.after(f"v{h}"))
                        target = half(values, h)[:, :, :, 0:HD].rearrange("p b h d -> p (b h) d")
                        if vb is None:
                            last = vec.tensor_copy(target, bank(2 + h).rearrange("p (b d) -> p b d", d=HD))
                        else:
                            for i in range(HB):
                                last = vec.tensor_tensor(
                                    values[:, HB * h + i, :, 0:HD],
                                    by_batch(2 + h)[:, i].rearrange("p (h d) -> p h d", d=HD),
                                    vb.rearrange("p (h d) -> p h d", d=HD), ALU.add)
                        last.then_inc(vec_done, V.step(f"v{h}"))

                @block.gpsimd
                def _(pool):
                    pool.wait_ge(vec_done, V.after("krest"))
                    pool.wait_ge(act_done, A.after("kmid"))
                    pool.tensor_tensor(key_parts[:, 2], key_rest, key_parts[:, 1], ALU.subtract).then_inc(
                        pool_done, G.step("klow"))
                    pool.wait_ge(loaded[pack], 16)
                    if ob is not None:
                        add_bias(pool, ob)
                    if n == 0:
                        pool.tensor_tensor(minus_pick, ones[0:peak_rows, 0:T].unsqueeze(1).broadcast_to([peak_rows, H, T]),
                                       W("C", "minus_pick", rows=slice(0, peak_rows)).unsqueeze(2).broadcast_to(
                                           [peak_rows, H, T]), ALU.mult).then_inc(pool_done, G.step("pick"))
                    if bias is not None:
                        pool.wait_ge(pe_done, P.after("v1"))
                        pool.tensor_scalar(bias16, bias, 1.0 / scale, None, ALU.mult).then_inc(
                            pool_done, G.step("bias16"))

                @block.tensor
                def _(pe):
                    pe.wait_ge(loaded[pack], 16)
                    out_tensor(pe)
                    if not self_attention:
                        k_product(pe)
                        if output["here"] is not None:
                            pe.wait_ge(vec_done, V.after("added1"))
                        v_product(pe)
                    ln_tensor(pe)
                    for h in range(2):
                        pe.wait_ge(act_done, A.after(f"xnT{h}"))
                        pe.matmul(bank(6 + h), q, half(normedT, h), start=True, stop=True).then_inc(
                            pe_done, P.step(f"q{h}"))
                    if self_attention:
                        k_product(pe)
                        v_product(pe)

                @block.scalar
                def _(act):
                    def high_keys():
                        act.wait_ge(pe_done, P.after("k"))
                        part(act, key_parts[:, 0], by_batch(4, 2), k_b).then_inc(act_done, A.step("khigh"))

                    def mid_keys():
                        act.wait_ge(vec_done, V.after("krest"))
                        act.copy(key_parts[:, 1], key_rest).then_inc(act_done, A.step("kmid"))

                    act.wait_ge(loaded[pack], 16)
                    ln_root(act)
                    if not self_attention:
                        high_keys()
                    ln_scalar(act)
                    if not self_attention:
                        mid_keys()
                    for h in range(2):
                        act.wait_ge(pe_done, P.after(f"q{h}"))
                        part(act, half(query_parts[:, 0], h), by_batch(6 + h), q_b).then_inc(
                            act_done, A.step(f"qhigh{h}"))
                    for h in range(2):
                        act.wait_ge(vec_done, V.after(f"qrest{h}"))
                        act.copy(half(query_parts[:, 1], h), half(query_rest, h)).then_inc(
                            act_done, A.step(f"qmid{h}"))
                    if self_attention:
                        high_keys()
                        mid_keys()

        peaks, p_inv = small[:, 20], small[:, 21, 0:1]
        def latent_prologue():
            q_rot, k_rot = scratch[:, 0:4], scratch[:, 4:8]
            lats, swaps = (S(12), S(15)), (S(13), S(17))
            qkvT, vlat = scratch[:, 8:11], [S(11), S(14)]
            mean_v, mean_z = probs[:, 0:B], probs[:, B:H]
            p_abs, p_sign, p_used, p_moved = (small[:, 16 + j, 0:1] for j in range(4))
            turns, red, absolute = shifted[:, 0], shifted[:, 1], shifted[:, 2]
            sums = small[:, 0]
            n_mats = len(ternary_weights)
            c1, c2 = 6.28125, float(2 * np.pi - 6.28125)
            groups = [(x, g) for x in "qk" for g in range(GROUPS)]
            at_bank = lambda u: 4 * ((u + 1) % 2)
            plan(pe=[*LN["pe"], "q", "k", "v", "mean", *[f"{x}{s}{g}" for x, g in groups for s in ("l", "s")],
                     "vl0", *[x for g in range(1, GROUPS) for x in (f"vl{g}", f"vo{g - 1}")], "vo3", "meanT", "vT", "wsum"],
                 act=[*LN["act"], "q", "k", "v", "mean", "abs", "sign", "ln", "exp", *[f"v{g}" for g in range(GROUPS)],
                      "vo", "sin_p", "abs_p", "cos_p"],
                 vec=[*LN["vec"], "moved", "qc0", "qs0", "pclip", "p", "pinv", "vclip",
                      *[f"{x}{s}{g}" for x, g in groups[1:4] for s in ("c", "s")], "z", "peak", "less",
                      *[f"{x}{s}{g}" for x, g in groups[4:] for s in ("c", "s")],
                      "wabs", "p0", "p1", "p2", "p3", "p4", "mean_values", "v", "wclip", "wrec"],
                 pool=["bias", *[f"{x}r{g}" for x, g in groups]])
            with nc.Block() as block:
                @block.vector
                def _(vec):
                    ts, stt = vec.tensor_scalar, vec.scalar_tensor_tensor

                    def chain(ins, name):
                        ins.then_inc(vec_done, V.step(name))
                        vec.wait_ge(vec_done, V.after(name))

                    def rotate(u):
                        x, g = groups[u]
                        bias = "q_lat_b" if x == "q" else "kv_lat_b"
                        swap = "q_swap_b" if x == "q" else "k_swap_b"
                        vec.wait_ge(pe_done, P.after(f"{x}l{g}"))
                        if u >= 2:
                            px, pg = groups[u - 2]
                            vec.wait_ge(pool_done, G.after(f"{px}r{pg}"))
                        stt(out=lats[u % 2], in0=by_batch(at_bank(u), 2), scalar=W("L0", bias),
                            in1=over_batches(W("L0", "cos"), B), op0=ALU.add,
                            op1=ALU.mult).then_inc(vec_done, V.step(f"{x}c{g}"))
                        vec.wait_ge(pe_done, P.after(f"{x}s{g}"))
                        stt(out=swaps[u % 2], in0=by_batch(at_bank(u) + 2, 2), scalar=W("L0", swap),
                            in1=over_batches(W("L0", "sin"), B), op0=ALU.add,
                            op1=ALU.mult).then_inc(vec_done, V.step(f"{x}s{g}"))

                    ln_vector(vec, residual, normed)
                    vec.wait_ge(loaded["L0"], 16)
                    ts(p_moved, W("L0", "p"), 0.0005, None, ALU.add).then_inc(vec_done, V.step("moved"))
                    rotate(0)
                    vec.wait_ge(act_done, A.after("sign"))
                    chain(ts(p_abs, p_abs, 0.001, 100.0, ALU.max, ALU.min), "pclip")
                    chain(vec.tensor_tensor(p_used, p_abs, p_sign, ALU.mult), "p")
                    vec.reciprocal(p_inv, p_used).then_inc(vec_done, V.step("pinv"))
                    ts(mean_v, mean_v, 1e-10, None, ALU.max).then_inc(vec_done, V.step("vclip"))
                    for u in range(1, 4):
                        rotate(u)
                    vec.wait_ge(act_done, A.after("ln"))
                    chain(ts(mean_z, mean_z, p_used, None, ALU.mult), "z")
                    chain(vec.tensor_reduce(peaks, mean_z, AXIS_X, ALU.max), "peak")
                    vec.tensor_tensor(mean_z, mean_z, peaks.unsqueeze(2).broadcast_to([128, B, T]),
                                      ALU.subtract).then_inc(vec_done, V.step("less"))
                    for u in range(4, 8):
                        rotate(u)
                    vec.wait_ge(loaded["L1"], 16)
                    vec.wait_ge(loaded["L3"], 16)
                    for m, (pack, name) in enumerate(ternary_weights):
                        last = vec.tensor_reduce(sums[:, m:m + 1], W(pack, name), AXIS_X, ALU.add,
                                                 apply_absolute_value=True)
                    last.then_inc(vec_done, V.step("wabs"))
                    chain(ts(turns, W("L1", "phases"), float(1 / (2 * np.pi)), ROUND, ALU.mult, ALU.add), "p0")
                    chain(ts(turns, turns, ROUND, None, ALU.subtract), "p1")
                    chain(stt(out=red, in0=turns, scalar=-c1, in1=W("L1", "phases"), op0=ALU.mult, op1=ALU.add), "p2")
                    chain(stt(out=red, in0=turns, scalar=-c2, in1=red, op0=ALU.mult, op1=ALU.add), "p3")
                    ts(red, red, PI_BELOW, -PI_BELOW, ALU.min, ALU.max).then_inc(vec_done, V.step("p4"))
                    for source, target, n, name in ((6, mean_values, "meanT", "mean_values"), (2, values, "vT", "v")):
                        vec.wait_ge(pe_done, P.after(n))
                        vec.tensor_copy(target[:, :, :, 0:HD].rearrange("p b h d -> p (b h) d"),
                                        banks(source, 2).rearrange("p (b d) -> p b d", d=HD)).then_inc(
                            vec_done, V.step(name))
                    vec.wait_ge(pe_done, P.after("wsum"))
                    chain(ts(weight_scales[:, 0:n_mats], bank(0, n_mats), 1.0 / (FF * D), 1e-5, ALU.mult, ALU.max),
                          "wclip")
                    vec.reciprocal(weight_inverses[:, 0:n_mats], weight_scales[:, 0:n_mats]).then_inc(
                        vec_done, V.step("wrec"))

                @block.gpsimd
                def _(pool):
                    pool.wait_ge(loaded["L0"], 16)
                    add_bias(pool, W("L0", "cproj_b"))
                    for u, (x, g) in enumerate(groups):
                        pool.wait_ge(vec_done, V.after(f"{x}s{g}"))
                        pool.tensor_tensor((q_rot if x == "q" else k_rot)[:, g], lats[u % 2], swaps[u % 2],
                                           ALU.add).then_inc(pool_done, G.step(f"{x}r{g}"))

                @block.tensor
                def _(pe):
                    def product(n, weight, source, start=True, stop=True):
                        for h in range(2):
                            last = pe.matmul(bank(n + h), weight, half(source, h), start=start, stop=stop)
                        return last

                    ln_tensor(pe)
                    pe.wait_ge(loaded["L0"], 16)
                    pe.wait_ge(act_done, A.after("xnT1"))
                    for j, x in enumerate("qkv"):
                        product(2 + 2 * j, W("L0", "qkv", j * D, D), normedT).then_inc(pe_done, P.step(x))
                    product(0, W("L0", "mean_v"), contextT).then_inc(pe_done, P.step("mean"))
                    pe.wait_ge(act_done, A.after("v"))
                    for u, (x, g) in enumerate(groups):
                        if u == 1:
                            pe.wait_ge(act_done, A.after("mean"))
                        if u >= 2:
                            px, pg = groups[u - 2]
                            pe.wait_ge(vec_done, V.after(f"{px}s{pg}"))
                        lat_w, swap_w = ("q_lat", "q_swap") if x == "q" else ("kv_lat", "k_swap")
                        source = qkvT[:, "qk".index(x)]
                        product(at_bank(u), W("L0", lat_w, g * 128, 128), source).then_inc(
                            pe_done, P.step(f"{x}l{g}"))
                        product(at_bank(u) + 2, W("L0", swap_w, g * 128, 128), source).then_inc(
                            pe_done, P.step(f"{x}s{g}"))
                    pe.wait_ge(vec_done, V.after("ks3"))
                    for g in range(GROUPS + 1):
                        if g < GROUPS:
                            if g >= 2:
                                pe.wait_ge(act_done, A.after(f"v{g - 2}"))
                            product(2 * (g % 2), W("L0", "kv_lat", g * 128, 128), qkvT[:, 2]).then_inc(
                                pe_done, P.step(f"vl{g}"))
                        if g:
                            pe.wait_ge(act_done, A.after(f"v{g - 1}"))
                            product(4, W("L0", "l2o", (g - 1) * 128, 128), vlat[(g - 1) % 2], start=g == 1,
                                    stop=g == GROUPS).then_inc(pe_done, P.step(f"vo{g - 1}"))
                    pe.wait_ge(act_done, A.after("exp"))
                    for b in range(B):
                        last = pe.transpose(by_batch(6, 2)[:, b], mean_v[:, b], ident)
                    last.then_inc(pe_done, P.step("meanT"))
                    pe.wait_ge(act_done, A.after("vo"))
                    for b in range(B):
                        last = pe.transpose(by_batch(2, 2)[:, b], S(12)[:, b], ident)
                    last.then_inc(pe_done, P.step("vT"))
                    pe.wait_ge(vec_done, V.after("wabs"))
                    pe.matmul(bank(0, n_mats), ones[:, 0:128], sums[:, 0:n_mats], start=True, stop=True).then_inc(
                        pe_done, P.step("wsum"))

                @block.scalar
                def _(act):
                    ln_root(act)
                    ln_scalar(act)
                    act.wait_ge(loaded["L0"], 16)
                    for j, x in enumerate("qkv"):
                        act.wait_ge(pe_done, P.after(x))
                        act.activation(qkvT[:, j], by_batch(2 + 2 * j, 2), ACT.Identity,
                                       bias=W("L0", "qkv_b", j, 1)).then_inc(act_done, A.step(x))
                    act.wait_ge(pe_done, P.after("mean"))
                    act.activation(mean_v, by_batch(0, 2), ACT.Abs, bias=W("L0", "shift")).then_inc(
                        act_done, A.step("mean"))
                    act.activation(p_abs, W("L0", "p"), ACT.Abs).then_inc(act_done, A.step("abs"))
                    act.wait_ge(vec_done, V.after("moved"))
                    act.activation(p_sign, p_moved, ACT.Sign).then_inc(act_done, A.step("sign"))
                    act.wait_ge(vec_done, V.after("vclip"))
                    act.activation(mean_z, mean_v, ACT.Ln).then_inc(act_done, A.step("ln"))
                    act.wait_ge(vec_done, V.after("less"))
                    act.activation(mean_v, mean_z, ACT.Exp).then_inc(act_done, A.step("exp"))
                    for g in range(GROUPS):
                        act.wait_ge(pe_done, P.after(f"vl{g}"))
                        if g >= 2:
                            act.wait_ge(pe_done, P.after(f"vo{g - 2}"))
                        act.activation(vlat[g % 2], by_batch(2 * (g % 2), 2), ACT.Identity, bias=W("L0", "kv_lat_b")).then_inc(
                            act_done, A.step(f"v{g}"))
                    act.wait_ge(pe_done, P.after("vo3"))
                    act.wait_ge(pool_done, G.after("kr3"))
                    act.copy(S(12), by_batch(4, 2)).then_inc(act_done, A.step("vo"))
                    act.wait_ge(vec_done, V.after("p4"))
                    act.activation(position_waves[:, 0], red, ACT.Sin).then_inc(act_done, A.step("sin_p"))
                    act.activation(absolute, red, ACT.Abs).then_inc(act_done, A.step("abs_p"))
                    act.wait_ge(act_done, A.after("abs_p"))
                    act.activation(position_waves[:, 1], absolute, ACT.Sin, bias=half_pi[:], scale=-1.0).then_inc(
                        act_done, A.step("cos_p"))
            return q_rot, k_rot

        def hinge_ffn():
            steps = INNER // 2
            s, g = S(0), S(1)
            hinge = [S(2), S(3)]
            plan(pe=[*LN["pe"], "s", "o0", "o1"], act=[*LN["act"], "s", *[f"h{i}" for i in range(steps)]],
                 vec=[*LN["vec"], *[f"g{i}" for i in range(steps)], "r0", "r1"], pool=["bias"])
            with nc.Block() as block:
                @block.vector
                def _(vec):
                    ln_vector(vec, residual, normed)
                    for i in range(steps):
                        vec.wait_ge(act_done, A.after(f"h{i}"))
                        w2 = W("L0", "w2", i, 1)
                        if i == 0:
                            last = vec.tensor_scalar(g, hinge[0], w2, W("L0", "b2"), ALU.mult, ALU.add)
                        else:
                            vec.wait_ge(vec_done, V.after(f"g{i - 1}"))
                            last = vec.scalar_tensor_tensor(out=g, in0=hinge[i % 2], scalar=w2, in1=g, op0=ALU.mult,
                                                            op1=ALU.add)
                        last.then_inc(vec_done, V.step(f"g{i}"))
                    vec.wait_ge(pool_done, G.after("bias"))
                    for h in range(2):
                        vec.wait_ge(pe_done, P.after(f"o{h}"))
                        vec.tensor_tensor(half(residual, h), half(residual, h), by_batch(4 + h), ALU.add).then_inc(
                            vec_done, V.step(f"r{h}"))

                @block.gpsimd
                def _(pool):
                    add_bias(pool, W("L0", "bout"))

                @block.tensor
                def _(pe):
                    out_tensor(pe)
                    ln_tensor(pe)
                    for h in range(2):
                        pe.wait_ge(act_done, A.after(f"xnT{h}"))
                        last = pe.matmul(bank(2 + h), W("L0", "win"), half(normedT, h), start=True, stop=True)
                    last.then_inc(pe_done, P.step("s"))
                    pe.wait_ge(vec_done, V.after(f"g{steps - 1}"))
                    for h in range(2):
                        for i in range(HB):
                            last = pe.matmul(by_batch(4 + h)[:, i], g[:, HB * h + i], W("L0", "wout"), start=True,
                                             stop=True)
                        last.then_inc(pe_done, P.step(f"o{h}"))

                @block.scalar
                def _(act):
                    ln_root(act)
                    ln_scalar(act)
                    act.wait_ge(pe_done, P.after("s"))
                    act.activation(s, by_batch(2, 2), ACT.Identity, bias=W("L0", "bin")).then_inc(
                        act_done, A.step("s"))
                    act.wait_ge(act_done, A.after("s"))
                    for i in range(steps):
                        if i >= 2:
                            act.wait_ge(vec_done, V.after(f"g{i - 2}"))
                        act.activation(hinge[i % 2], s, ACT.Relu, bias=W("L0", "b1", i, 1),
                                       scale=W("L0", "w1", i, 1)).then_inc(act_done, A.step(f"h{i}"))

        stages = []

        def stage(f):
            stages.append(f)

        stage(lambda: (
            latent_attention(LAT ** -0.5, W("L0", "causal"), *latent_prologue()),
            attention_out(W("L0", "cproj"), bias=W("L0", "l2o_b"))))

        def cross(pack):
            bias = W("L3", "alibi") if pack == "L3" else None
            stacked_prologue(pack, W(pack, "xq"), W(pack, "xk"), W(pack, "xq_b"), W(pack, "xk_b"), W(pack, "xv"),
                             W(pack, "xv_b"), W(pack, "xo_b"), bias=bias, scale=HD ** -0.5)
            stacked_attention(HD ** -0.5, bias=bias)
            attention_out(W(pack, "xo"))

        stage(lambda: cross("L0"))
        stage(hinge_ffn)

        def phase_memory():
            pv, keys, kv, hidden, branch, gates, logit1, diff, w_pos, w_kv, angle, sin_k, cos_k = (
                S(i) for i in range(13))
            tmp = S(13)
            sin_p, cos_p = position_waves[:, 0], position_waves[:, 1]
            carry = probs[:, 0:B]
            a0, a1, m0, m1 = (x for x in (probs[:, B:H], probsT[:, 0:B], probsT[:, B:H], k_heads[:, 0:B]))
            m2, m3 = k_heads[:, B:H], tmp
            w = lambda name: W("L1", name)
            plan(pe=[*LN["pe"], "pv", "keys", "hidden", "kv", "branch", "gate", "l0", "l1", "turn", "lnT", "out"],
                 act=[*LN["act"], "pv", "keys", "hidden", "branch", "kv", "abs_k", "sin_k", "cos_k", "gates", "l1",
                      "log", "root", "w_pos", "w_kv", "tokens", "root2", "ln"],
                 vec=[*LN["vec"], "const", "carry", "cv", "cm", "sv", "k0", "angle", "sm", "pc", "ps", "p", *ternary_steps("L1"),
                      "g", "gmax", "vg", "wc", "wm", "diff", "ws", "wn", "ks", "k", "bp", "bk", "b",
                      *[x + "2" for x in LN["vec"]], "r0", "r1"],
                 pool=["bias", "input", "kc", "wr"])
            with nc.Block() as block:
                @block.tensor
                def _(pe):
                    def product(n, weight, source, start=True, stop=True, rows=128):
                        for h in range(2):
                            last = pe.matmul(bank(n + h, rows=rows), weight, half(source, h), start=start, stop=stop)
                        return last

                    ln_tensor(pe)
                    pe.wait_ge(loaded["L1"], 16)
                    pe.wait_ge(act_done, A.after("xnT1"))
                    product(0, w("wpv"), normedT).then_inc(pe_done, P.step("pv"))
                    product(2, w("wk"), normedT).then_inc(pe_done, P.step("keys"))
                    product(6, w("wg1"), normedT, stop=False)
                    product(6, w("wg1_shift"), normedT_padded[:, :, 0:T], start=False).then_inc(
                        pe_done, P.step("hidden"))
                    product(4, w("wkv"), normedT).then_inc(pe_done, P.step("kv"))
                    pe.wait_ge(act_done, A.after("pv"))
                    product(0, w("wb1"), normedT, rows=64).then_inc(pe_done, P.step("branch"))
                    pe.wait_ge(act_done, A.after("hidden"))
                    product(6, w("wg2"), hidden).then_inc(pe_done, P.step("gate"))
                    pe.wait_ge(act_done, A.after("kv"))
                    product(2, W("L1", "wb2_0", rows=slice(0, 64)), branch[0:64]).then_inc(pe_done, P.step("l0"))
                    product(4, W("L1", "wb2_1", rows=slice(0, 64)), branch[0:64]).then_inc(pe_done, P.step("l1"))
                    pe.wait_ge(vec_done, V.after("b"))
                    for b in range(B):
                        last = pe.transpose(by_batch(0, 2)[:, b], a0[:, b], ident)
                    last.then_inc(pe_done, P.step("turn"))
                    pe.wait_ge(vec_done, V.after("xn12"))
                    for b in range(B):
                        last = pe.transpose(by_batch(2, 2)[:, b], a1[:, b], ident)
                    last.then_inc(pe_done, P.step("lnT"))
                    pe.wait_ge(act_done, A.after("ln"))
                    for b in range(B):
                        last = pe.matmul(by_batch(4, 2)[:, b], m0[:, b], w("wo"), start=True, stop=True)
                    last.then_inc(pe_done, P.step("out"))

                @block.scalar
                def _(act):
                    ln_root(act)
                    ln_scalar(act)
                    act.wait_ge(pe_done, P.after("pv"))
                    act.activation(pv, by_batch(0, 2), ACT.Identity, bias=w("bpv")).then_inc(act_done, A.step("pv"))
                    act.wait_ge(pe_done, P.after("keys"))
                    act.activation(keys, by_batch(2, 2), ACT.Tanh, bias=w("bk")).then_inc(act_done, A.step("keys"))
                    act.wait_ge(pe_done, P.after("hidden"))
                    act.activation(hidden, by_batch(6, 2), ACT.Gelu, bias=w("bg1")).then_inc(
                        act_done, A.step("hidden"))
                    act.wait_ge(pe_done, P.after("branch"))
                    act.activation(branch[0:64], psum[0:64, 0:2, :].rearrange("p k (b c) -> p (k b) c", c=T), ACT.Gelu,
                                   bias=W("L1", "bb1", rows=slice(0, 64))).then_inc(act_done, A.step("branch"))
                    act.activation(kv, by_batch(4, 2), ACT.Identity, bias=w("bkv")).then_inc(act_done, A.step("kv"))
                    act.wait_ge(vec_done, V.after("angle"))
                    act.activation(logit1, angle, ACT.Abs).then_inc(act_done, A.step("abs_k"))
                    act.activation(sin_k, angle, ACT.Sin).then_inc(act_done, A.step("sin_k"))
                    act.wait_ge(act_done, A.after("abs_k"))
                    act.activation(cos_k, logit1, ACT.Sin, bias=half_pi[:], scale=-1.0).then_inc(
                        act_done, A.step("cos_k"))
                    act.wait_ge(pe_done, P.after("gate"))
                    act.activation(gates, by_batch(6, 2), ACT.Sigmoid, bias=w("bg2")).then_inc(
                        act_done, A.step("gates"))
                    act.wait_ge(pe_done, P.after("l1"))
                    act.wait_ge(act_done, A.after("cos_k"))
                    act.activation(logit1, by_batch(4, 2), ACT.Identity, bias=w("bb2_1")).then_inc(
                        act_done, A.step("l1"))
                    act.wait_ge(vec_done, V.after("gmax"))
                    act.activation(m3, m3, ACT.Ln).then_inc(act_done, A.step("log"))
                    act.wait_ge(act_done, A.after("log"))
                    act.activation(m2, m3, ACT.Exp, scale=-0.5).then_inc(act_done, A.step("root"))
                    act.wait_ge(vec_done, V.after("diff"))
                    act.activation(w_pos, diff, ACT.Sigmoid).then_inc(act_done, A.step("w_pos"))
                    act.activation(w_kv, diff, ACT.Sigmoid, scale=-1.0).then_inc(act_done, A.step("w_kv"))
                    act.wait_ge(pe_done, P.after("turn"))
                    act.activation(a1, by_batch(0, 2), ACT.Copy, scale=float(D) ** -0.5).then_inc(
                        act_done, A.step("tokens"))
                    ln_root(act, again="2")
                    act.wait_ge(pe_done, P.after("lnT"))
                    act.activation(m0, by_batch(2, 2), ACT.Identity, bias=w("ln_b"), scale=w("ln_g")).then_inc(
                        act_done, A.step("ln"))

                @block.gpsimd
                def _(pool):
                    pool.wait_ge(loaded["L1"], 16)
                    add_bias(pool, w("bo"))
                    pool.wait_ge(pool_done, G.after("bias"))
                    pool.tensor_tensor(residual[:], residual[:], normed[:], ALU.add).then_inc(
                        pool_done, G.step("input"))
                    pool.wait_ge(vec_done, V.after("wm"))
                    pool.tensor_tensor(m0, m0, cos_k, ALU.mult).then_inc(pool_done, G.step("kc"))
                    pool.wait_ge(act_done, A.after("w_kv"))
                    pool.tensor_tensor(w_kv, w_kv, m2, ALU.mult).then_inc(pool_done, G.step("wr"))

                @block.vector
                def _(vec):
                    tt, ts, stt = vec.tensor_tensor, vec.tensor_scalar, vec.scalar_tensor_tensor

                    ln_vector(vec, residual, normed)
                    vec.memset(carry, 1.0).then_inc(vec_done, V.step("const"))
                    vec.wait_ge(vec_done, V.after("const"))
                    vec.memset(carry[:, :, 0:1], 0.0).then_inc(vec_done, V.step("carry"))
                    vec.wait_ge(vec_done, V.after("carry"))

                    def scan(out, values, name):
                        vec.tensor_tensor_scan(flat(out), flat(carry), flat(values), 0.0, ALU.mult,
                                               ALU.add).then_inc(vec_done, V.step(name))

                    vec.wait_ge(act_done, A.after("pv"))
                    tt(a0, pv, over_batches(cos_p, B), ALU.mult).then_inc(vec_done, V.step("cv"))
                    vec.wait_ge(vec_done, V.after("cv"))
                    scan(m0, a0, "cm")
                    tt(a1, pv, over_batches(sin_p, B), ALU.mult).then_inc(vec_done, V.step("sv"))
                    vec.wait_ge(vec_done, V.after("sv"))
                    vec.wait_ge(act_done, A.after("keys"))
                    ts(angle, keys, PI, PI_BELOW, ALU.mult, ALU.min).then_inc(vec_done, V.step("k0"))
                    vec.wait_ge(vec_done, V.after("k0"))
                    ts(angle, angle, -PI_BELOW, None, ALU.max).then_inc(vec_done, V.step("angle"))
                    scan(m1, a1, "sm")
                    vec.wait_ge(vec_done, V.after("sm"))
                    tt(m0, m0, over_batches(cos_p, B), ALU.mult).then_inc(vec_done, V.step("pc"))
                    tt(m1, m1, over_batches(sin_p, B), ALU.mult).then_inc(vec_done, V.step("ps"))
                    vec.wait_ge(vec_done, V.after("ps"))
                    tt(pv, m0, m1, ALU.add).then_inc(vec_done, V.step("p"))
                    make_ternary(vec, "L1", flat(shifted[:, 0:HB]))
                    vec.wait_ge(act_done, A.after("gates"))
                    scan(m2, gates, "g")
                    vec.wait_ge(vec_done, V.after("g"))
                    ts(m3, m2, 1.0, None, ALU.max).then_inc(vec_done, V.step("gmax"))
                    tt(kv, kv, gates, ALU.mult).then_inc(vec_done, V.step("vg"))
                    vec.wait_ge(vec_done, V.after("vg"))
                    vec.memset(a0[:, :, 0:1], 0.0)
                    vec.memset(a1[:, :, 0:1], 0.0)
                    tt(a0[:, :, 1:T], cos_k[:, :, 0:T - 1], kv[:, :, 1:T], ALU.mult).then_inc(vec_done, V.step("wc"))
                    vec.wait_ge(vec_done, V.after("wc"))
                    scan(m0, a0, "wm")
                    vec.wait_ge(act_done, A.after("l1"))
                    stt(out=diff, in0=by_batch(2, 2), scalar=w("bb2_0"), in1=logit1, op0=ALU.add,
                        op1=ALU.subtract).then_inc(vec_done, V.step("diff"))
                    tt(a1[:, :, 1:T], sin_k[:, :, 0:T - 1], kv[:, :, 1:T], ALU.mult).then_inc(vec_done, V.step("ws"))
                    vec.wait_ge(vec_done, V.after("ws"))
                    scan(m1, a1, "wn")
                    vec.wait_ge(vec_done, V.after("wn"))
                    tt(m1, m1, sin_k, ALU.mult).then_inc(vec_done, V.step("ks"))
                    vec.wait_ge(vec_done, V.after("ks"))
                    vec.wait_ge(pool_done, G.after("kc"))
                    tt(m0, m0, m1, ALU.add).then_inc(vec_done, V.step("k"))
                    vec.wait_ge(act_done, A.after("w_pos"))
                    tt(pv, pv, w_pos, ALU.mult).then_inc(vec_done, V.step("bp"))
                    vec.wait_ge(pool_done, G.after("wr"))
                    vec.wait_ge(vec_done, V.after("bp"))
                    tt(a1, m0, w_kv, ALU.mult).then_inc(vec_done, V.step("bk"))
                    vec.wait_ge(vec_done, V.after("bk"))
                    tt(a0, pv, a1, ALU.add).then_inc(vec_done, V.step("b"))
                    vec.wait_ge(act_done, A.after("tokens"))
                    ln_vector(vec, a1, a1, again="2")
                    vec.wait_ge(pe_done, P.after("out"))
                    for h in range(2):
                        tt(half(residual, h), half(residual, h), by_batch(4 + h), ALU.add).then_inc(
                            vec_done, V.step(f"r{h}"))

        stage(phase_memory)
        stage(lambda: cross("L1"))

        def quantised_ffn(pack, gated):
            w = lambda name: W(pack, name)
            hidden = scratch[:, 0:4].rearrange("p a b c -> p (a b c)").rearrange("p (b f) -> p b f", f=FF)
            squares = scratch[:, 4:8].rearrange("p a b c -> p (a b c)").rearrange("p (b f) -> p b f", f=FF)
            scaled = S(8)
            xq = S(9).bitcast(BF16)[:, :, 0:D]
            xqT = S(9).bitcast(BF16)[:, :, D:2 * D]
            up_q, down_q = ternary[pack][:, 0], ternary[pack][:, 1]
            gate_q = ternary[pack][:, 2] if gated else None
            up_scale, down_scale, gate_scale = (weight_scales[:, j:j + 1] for j in ((2, 3, 4) if gated else (0, 1, 0)))
            hq = probs.bitcast(BF16).rearrange("p h k -> p (h k)").rearrange("p (b f) -> p b f", f=FF)
            hqT = probsT[:].bitcast(BF16).rearrange("p h k -> p (h k)").rearrange("p (b f) -> p b f", f=FF)
            up_in = shifted.rearrange("p h k -> p (h k)").rearrange("p (s f) -> p s f", f=FF)
            amax, inv, tok, up_s, gate_s = (small[:, 3 + j] for j in range(5))
            amax2, inv2, tok2 = (small[:, 8 + j] for j in range(3))
            last_b = B - 1
            up_at = lambda b: 2 * (b % 4) if gated else b
            plan(pe=["xqT", *[f"u{b}" for b in range(B)], "hT0", *[x for b in range(1, B) for x in (f"hT{b}", f"o{b - 1}")],
                     f"o{B - 1}"],
                 act=["root", "xqT", *[f"h{b}" for b in range(B)], *[x for b in range(0, B, 2) for x in (f"i{b + 1}", f"hT{b}", f"hT{b + 1}")]],
                 vec=[*LN["vec"], "amax", "aclip", "inv", "sx", "x1", "x2", "xq", "tok", "scales", "scales2",
                      *[f"s{b}" for b in range(B)],
                      *[x for h in range(2) for x in (
                          *[f"{c}{h}" for c in ("amax2", "aclip2", "inv2", "sx2")],
                          *[x for b in range(HB * h, HB * h + HB) for x in (
                              [f"m{b}", f"n{b}", f"i{b}"] if b % 2 == 0 else [f"m{b}", f"n{b}"])])],
                      "tok2", "tok2w", *[f"r{b}" for b in range(B)]],
                 pool=[*([] if gated else ["bias"]),
                       *([f"t{b}" for b in range(B)] if gated else [])])
            with nc.Block() as block:
                @block.vector
                def _(vec):
                    ts, stt = vec.tensor_scalar, vec.scalar_tensor_tensor

                    def chain(ins, name):
                        ins.then_inc(vec_done, V.step(name))
                        vec.wait_ge(vec_done, V.after(name))

                    vec.wait_ge(loaded[pack], 16)
                    ln_vector(vec, residual, normed)
                    vec.wait_ge(vec_done, V.after("xn1"))
                    chain(vec.tensor_reduce(amax, normed[:], AXIS_X, ALU.max, apply_absolute_value=True), "amax")
                    chain(ts(amax, amax, 1e-5, None, ALU.max), "aclip")
                    chain(vec.reciprocal(inv, amax), "inv")
                    chain(ts(inv, inv, 127.0, None, ALU.mult), "sx")
                    chain(vec.tensor_tensor(scaled, normed[:], inv.unsqueeze(2).broadcast_to([128, B, D]), ALU.mult), "x1")
                    chain(ts(scaled, scaled, 127.0, -128.0, ALU.min, ALU.max), "x2")
                    chain(ts(xq, scaled, ROUND, ROUND, ALU.add, ALU.subtract), "xq")
                    chain(ts(tok, amax, 1.0 / 127.0, None, ALU.mult), "tok")
                    chain(ts(up_s, tok, up_scale, None, ALU.mult), "scales")
                    chain(ts(gate_s, tok, gate_scale, None, ALU.mult), "scales2")
                    for b in range(B):
                        vec.wait_ge(pe_done, P.after(f"u{b}"))
                        if gated:
                            vec.wait_ge(act_done, A.after(f"h{b}"))
                            if b >= 2:
                                vec.wait_ge(pool_done, G.after(f"t{b - 2}"))
                            stt(out=up_in[:, b % 2], in0=bank(up_at(b)), scalar=up_s[:, b:b + 1],
                                in1=squares[:, b], op0=ALU.mult, op1=ALU.mult).then_inc(vec_done, V.step(f"s{b}"))
                        else:
                            stt(out=squares[:, b], in0=bank(up_at(b)), scalar=up_s[:, b:b + 1], in1=w("up_b"),
                                op0=ALU.mult, op1=ALU.add).then_inc(vec_done, V.step(f"s{b}"))
                    for h in range(2):
                        half_b = slice(HB * h, HB * h + HB)
                        if gated:
                            vec.wait_ge(pool_done, G.after(f"t{HB * h + HB - 1}"))
                        else:
                            vec.wait_ge(act_done, A.after(f"h{HB * h + HB - 1}"))
                        chain(vec.tensor_reduce(amax2[:, half_b], hidden[:, half_b], AXIS_X, ALU.max,
                                                apply_absolute_value=True), f"amax2{h}")
                        chain(ts(amax2[:, half_b], amax2[:, half_b], 1e-5, None, ALU.max), f"aclip2{h}")
                        chain(vec.reciprocal(inv2[:, half_b], amax2[:, half_b]), f"inv2{h}")
                        chain(ts(inv2[:, half_b], inv2[:, half_b], 127.0, None, ALU.mult), f"sx2{h}")
                        for b in range(HB * h, HB * h + HB):
                            chain(ts(hidden[:, b], hidden[:, b], inv2[:, b:b + 1], 127.0, ALU.mult, ALU.min), f"m{b}")
                            chain(ts(hidden[:, b], hidden[:, b], -128.0, ROUND, ALU.max, ALU.add), f"n{b}")
                            if b % 2 == 0:
                                ts(hq[:, b], hidden[:, b], ROUND, None, ALU.subtract).then_inc(
                                    vec_done, V.step(f"i{b}"))
                    chain(ts(tok2, amax2, 1.0 / 127.0, None, ALU.mult), "tok2")
                    chain(ts(tok2, tok2, down_scale, None, ALU.mult), "tok2w")
                    if not gated:
                        vec.wait_ge(pool_done, G.after("bias"))
                    for b in range(B):
                        vec.wait_ge(pe_done, P.after(f"o{b // HB * HB + HB - 1}"))
                        stt(out=residual[:, b], in0=by_batch(6, 2)[:, b], scalar=tok2[:, b:b + 1], in1=residual[:, b],
                            op0=ALU.mult, op1=ALU.add).then_inc(vec_done, V.step(f"r{b}"))

                @block.gpsimd
                def _(pool):
                    if not gated:
                        pool.wait_ge(loaded[pack], 16)
                        add_bias(pool, w("down_b"))
                    for b in range(B if gated else 0):
                        pool.wait_ge(vec_done, V.after(f"s{b}"))
                        pool.tensor_tensor(hidden[:, b], up_in[:, b % 2], squares[:, b], ALU.mult).then_inc(
                            pool_done, G.step(f"t{b}"))

                @block.tensor
                def _(pe):
                    out_tensor(pe)
                    pe.wait_ge(vec_done, V.after("xq"))
                    turned = psum[:, 0, :].bitcast(BF16).rearrange("p (b c) -> p b c", c=T)
                    for b in range(B):
                        last = pe.transpose(turned[:, b], xq[:, b], ident16[:])
                    last.then_inc(pe_done, P.step("xqT"))
                    pe.wait_ge(act_done, A.after("xqT"))
                    for b in range(B):
                        if gated:
                            if b >= 4:
                                pe.wait_ge(vec_done, V.after(f"s{b - 4}"))
                            pe.matmul(bank(up_at(b) + 1), xqT[:, b], gate_q, start=True, stop=True)
                        pe.matmul(bank(up_at(b)), xqT[:, b], up_q, start=True, stop=True).then_inc(
                            pe_done, P.step(f"u{b}"))

                    def down(b):
                        pe.wait_ge(act_done, A.after(f"hT{b}"))
                        for c in range(4):
                            last = pe.matmul(by_batch(6, 2)[:, b], hqT[:, b, c * 128:(c + 1) * 128],
                                             down_q[:, c * 128:(c + 1) * 128], start=c == 0, stop=c == 3)
                        last.then_inc(pe_done, P.step(f"o{b}"))

                    for b in range(B):
                        if b % 2 == 0:
                            pe.wait_ge(vec_done, V.after(f"i{b}"))
                        else:
                            pe.wait_ge(act_done, A.after(f"i{b}"))
                        if b == 0:
                            pe.wait_ge(vec_done, V.after(f"s{last_b}"))
                        if b >= 2:
                            pe.wait_ge(act_done, A.after(f"hT{b - 2}"))
                        turned = psum[:, b % 2, 0:256].bitcast(BF16).rearrange("p (c k) -> p c k", k=T)
                        for c in range(4):
                            last = pe.transpose(turned[:, c], hq[:, b, c * 128:(c + 1) * 128], ident16[:])
                        last.then_inc(pe_done, P.step(f"hT{b}"))
                        if b:
                            down(b - 1)
                    down(B - 1)

                @block.scalar
                def _(act):
                    ln_root(act)
                    act.wait_ge(pe_done, P.after("xqT"))
                    act.copy(xqT, psum[:, 0, :].bitcast(BF16).rearrange("p (b c) -> p b c", c=T)).then_inc(
                        act_done, A.step("xqT"))
                    for b in range(B):
                        if gated:
                            act.wait_ge(pe_done, P.after(f"u{b}"))
                            act.wait_ge(vec_done, V.after("scales2"))
                            last = act.activation(squares[:, b], bank(up_at(b) + 1), ACT.Relu,
                                                  scale=gate_s[:, b:b + 1])
                        else:
                            act.wait_ge(vec_done, V.after(f"s{b}"))
                            last = act.activation(hidden[:, b], squares[:, b], ACT.Gelu)
                        last.then_inc(act_done, A.step(f"h{b}"))

                    def copy(b):
                        act.wait_ge(pe_done, P.after(f"hT{b}"))
                        act.copy(hqT[:, b], psum[:, b % 2, 0:256].bitcast(BF16)).then_inc(act_done, A.step(f"hT{b}"))

                    for b in range(0, B, 2):
                        act.wait_ge(vec_done, V.after(f"n{b + 1}"))
                        act.activation(hq[:, b + 1], hidden[:, b + 1], ACT.Identity, bias=minus_round[:]).then_inc(
                            act_done, A.step(f"i{b + 1}"))
                        copy(b)
                        copy(b + 1)

        stage(lambda: quantised_ffn("L1", False))

        def recurrence():
            chunk = 512 // B
            banks_used = T // chunk
            states = S(0).rearrange("p b t -> p (b t)").rearrange("p (t b) -> p t b", b=B)
            plan(pe=[*LN["pe"], "inputs", "hT"], act=[*LN["act"]], vec=[*LN["vec"], *ternary_steps("L3"), "r"])
            with nc.Block() as block:
                @block.vector
                def _(vec):
                    ln_vector(vec, residual, normed)
                    make_ternary(vec, "L3", flat(S(1)[:, 0:HB]))
                    vec.wait_ge(pe_done, P.after("hT"))
                    vec.tensor_tensor(residual[:], residual[:], by_batch(0, 2), ALU.add).then_inc(
                        vec_done, V.step("r"))

                @block.tensor
                def _(pe):
                    ln_tensor(pe)
                    pe.wait_ge(loaded["L2"], 16)
                    pe.wait_ge(act_done, A.after("xnT1"))
                    by_step = normedT.rearrange("p b t -> p t b")

                    def from_inputs(start, steps):
                        return pe.matmul(banks(2, banks_used)[:, start * B:(start + steps) * B], W("L2", "wi"),
                                         by_step[:, start:start + steps], start=True, stop=False,
                                         skip_group_check=True)

                    def from_biases(start, steps):
                        return pe.matmul(banks(2, banks_used)[:, start * B:(start + steps) * B],
                                         W("L2", "ih_b", rows=slice(0, 2)),
                                         ones[0:2, 0:B].unsqueeze(1).broadcast_to([2, steps, B]), start=False,
                                         stop=True, skip_group_check=True)

                    from_inputs(0, chunk)
                    from_biases(0, chunk).then_inc(pe_done, P.step("inputs"))

                    def step(t):
                        pe.wait_ge(state_made, t)
                        pe.matmul(banks(2, 2)[:, t * B:(t + 1) * B], W("L2", "wh"), states[:, t - 1],
                                  start=False, stop=True, skip_group_check=True).then_inc(sum_made, 1)

                    for t in range(1, T):
                        step(t)
                        start = (t // chunk + 1) * chunk
                        if start < T and t % chunk in (8, 16):
                            (from_inputs if t % chunk == 8 else from_biases)(start, chunk)
                    pe.wait_ge(state_made, T)
                    for b in range(B):
                        last = pe.transpose(by_batch(0, 2)[:, b], states[:, :, b], ident)
                    last.then_inc(pe_done, P.step("hT"))

                @block.scalar
                def _(act):
                    ln_root(act)
                    ln_scalar(act)
                    act.preload_act_table(ACT.Tanh)
                    act.wait_ge(pe_done, P.after("inputs"))

                    def step(t):
                        if t:
                            act.wait_ge(sum_made, t)
                        act.activation(states[:, t], banks(2, 2)[:, t * B:(t + 1) * B],
                                       ACT.Tanh).then_inc(state_made, 1)

                    for t in range(T):
                        step(t)

        stage(recurrence)

        stage(lambda: (
            stacked_prologue("L2", W("L2", "xq"), W("L2", "xk")),
            stacked_attention(D ** -0.5, values=mean_values),
            attention_out(W("L2", "xo"), gem=(peaks, p_inv, W("L0", "shift")))))

        def experts_ffn():
            rows = PARTS * EXPERTS
            weight_of = S(0).bitcast(BF16)[0:rows, 0:HB].rearrange("p b t -> p (b t)").rearrange(
                "p (b t) -> p b t", b=B)
            pick16 = flat(S(0).bitcast(BF16)[0:rows, HB:B])
            parts = flat(S(13)[:, 3:4]).bitcast(BF16)[:, 0:B * rows].rearrange("p (b m e) -> p b m e", b=B, m=PARTS)
            units = scratch[:, 1:3]
            sig = [S(3 + j)[:, 0:HB] for j in range(3)]
            gated = [S(6 + j)[:, 0:HB] for j in range(3)]
            part = [S(9 + j)[:, 0:HB] for j in range(3)]
            order = [(e, h, c) for e in range(EXPERTS) for h in range(2) for c in range(2)]
            row = lambda j: S(12)[:, j, 0:B * EXPERTS].rearrange("p (b e) -> p b e", e=EXPERTS)
            score, best1, best2, rank, less = (row(j) for j in range(5))
            one1, one2, weight = (S(13)[:, j, 0:B * EXPERTS].rearrange("p (b e) -> p b e", e=EXPERTS)
                                  for j in range(3))
            top, total, top1, top2, peak, denom, rec = (small[:, j] for j in range(7))
            wide = lambda col: col.unsqueeze(2).broadcast_to([128, B, EXPERTS])
            priority = over_batches(W("C", "priority"), B)
            gates = ["top", "less", "sum", "rec", "score", "m1", "e1", "rank1", "pr1", "one1", "s2", "m2", "e2",
                     "rank2", "pr2", "one2", "den", "deneps", "denrec", "w1", "w2", "w", "wn", "high", "rest", "mid", "low", "share"]
            plan(pe=[*LN["pe"], "gate", "h0", "h1", "h2", "wT", "c0", "c2",
                     *[f"{x}{u}" for u in range(3, len(order)) for x in (["c", "h"] if u % 2 == 0 else ["h"])],
                     "out0", "out1"],
                 act=[*LN["act"], "exp", "s0", "s1", "s2", "wT", *[f"s{u}" for u in range(3, len(order))]],
                 vec=[*LN["vec"], *gates, *[f"{x}{u}" for u in range(len(order)) for x in "gp"],
                      *[f"b{b}" for b in range(B)], "r0", "r1"],
                 pool=["pick", *[f"a{u}" for u in range(4, len(order))]])
            with nc.Block() as block:
                @block.vector
                def _(vec):
                    tt, ts, stt = vec.tensor_tensor, vec.tensor_scalar, vec.scalar_tensor_tensor

                    def chain(ins, name):
                        ins.then_inc(vec_done, V.step(name))
                        vec.wait_ge(vec_done, V.after(name))

                    ln_vector(vec, residual, normed)
                    logits = bank(7, B * EXPERTS).rearrange("p (b e) -> p b e", e=EXPERTS)
                    vec.wait_ge(pe_done, P.after("gate"))
                    chain(vec.tensor_reduce(top, logits, AXIS_X, ALU.max), "top")
                    chain(tt(less, logits, wide(top), ALU.subtract), "less")
                    vec.wait_ge(act_done, A.after("exp"))
                    chain(vec.tensor_reduce(total, score, AXIS_X, ALU.add), "sum")
                    chain(vec.reciprocal(rec, total), "rec")
                    chain(tt(score, score, wide(rec), ALU.mult), "score")
                    chain(vec.tensor_reduce(top1, score, AXIS_X, ALU.max), "m1")
                    chain(tt(best1, score, wide(top1), ALU.is_equal), "e1")
                    chain(tt(rank, best1, priority, ALU.mult), "rank1")
                    chain(vec.tensor_reduce(peak, rank, AXIS_X, ALU.max), "pr1")
                    chain(tt(one1, rank, wide(peak), ALU.is_equal), "one1")
                    chain(stt(out=less, in0=one1, scalar=-2.0, in1=score, op0=ALU.mult, op1=ALU.add), "s2")
                    chain(vec.tensor_reduce(top2, less, AXIS_X, ALU.max), "m2")
                    chain(tt(best2, less, wide(top2), ALU.is_equal), "e2")
                    chain(tt(rank, best2, priority, ALU.mult), "rank2")
                    chain(vec.tensor_reduce(peak, rank, AXIS_X, ALU.max), "pr2")
                    chain(tt(one2, rank, wide(peak), ALU.is_equal), "one2")
                    chain(tt(denom, top1, top2, ALU.add), "den")
                    chain(ts(total, denom, 1e-9, None, ALU.add), "deneps")
                    chain(vec.reciprocal(rec, total), "denrec")
                    chain(tt(one1, one1, wide(top1), ALU.mult), "w1")
                    chain(tt(one2, one2, wide(top2), ALU.mult), "w2")
                    chain(tt(weight, one1, one2, ALU.add), "w")
                    chain(tt(weight, weight, wide(rec), ALU.mult), "wn")
                    chain(vec.tensor_copy(parts[:, :, 0], weight), "high")
                    chain(tt(weight, weight, parts[:, :, 0], ALU.subtract), "rest")
                    chain(vec.tensor_copy(parts[:, :, 1], weight), "mid")
                    tt(parts[:, :, 2], weight, parts[:, :, 1], ALU.subtract).then_inc(vec_done, V.step("low"))
                    tt(denom, denom, rec, ALU.mult).then_inc(vec_done, V.step("share"))
                    for u, (e, h, c) in enumerate(order):
                        pair = 2 * (u % 3)
                        vec.wait_ge(act_done, A.after(f"s{u}"))
                        if u >= 3:
                            vec.wait_ge(vec_done, V.after(f"p{u - 3}"))
                        bias = W("L2", "experts_b", 4 * e + c, 1)
                        stt(out=gated[u % 3], in0=by_batch(pair), scalar=bias, in1=sig[u % 3], op0=ALU.add,
                            op1=ALU.mult).then_inc(vec_done, V.step(f"g{u}"))
                        vec.wait_ge(vec_done, V.after(f"g{u}"))
                        if u - 3 >= 4:
                            vec.wait_ge(pool_done, G.after(f"a{u - 3}"))
                        target = half(units[:, c], h) if e == 0 else part[u % 3]
                        vec.wait_ge(pe_done, P.after(f"c{u - c}"))
                        tt(target, gated[u % 3], by_batch(6 + u // 2 % 2), ALU.mult).then_inc(
                            vec_done, V.step(f"p{u}"))
                    for b in range(B):
                        stt(out=residual[:, b], in0=W("L2", "bo"), scalar=denom[:, b:b + 1], in1=residual[:, b],
                            op0=ALU.mult, op1=ALU.add).then_inc(vec_done, V.step(f"b{b}"))
                    vec.wait_ge(vec_done, V.after(f"b{B - 1}"))
                    for h in range(2):
                        vec.wait_ge(pe_done, P.after(f"out{h}"))
                        tt(half(residual, h), half(residual, h), by_batch(h), ALU.add).then_inc(
                            vec_done, V.step(f"r{h}"))

                @block.gpsimd
                def _(pool):
                    pool.wait_ge(vec_done, V.after("aggr"))
                    pool.tensor_copy(pick16, W("C", "pick", rows=slice(0, rows))).then_inc(pool_done, G.step("pick"))
                    for u, (e, h, c) in enumerate(order):
                        if e == 0:
                            continue
                        total_at = half(units[:, c], h)
                        pool.wait_ge(vec_done, V.after(f"p{u}"))
                        if u >= 8:
                            pool.wait_ge(pool_done, G.after(f"a{u - 4}"))
                        pool.tensor_tensor(total_at, total_at, part[u % 3], ALU.add).then_inc(
                            pool_done, G.step(f"a{u}"))

                @block.tensor
                def _(pe):
                    out_tensor(pe)
                    ln_tensor(pe)
                    pe.wait_ge(act_done, A.after("xnT1"))
                    pe.wait_ge(loaded["L2"], 16)
                    for b in range(B):
                        last = pe.matmul(bank(7)[:, b * EXPERTS:(b + 1) * EXPERTS], normedT[:, b], W("L2", "wg"),
                                         start=True, stop=True)
                    last.then_inc(pe_done, P.step("gate"))

                    def hidden(u):
                        e, h, c = order[u]
                        if u >= 3:
                            pe.wait_ge(vec_done, V.after(f"g{u - 3}"))
                        for j in range(2):
                            at = e * 2 * EH + j * EH + c * 128
                            last = pe.matmul(bank(2 * (u % 3) + j), W("L2", "experts", at, 128), half(normedT, h),
                                             start=True, stop=True)
                        last.then_inc(pe_done, P.step(f"h{u}"))

                    def spread(u):
                        e, h, c = order[u]
                        if u >= 4:
                            pe.wait_ge(vec_done, V.after(f"p{u - 3}"))
                        pe.matmul(bank(6 + u // 2 % 2), pick16[:, e * 128:(e + 1) * 128], half(weight_of, h),
                                  start=True, stop=True).then_inc(pe_done, P.step(f"c{u}"))

                    for u in range(3):
                        hidden(u)
                    pe.wait_ge(vec_done, V.after("low"))
                    for b in range(B):
                        last = pe.matmul(by_batch(6, 2)[0:rows, b], parts[:, b].rearrange("p m e -> p (m e)"), ident16[:],
                                         start=True, stop=True)
                    last.then_inc(pe_done, P.step("wT"))
                    pe.wait_ge(act_done, A.after("wT"))
                    pe.wait_ge(pool_done, G.after("pick"))
                    spread(0)
                    spread(2)
                    for u in range(3, len(order)):
                        if u % 2 == 0:
                            spread(u)
                        hidden(u)
                    for h in range(2):
                        if h == 0:
                            pe.wait_ge(vec_done, V.after(f"g{len(order) - 1}"))
                            pe.wait_ge(pool_done, G.after(f"a{len(order) - 1}"))
                        for b in range(HB * h, HB * h + HB):
                            for c in range(2):
                                last = pe.matmul(by_batch(0, 2)[:, b], units[:, c, b], W("L2", "wo", c * D, D),
                                                 start=c == 0, stop=c == 1)
                        last.then_inc(pe_done, P.step(f"out{h}"))

                @block.scalar
                def _(act):
                    ln_root(act)
                    ln_scalar(act)
                    act.wait_ge(vec_done, V.after("less"))
                    act.activation(score, less, ACT.Exp).then_inc(act_done, A.step("exp"))

                    def sigmoid(u):
                        e, h, c = order[u]
                        act.wait_ge(pe_done, P.after(f"h{u}"))
                        if u >= 3:
                            act.wait_ge(vec_done, V.after(f"g{u - 3}"))
                        act.activation(sig[u % 3], by_batch(2 * (u % 3) + 1), ACT.Sigmoid,
                                       bias=W("L2", "experts_b", 4 * e + 2 + c, 1)).then_inc(
                            act_done, A.step(f"s{u}"))

                    for u in range(3):
                        sigmoid(u)
                    act.wait_ge(pe_done, P.after("wT"))
                    act.copy(weight_of, by_batch(6, 2)[0:rows]).then_inc(act_done, A.step("wT"))
                    for u in range(3, len(order)):
                        sigmoid(u)

        stage(experts_ffn)

        stage(lambda: (
            stacked_prologue("L3", W("L3", "sq"), W("L3", "sk"), wv=W("L3", "sv"), self_attention=True,
                             mask=W("L3", "sparse")),
            stacked_attention(HD ** -0.5, mask=True),
            attention_out(W("L3", "so"))))
        stage(lambda: cross("L3"))
        stage(lambda: quantised_ffn("L3", True))

        for f in stages:
            f()

        with nc.Block() as block:
            @block.sync
            def _(sync):
                sync.dma_start(out_dram.rearrange("b t d -> t b d"), residual[:]).then_inc(stored, 16)
                sync.wait_ge(stored, 16)


def _columns(v, rows=128):
    return np.asarray(v).reshape(rows, 1)


def _rows(v):
    v = np.asarray(v).reshape(1, -1)
    return np.broadcast_to(v, (128, v.shape[1]))


def _stack(a):
    return a.reshape(-1, 128, a.shape[1]).transpose(1, 0, 2).reshape(128, -1)


def _latent_blocks(w):
    out = np.zeros((H, HD, GROUPS, 4, LAT), w.dtype)
    for h in range(H):
        out[h, :, h // 4, h % 4] = w.T
    return out.reshape(D, -1)


def _stacked(w):
    return np.swapaxes(w.reshape(*w.shape[:-1], H, HD), -2, -1).reshape(w.shape)


def _swap(w):
    return w.reshape(LAT // 2, 2, -1)[:, ::-1].reshape(w.shape)


def _pad(a, rows=128):
    return np.concatenate([a, np.zeros((rows - a.shape[0], a.shape[1]), a.dtype)])


def lay_out(i):
    f = np.float32
    pos = np.arange(T)
    freq = 1.0 / 10000.0 ** (np.arange(0, LAT, 2, dtype=f) / f(LAT))
    angle = np.outer(pos.astype(f), freq.astype(f)).astype(f)
    cos = np.tile(np.repeat(np.cos(angle), 2, axis=1).T, (4, 1)).astype(f)
    sign = np.tile(np.array([-1.0, 1.0], f), LAT // 2)[:, None]
    sin = np.tile(np.repeat(np.sin(angle), 2, axis=1).T * sign, (4, 1)).astype(f)
    l2o = np.zeros((4, LAT, GROUPS, H, HD), f)
    for h in range(H):
        l2o[h % 4, :, h // 4, h] = i["L0_attn_l2o_w"].T
    wqk = np.zeros((4, LAT, 4, LAT), f)
    for j in range(4):
        wqk[j, :, j] = i["L0_attn_wqk_w"].T
    per = INNER // 2

    def hinges(a):
        return a.reshape(M, 2, per).transpose(1, 0, 2).reshape(2 * M, per)

    rows, cols = pos[:, None], pos[None, :]
    causal = cols <= rows
    sparse = (causal & (cols >= rows - 31)) | (causal & ((rows - cols) % 64 == 0))
    start = 2.0 ** (-2.0 ** (-(4 - 3)))
    slopes = np.asarray([start * start ** n for n in range(H)], f)
    distance = -np.abs(rows - cols).astype(f)
    alibi = (slopes[None, :, None] * distance[:, None, :]).astype(f)

    def cross(p, q, k, v, o, turn):
        w = {n: (i[f"{p}_{m}"].T if turn else i[f"{p}_{m}"]) for n, m in (("xq", q), ("xk", k), ("xv", v), ("xo", o))}
        return {n: _stacked(a) if n in ("xq", "xk") else a for n, a in w.items()}

    L0 = {
        "qkv": i["L0_attn_c_attn_w"].T, "q_lat": _latent_blocks(i["L0_attn_q2l_w"]),
        "q_swap": _latent_blocks(_swap(i["L0_attn_q2l_w"])), "kv_lat": _latent_blocks(i["L0_attn_kv2l_w"]),
        "k_swap": _latent_blocks(_swap(i["L0_attn_kv2l_w"])), "l2o": l2o.reshape(128, -1), "wqk": wqk.reshape(128, 128),
        "cproj": i["L0_attn_cproj_w"].T, "qkv_b": i["L0_attn_c_attn_b"].reshape(3, D).T,
        "q_lat_b": _columns(np.tile(i["L0_attn_q2l_b"], 4)), "q_swap_b": _columns(np.tile(_swap(i["L0_attn_q2l_b"]), 4)),
        "kv_lat_b": _columns(np.tile(i["L0_attn_kv2l_b"], 4)),
        "k_swap_b": _columns(np.tile(_swap(i["L0_attn_kv2l_b"]), 4)),
        "wqk_b": _columns(np.tile(i["L0_attn_wqk_b"], 4)), "l2o_b": _columns(np.tile(i["L0_attn_l2o_b"], H)),
        "cproj_b": _rows(i["L0_attn_cproj_b"]), "cos": cos, "sin": sin,
        "causal": np.where(causal, 0.0, MASKED).astype(f),
        **cross("L0_xattn", "wq_w", "wk_w", "wv_w", "wo_w", True),
        "xq_b": _columns(_stacked(i["L0_xattn_wq_b"])), "xk_b": _columns(_stacked(i["L0_xattn_wk_b"])), "xv_b": _rows(i["L0_xattn_wv_b"]),
        "xo_b": _rows(i["L0_xattn_wo_b"]),
        "win": np.tile(i["L0_ffn_Win"], (1, 2)), "wout": np.tile(i["L0_ffn_Wout"], (2, 1)),
        "bin": _columns(np.tile(i["L0_ffn_bin_"], 2)), "w1": hinges(i["L0_ffn_W1"]), "b1": hinges(i["L0_ffn_b1"]),
        "w2": hinges(i["L0_ffn_W2"]), "b2": _pad(_columns(i["L0_ffn_b2"], M)), "bout": _rows(i["L0_ffn_bout"]),
        "mean_v": i["L2_xattn_WV"].T, "p": _columns(i["L2_xattn_p_param"]), "shift": _columns(i["L2_xattn_shift"]),
    }
    L1 = {
        "phases": i["L1_attn_pos_phases"][:T].T, "wpv": i["L1_attn_Wpv"], "wk": i["L1_attn_Wk"],
        "wkv": i["L1_attn_Wkv"], "wg1": i["L1_attn_Wg1"][:D], "wg1_shift": i["L1_attn_Wg1"][D:],
        "wg2": np.tile(i["L1_attn_Wg2"], (1, D)), "wb1": i["L1_attn_Wb1"],
        "wb2_0": _pad(np.tile(i["L1_attn_Wb2"][:, 0:1], (1, D))), "wb2_1": _pad(np.tile(i["L1_attn_Wb2"][:, 1:2], (1, D))),
        "wo": i["L1_attn_Wo"], "bpv": _columns(i["L1_attn_bpv"]), "bk": _columns(i["L1_attn_bk"]),
        "bkv": _columns(i["L1_attn_bkv"]), "bg1": _columns(i["L1_attn_bg1"]), "bg2": _rows(i["L1_attn_bg2"]),
        "bb1": _pad(_columns(i["L1_attn_bb1"], 64)), "bb2_0": _rows(i["L1_attn_bb2"][0:1]),
        "bb2_1": _rows(i["L1_attn_bb2"][1:2]), "ln_g": _columns(i["L1_attn_ln_g"]), "ln_b": _columns(i["L1_attn_ln_b"]),
        "bo": _rows(i["L1_attn_bo"]), **cross("L1_xattn", "wq", "wk", "wv", "wo", True),
        "xq_b": _columns(_stacked(i["L1_xattn_bq"])), "xk_b": _columns(_stacked(i["L1_xattn_bk"])), "xv_b": _rows(i["L1_xattn_bv"]),
        "xo_b": _rows(i["L1_xattn_bo"]), "up": i["L1_ffn_W1"].T, "down": _stack(i["L1_ffn_W2"].T),
        "up_b": _rows(i["L1_ffn_b1"]), "down_b": _rows(i["L1_ffn_b2"]),
    }
    L2 = {
        "wi": i["L2_attn_Wi"].T, "wh": i["L2_attn_Wh"].T,
        "ih_b": _pad(np.stack([i["L2_attn_bi"], i["L2_attn_bh"]])),
        "xq": _stacked(i["L2_xattn_WQ"].T), "xk": _stacked(i["L2_xattn_WK"].T), "xo": i["L2_xattn_Wout"].T, "wg": i["L2_ffn_Wg"].T,
        "experts": i["L2_ffn_W1"].transpose(2, 0, 1).reshape(D, -1),
        "experts_b": i["L2_ffn_b1"].reshape(EXPERTS, 4, 128).transpose(2, 0, 1).reshape(128, -1),
        "wo": _stack(i["L2_ffn_Wo"].T), "bo": _rows(i["L2_ffn_bo"]),
    }
    L3 = {
        "sq": _stacked(i["L3_attn_Wq"].T), "sk": _stacked(i["L3_attn_Wk"].T), "sv": i["L3_attn_Wv"].T, "so": i["L3_attn_Wo"].T,
        "sparse": np.where(sparse, 0.0, MASKED).astype(f), **cross("L3_xattn", "Wq", "Wk", "Wv", "Wo", False),
        "xq_b": _columns(_stacked(i["L3_xattn_bq"])), "xk_b": _columns(_stacked(i["L3_xattn_bk"])), "xv_b": _rows(i["L3_xattn_bv"]),
        "xo_b": _rows(i["L3_xattn_bo"]), "alibi": alibi.reshape(T, -1),
        "gate": i["L3_ffn_w_gate"].T, "up": i["L3_ffn_w_up"].T, "down": _stack(i["L3_ffn_w_down"].T),
    }
    pick = np.zeros((128, EXPERTS, 128), f)
    for m in range(PARTS):
        pick[m * EXPERTS + np.arange(EXPERTS), np.arange(EXPERTS)] = 1.0
    minus_pick = np.zeros((128, H), f)
    minus_pick[:PARTS * H] = -np.tile(np.eye(H, dtype=f), (PARTS, 1))
    C = {
        "identity": np.eye(128, dtype=f), 
        "latent_mask": (np.arange(128)[:, None] // LAT == np.arange(GROUPS)).astype(f),
        "minus_pick": minus_pick,
        "pick": pick.reshape(128, -1), "priority": _rows(np.arange(EXPERTS, 0, -1).astype(f)),
    }
    packs = {}
    for name, parts in (("L0", L0), ("L1", L1), ("L2", L2), ("L3", L3), ("C", C)):
        assert all(parts[n].shape == (128, w) for n, w in COLUMNS[name]), [
            (n, parts[n].shape, w) for n, w in COLUMNS[name] if parts[n].shape != (128, w)]
        packs[name] = np.ascontiguousarray(np.concatenate([parts[n] for n, _ in COLUMNS[name]], axis=1))
    return packs


def kernel(**inputs):
    import concourse.bacc as bacc
    from concourse.bass_utils import run_bass_kernel_spmd

    inputs = {k: np.asarray(v) for k, v in inputs.items()}
    nc = bacc.Bacc("TRN2", target_bir_lowering=False, num_devices=1)
    packs = lay_out(inputs)
    arrays = {f"in_{p}": a for p, a in packs.items()}
    arrays["in_x"] = np.ascontiguousarray(inputs["x"])
    arrays["in_ctx"] = np.ascontiguousarray(inputs["ctx_1024"])
    drams = {n: nc.dram_tensor(n, a.shape, F32, kind="ExternalInput").ap() for n, a in arrays.items()}
    out = nc.dram_tensor("out_x", (B, T, D), F32, kind="ExternalOutput").ap()
    build(nc, {p: drams[f"in_{p}"] for p in packs}, drams["in_x"], drams["in_ctx"], out)
    result = run_bass_kernel_spmd(nc, [arrays], core_ids=[0])
    return result.results[0]["out_x"]
```
